# Optimizing a Trainium2 kernel written in Bass

```python
import numpy as np
import jax
import jax.numpy as jnp

def _softmax(x, axis=-1):
    return jax.nn.softmax(x, axis=axis)

def _gelu(x):
    return jax.nn.gelu(x, approximate=True)

def _silu(x):
    return jax.nn.silu(x)

def _sigmoid(x):
    return jax.nn.sigmoid(x)

def _layernorm(x, axis=-1, eps=1e-05):
    m = jnp.mean(x, axis=axis, keepdims=True)
    v = jnp.var(x, axis=axis, keepdims=True)
    return (x - m) / jnp.sqrt(v + eps)

def _scatter_add(tgt, idx, src, axis=0):
    return tgt.at[idx].add(src)

def _segment_sum(src, seg, n):
    return jax.ops.segment_sum(src, seg, n)
kernel_name = 'mk_audio_tower_d2_tok_audfeat512_r4_f5960c'

def setup_inputs(seed: int=0):
    np.random.seed(seed)
    _w = jnp.asarray

    def _rec_inputs():
        import jax
        import jax.numpy as jnp
        _rk = jax.random.key(seed)
        x = -0.000292821 + 1.00034 * jax.random.normal(jax.random.fold_in(_rk, 1), (16, 375, 128), jnp.float32)
        return x
    x = _rec_inputs()

    def _L0_tok_setup():
        import jax, jax.numpy as jnp
        import numpy as np
        B, T, C, HID, K, H = (8, 256, 128, 512, 31, 4)
        key = jax.random.key(seed)
        ks = jax.random.split(key, 8)
        n = lambda k_, sh, sc: jax.random.normal(k_, sh, dtype=jnp.float32) * sc
        return {'x': n(ks[0], (B, T, C), 1.0), 'Wl': n(ks[1], (H * K, C), 0.05), 'bl': n(ks[2], (H * K,), 0.01), 'bias': n(ks[3], (C,), 0.02), 'Wc': n(ks[4], (HID, C, K), 0.01), 'bc': n(ks[5], (HID,), 0.01), 'W2': n(ks[6], (C, HID), 0.01), 'b2': n(ks[7], (C,), 0.01)}
    _L0_tok_all = _L0_tok_setup()
    _L0_tok_in = {k: v for k, v in _L0_tok_all.items() if k in ('Wl', 'bl', 'bias', 'Wc', 'bc', 'W2', 'b2')}
    del _L0_tok_all

    def _L0_attn_setup():
        import jax, jax.numpy as jnp
        import numpy as np
        from math import log
        MODEL_DIM = 128
        NUM_HEADS = 8
        DIM_HEAD = 64
        INNER = NUM_HEADS * DIM_HEAD
        B, L = (8, 256)
        EPS = 1e-05

        def _rel_pos_emb(seq_len, d):
            rel = jnp.arange(seq_len, dtype=jnp.float32)[:, None] - jnp.arange(d, dtype=jnp.float32)[None, :]
            freqs = jnp.exp(-jnp.arange(0, 2 * d, 2, dtype=jnp.float32) * (log(10000.0) / MODEL_DIM))
            angle = rel * freqs[None, :]
            even = jnp.arange(d) % 2 == 0
            return jnp.where(even[None, :], jnp.cos(angle), jnp.sin(angle))
        key = jax.random.key(seed)
        ks = jax.random.split(key, 9)
        x = jax.random.normal(ks[0], (B, L, MODEL_DIM), dtype=jnp.float32)
        gamma = jnp.ones((MODEL_DIM,), jnp.float32)
        beta = jnp.zeros((MODEL_DIM,), jnp.float32)
        w_qkv = jax.random.normal(ks[1], (3 * INNER, MODEL_DIM), jnp.float32) * MODEL_DIM ** (-0.5)
        b_qkv = jnp.zeros((3 * INNER,), jnp.float32)
        w_pos = jax.random.normal(ks[2], (INNER, MODEL_DIM), jnp.float32) * MODEL_DIM ** (-0.5)
        w_out = jax.random.normal(ks[3], (MODEL_DIM, INNER), jnp.float32) * INNER ** (-0.5)
        b_out = jnp.zeros((MODEL_DIM,), jnp.float32)
        bound = (6.0 / (NUM_HEADS + DIM_HEAD)) ** 0.5
        u_bias = jax.random.uniform(ks[4], (NUM_HEADS, DIM_HEAD), jnp.float32, -bound, bound)
        v_bias = jax.random.uniform(ks[5], (NUM_HEADS, DIM_HEAD), jnp.float32, -bound, bound)
        return {'x': x, 'gamma': gamma, 'beta': beta, 'w_qkv': w_qkv, 'b_qkv': b_qkv, 'w_pos': w_pos, 'w_out': w_out, 'b_out': b_out, 'u_bias': u_bias, 'v_bias': v_bias}
    _L0_attn_all = _L0_attn_setup()
    _L0_attn_in = {k: v for k, v in _L0_attn_all.items() if k in ('gamma', 'beta', 'w_qkv', 'b_qkv', 'w_pos', 'w_out', 'b_out', 'u_bias', 'v_bias')}
    del _L0_attn_all

    def _L0_ffn_setup():
        import jax, jax.numpy as jnp
        import numpy as np
        B, S, D = (2, 512, 128)
        E, H, TOP_K = (8, 256, 2)
        SCALE = 1.0
        key = jax.random.key(seed)
        ks = jax.random.split(key, 7)
        s = lambda fan_in: 1.0 / np.sqrt(fan_in)
        return {'x': jax.random.normal(ks[0], (B, S, D), dtype=jnp.float32), 'gate_w': jax.random.normal(ks[1], (E, D), dtype=jnp.float32) * s(D), 'w1': jax.random.normal(ks[2], (E, H, D), dtype=jnp.float32) * s(D), 'w2': jax.random.normal(ks[3], (E, D, H), dtype=jnp.float32) * s(H), 'sg_gate': jax.random.normal(ks[4], (H, D), dtype=jnp.float32) * s(D), 'sg_up': jax.random.normal(ks[5], (H, D), dtype=jnp.float32) * s(D), 'sg_down': jax.random.normal(ks[6], (D, H), dtype=jnp.float32) * s(H)}
    _L0_ffn_all = _L0_ffn_setup()
    _L0_ffn_in = {k: v for k, v in _L0_ffn_all.items() if k in ('gate_w', 'w1', 'w2', 'sg_gate', 'sg_up', 'sg_down')}
    del _L0_ffn_all

    def _L1_attn_setup():
        import math
        import jax, jax.numpy as jnp
        import numpy as np
        B, N, C, H = (4, 576, 128, 8)
        HD = C // H
        key = jax.random.key(seed)
        k0, k1, k2 = jax.random.split(key, 3)
        x = jax.random.normal(k0, (B, N, C), dtype=jnp.float32)
        w_in = jax.random.normal(k1, (3 * C, C), dtype=jnp.float32) * 0.02
        b_in = jnp.zeros((3 * C,), dtype=jnp.float32)
        w_out = jax.random.normal(k2, (C, C), dtype=jnp.float32) * 0.02
        b_out = jnp.zeros((C,), dtype=jnp.float32)
        return {'x': x, 'w_in': w_in, 'b_in': b_in, 'w_out': w_out, 'b_out': b_out}
    _L1_attn_all = _L1_attn_setup()
    _L1_attn_in = {k: v for k, v in _L1_attn_all.items() if k in ('w_in', 'b_in', 'w_out', 'b_out')}
    del _L1_attn_all

    def _L1_ffn_setup():
        import jax, jax.numpy as jnp
        import numpy as np
        DIM = 128
        MOE_DIM = 64
        E = 64
        G = 8
        TOPK_G = 4
        K = 8
        SCALE = 2.5
        CAP = 256

        def _gate(x2, gate_w, gate_b):
            T = x2.shape[0]
            scores = jax.nn.sigmoid(x2 @ gate_w.T)
            s = (scores + gate_b).reshape(T, G, E // G)
            group_scores = jax.lax.top_k(s, 2)[0].sum(-1)
            top_groups = jax.lax.top_k(group_scores, TOPK_G)[1]
            gmask = jnp.zeros((T, G), bool).at[jnp.arange(T)[:, None], top_groups].set(True)
            s = jnp.where(gmask[..., None], s, -jnp.inf).reshape(T, E)
            idx = jax.lax.top_k(s, K)[1]
            w = jnp.take_along_axis(scores, idx, axis=1)
            w = w / w.sum(-1, keepdims=True) * SCALE
            return (w, idx)

        def _moe_forward(x, gate_w, gate_b, w1, w3, w2):
            shape = x.shape
            x2 = x.reshape(-1, DIM)
            T = x2.shape[0]
            w, idx = _gate(x2, gate_w, gate_b)
            flat_e = idx.reshape(-1)
            oh = (flat_e[:, None] == jnp.arange(E)[None, :]).astype(jnp.int32)
            pos = (jnp.cumsum(oh, axis=0) * oh).sum(-1) - 1
            x_rep = jnp.repeat(x2, K, axis=0)
            xb = jnp.zeros((E, CAP, DIM), x2.dtype).at[flat_e, pos].set(x_rep, mode='drop')
            h = jax.nn.silu(jnp.einsum('ecd,edm->ecm', xb, w1)) * jnp.einsum('ecd,edm->ecm', xb, w3)
            yb = jnp.einsum('ecm,emd->ecd', h, w2)
            y = yb.at[flat_e, pos].get(mode='fill', fill_value=0.0) * w.reshape(-1)[:, None]
            return y.reshape(T, K, DIM).sum(1).reshape(shape)
        key = jax.random.key(seed)
        ks = jax.random.split(key, 6)
        x = jax.random.normal(ks[0], (4, 128, DIM), jnp.float32)
        gate_w = jax.random.normal(ks[1], (E, DIM), jnp.float32) / np.sqrt(DIM).astype(np.float32)
        gate_b = jax.random.normal(ks[2], (E,), jnp.float32) * 0.01
        w1 = jax.random.normal(ks[3], (E, DIM, MOE_DIM), jnp.float32) / np.sqrt(DIM).astype(np.float32)
        w3 = jax.random.normal(ks[4], (E, DIM, MOE_DIM), jnp.float32) / np.sqrt(DIM).astype(np.float32)
        w2 = jax.random.normal(ks[5], (E, MOE_DIM, DIM), jnp.float32) / np.sqrt(MOE_DIM).astype(np.float32)
        return {'x': x, 'gate_w': gate_w, 'gate_b': gate_b, 'w1': w1, 'w3': w3, 'w2': w2}
    _L1_ffn_all = _L1_ffn_setup()
    _L1_ffn_in = {k: v for k, v in _L1_ffn_all.items() if k in ('gate_w', 'gate_b', 'w1', 'w3', 'w2')}
    del _L1_ffn_all
    return {'x': x, 'L0_tok_Wl': _L0_tok_in['Wl'], 'L0_tok_bl': _L0_tok_in['bl'], 'L0_tok_bias': _L0_tok_in['bias'], 'L0_tok_Wc': _L0_tok_in['Wc'], 'L0_tok_bc': _L0_tok_in['bc'], 'L0_tok_W2': _L0_tok_in['W2'], 'L0_tok_b2': _L0_tok_in['b2'], 'L0_attn_gamma': _L0_attn_in['gamma'], 'L0_attn_beta': _L0_attn_in['beta'], 'L0_attn_w_qkv': _L0_attn_in['w_qkv'], 'L0_attn_b_qkv': _L0_attn_in['b_qkv'], 'L0_attn_w_pos': _L0_attn_in['w_pos'], 'L0_attn_w_out': _L0_attn_in['w_out'], 'L0_attn_b_out': _L0_attn_in['b_out'], 'L0_attn_u_bias': _L0_attn_in['u_bias'], 'L0_attn_v_bias': _L0_attn_in['v_bias'], 'L0_ffn_gate_w': _L0_ffn_in['gate_w'], 'L0_ffn_w1': _L0_ffn_in['w1'], 'L0_ffn_w2': _L0_ffn_in['w2'], 'L0_ffn_sg_gate': _L0_ffn_in['sg_gate'], 'L0_ffn_sg_up': _L0_ffn_in['sg_up'], 'L0_ffn_sg_down': _L0_ffn_in['sg_down'], 'L1_attn_w_in': _L1_attn_in['w_in'], 'L1_attn_b_in': _L1_attn_in['b_in'], 'L1_attn_w_out': _L1_attn_in['w_out'], 'L1_attn_b_out': _L1_attn_in['b_out'], 'L1_ffn_gate_w': _L1_ffn_in['gate_w'], 'L1_ffn_gate_b': _L1_ffn_in['gate_b'], 'L1_ffn_w1': _L1_ffn_in['w1'], 'L1_ffn_w3': _L1_ffn_in['w3'], 'L1_ffn_w2': _L1_ffn_in['w2']}

def reference(x, L0_tok_Wl, L0_tok_bl, L0_tok_bias, L0_tok_Wc, L0_tok_bc, L0_tok_W2, L0_tok_b2, L0_attn_gamma, L0_attn_beta, L0_attn_w_qkv, L0_attn_b_qkv, L0_attn_w_pos, L0_attn_w_out, L0_attn_b_out, L0_attn_u_bias, L0_attn_v_bias, L0_ffn_gate_w, L0_ffn_w1, L0_ffn_w2, L0_ffn_sg_gate, L0_ffn_sg_up, L0_ffn_sg_down, L1_attn_w_in, L1_attn_b_in, L1_attn_w_out, L1_attn_b_out, L1_ffn_gate_w, L1_ffn_gate_b, L1_ffn_w1, L1_ffn_w3, L1_ffn_w2):
    import jax
    import jax.numpy as jnp

    def _L0_tok_ref(x, Wl, bl, bias, Wc, bc, W2, b2):
        import jax, jax.numpy as jnp
        import numpy as np
        B, T, C, HID, K, H = (8, 256, 128, 512, 31, 4)
        Bq, Tq, Cq = x.shape
        d = Cq // H
        logits = (x @ Wl.T + bl).reshape(Bq, Tq, H, K)
        offs = jnp.arange(K) - (K - 1) // 2
        pos = jnp.arange(Tq)[:, None] + offs[None, :]
        valid = (pos >= 0) & (pos < Tq)
        logits = jnp.where(valid[None, :, None, :], logits, -jnp.inf)
        w = jax.nn.softmax(logits, axis=-1)
        xg = x.reshape(Bq, Tq, H, d)[:, jnp.clip(pos, 0, Tq - 1)]
        y = jnp.einsum('bthk,btkhd->bthd', w, xg).reshape(Bq, Tq, Cq)
        y = y.transpose(0, 2, 1) + bias[None, :, None]
        z = jax.lax.conv_general_dilated(y, Wc, (1,), 'VALID', dimension_numbers=('NCH', 'OIH', 'NCH'))
        z = z + bc[None, :, None]
        z = jax.nn.selu(z.transpose(0, 2, 1))
        return z @ W2.T + b2

    def _L0_attn_ref(x, gamma, beta, w_qkv, b_qkv, w_pos, w_out, b_out, u_bias, v_bias):
        import jax, jax.numpy as jnp
        import numpy as np
        from math import log
        MODEL_DIM = 128
        NUM_HEADS = 8
        DIM_HEAD = 64
        INNER = NUM_HEADS * DIM_HEAD
        B, L = (8, 256)
        EPS = 1e-05

        def _rel_pos_emb(seq_len, d):
            rel = jnp.arange(seq_len, dtype=jnp.float32)[:, None] - jnp.arange(d, dtype=jnp.float32)[None, :]
            freqs = jnp.exp(-jnp.arange(0, 2 * d, 2, dtype=jnp.float32) * (log(10000.0) / MODEL_DIM))
            angle = rel * freqs[None, :]
            even = jnp.arange(d) % 2 == 0
            return jnp.where(even[None, :], jnp.cos(angle), jnp.sin(angle))
        b, l, d = x.shape
        h, dh = (NUM_HEADS, DIM_HEAD)
        mu = jnp.mean(x, axis=-1, keepdims=True)
        var = jnp.mean(jnp.square(x - mu), axis=-1, keepdims=True)
        xn = (x - mu) * jax.lax.rsqrt(var + EPS) * gamma + beta
        pe = _rel_pos_emb(l, d)
        pos = (pe @ w_pos.T).reshape(l, h, dh)
        pos = jnp.transpose(pos, (1, 0, 2))
        qkv = xn @ w_qkv.T + b_qkv
        q, k, v = jnp.split(qkv, 3, axis=-1)

        def to_heads(t):
            return jnp.transpose(t.reshape(b, l, h, dh), (0, 2, 1, 3))
        q, k, v = (to_heads(q), to_heads(k), to_heads(v))
        scale = dh ** (-0.5)
        content = jnp.einsum('bhld,bhmd->bhlm', q + u_bias[None, :, None, :], k)
        pos_score = jnp.einsum('bhld,hmd->bhlm', q + v_bias[None, :, None, :], pos)
        attn = jax.nn.softmax((content + pos_score) * scale, axis=-1)
        out = jnp.einsum('bhlm,bhmd->bhld', attn, v)
        out = jnp.transpose(out, (0, 2, 1, 3)).reshape(b, l, h * dh)
        return out @ w_out.T + b_out

    def _L0_ffn_ref(x, gate_w, w1, w2, sg_gate, sg_up, sg_down):
        import jax, jax.numpy as jnp
        import numpy as np
        B, S, D = (2, 512, 128)
        E, H, TOP_K = (8, 256, 2)
        SCALE = 1.0
        b, s_len, d = x.shape
        xf = x.reshape(-1, d)
        n = xf.shape[0]
        logits = xf @ gate_w.T * SCALE
        topk_w, idx = jax.lax.top_k(logits, TOP_K)
        topk_w = jax.nn.softmax(topk_w, axis=-1)
        comb = jnp.zeros((n, E), dtype=xf.dtype).at[jnp.arange(n)[:, None], idx].add(topk_w)
        h = jax.nn.silu(jnp.einsum('td,ehd->teh', xf, w1))
        eo = jnp.einsum('teh,edh->ted', h, w2)
        routed = jnp.einsum('te,ted->td', comb, eo)
        shared = jax.nn.silu(xf @ sg_gate.T) * (xf @ sg_up.T) @ sg_down.T
        return (routed + shared).reshape(b, s_len, d)

    def _L1_attn_ref(x, w_in, b_in, w_out, b_out):
        import math
        import jax, jax.numpy as jnp
        import numpy as np
        B, N, C, H = (4, 576, 128, 8)
        HD = C // H
        b, n, c = x.shape
        y = jnp.einsum('bnc,fc->bnf', x, w_in) + b_in

        def to_heads(t):
            return t.reshape(b, n, H, HD).transpose(0, 2, 1, 3)
        q, k, v = (to_heads(t) for t in jnp.split(y, 3, axis=1))
        w = jnp.einsum('bhqd,bhkd->bhqk', q, k) / math.sqrt(HD)
        o = jnp.einsum('bhqk,bhkd->bhqd', w, v)
        o = o.transpose(0, 2, 1, 3).reshape(b, n, c)
        return jnp.einsum('bnc,fc->bnf', o, w_out) + b_out

    def _L1_ffn_ref(x, gate_w, gate_b, w1, w3, w2):
        import jax, jax.numpy as jnp
        import numpy as np
        DIM = 128
        MOE_DIM = 64
        E = 64
        G = 8
        TOPK_G = 4
        K = 8
        SCALE = 2.5
        CAP = 256

        def _gate(x2, gate_w, gate_b):
            T = x2.shape[0]
            scores = jax.nn.sigmoid(x2 @ gate_w.T)
            s = (scores + gate_b).reshape(T, G, E // G)
            group_scores = jax.lax.top_k(s, 2)[0].sum(-1)
            top_groups = jax.lax.top_k(group_scores, TOPK_G)[1]
            gmask = jnp.zeros((T, G), bool).at[jnp.arange(T)[:, None], top_groups].set(True)
            s = jnp.where(gmask[..., None], s, -jnp.inf).reshape(T, E)
            idx = jax.lax.top_k(s, K)[1]
            w = jnp.take_along_axis(scores, idx, axis=1)
            w = w / w.sum(-1, keepdims=True) * SCALE
            return (w, idx)

        def _moe_forward(x, gate_w, gate_b, w1, w3, w2):
            shape = x.shape
            x2 = x.reshape(-1, DIM)
            T = x2.shape[0]
            w, idx = _gate(x2, gate_w, gate_b)
            flat_e = idx.reshape(-1)
            oh = (flat_e[:, None] == jnp.arange(E)[None, :]).astype(jnp.int32)
            pos = (jnp.cumsum(oh, axis=0) * oh).sum(-1) - 1
            x_rep = jnp.repeat(x2, K, axis=0)
            xb = jnp.zeros((E, CAP, DIM), x2.dtype).at[flat_e, pos].set(x_rep, mode='drop')
            h = jax.nn.silu(jnp.einsum('ecd,edm->ecm', xb, w1)) * jnp.einsum('ecd,edm->ecm', xb, w3)
            yb = jnp.einsum('ecm,emd->ecd', h, w2)
            y = yb.at[flat_e, pos].get(mode='fill', fill_value=0.0) * w.reshape(-1)[:, None]
            return y.reshape(T, K, DIM).sum(1).reshape(shape)
        return _moe_forward(x, gate_w, gate_b, w1, w3, w2)
    h = _L0_tok_ref(x, L0_tok_Wl, L0_tok_bl, L0_tok_bias, L0_tok_Wc, L0_tok_bc, L0_tok_W2, L0_tok_b2)
    h = h + _L0_attn_ref(_layernorm(h, axis=-1), L0_attn_gamma, L0_attn_beta, L0_attn_w_qkv, L0_attn_b_qkv, L0_attn_w_pos, L0_attn_w_out, L0_attn_b_out, L0_attn_u_bias, L0_attn_v_bias)
    h = h + _L0_ffn_ref(_layernorm(h, axis=-1), L0_ffn_gate_w, L0_ffn_w1, L0_ffn_w2, L0_ffn_sg_gate, L0_ffn_sg_up, L0_ffn_sg_down)
    h = h + _L1_attn_ref(_layernorm(h, axis=-1), L1_attn_w_in, L1_attn_b_in, L1_attn_w_out, L1_attn_b_out)
    h = h + _L1_ffn_ref(_layernorm(h, axis=-1), L1_ffn_gate_w, L1_ffn_gate_b, L1_ffn_w1, L1_ffn_w3, L1_ffn_w2)
    return h

_drawn_inputs = setup_inputs


def setup_inputs(seed=0):
    import zlib

    import numpy as np

    out = dict(_drawn_inputs(seed))
    spreads = {'L0_attn_gamma': (1.0, 0.2),
     'L0_attn_beta': (0.0, 0.1),
     'L0_attn_b_qkv': (0.0, 0.1),
     'L0_attn_b_out': (0.0, 0.1),
     'L1_attn_b_in': (0.0, 0.1),
     'L1_attn_b_out': (0.0, 0.1)}
    factors = {}
    for name, (base, spread) in spreads.items():
        noise = np.random.default_rng([zlib.crc32(name.encode()), seed]).standard_normal(out[name].shape)
        drawn = base * np.exp(spread * noise) if base else spread * noise
        out[name] = jnp.asarray(drawn.astype(out[name].dtype))
    for name, factor in factors.items():
        out[name] = (out[name] * factor).astype(out[name].dtype)
    return out
```

```python
from contextlib import ExitStack

import numpy as np

import concourse.bass as bass
from concourse import mybir

F32 = mybir.dt.float32
F16 = mybir.dt.float16
BF16 = mybir.dt.bfloat16
U32 = mybir.dt.uint32
ALU = mybir.AluOpType
ACT = mybir.ActivationFunctionType
AX = mybir.AxisListType

B, T, C = 16, 375, 128
TAPS = 31
TOK = T - TAPS + 1
J = 3
A = TOK // J
HEADS_T = 4
LK = HEADS_T * TAPS
TILES = 4
TT = 94
TW = TT + TAPS - 1
TP = TILES * TT
BROW = TW * HEADS_T
HID = 512
OC = HID // 128
H0, DH = 8, 64
E0, F0 = 8, 256
E1, F1, CAP = 64, 64, 256
NTOK = B * TOK
ROW = C + E1 + 1
SLOTS = E1 * CAP
LO = 2048.0
ALPHA = 1.6732632423543772848170429916717
LAMBDA = 1.0507009873554804934193349852946
EPS = 1e-5
UNITS = H0 * J

PASSES = 3
CHUNK = TAPS * PASSES
POINTS = UNITS + 2 * (E0 + 1) + 8
SPANS = [(0, 12), (12, 24), (24, 35), (35, POINTS)]
FILL = {}
for _o, (_p0, _p1) in enumerate(SPANS):
    for _p in range(_p0, _p1):
        FILL[_p] = (_o, CHUNK * (_p - _p0) // (_p1 - _p0), CHUNK * (_p - _p0 + 1) // (_p1 - _p0))
CHUNK_END = {_p1 - 1: _o for _o, (_p0, _p1) in enumerate(SPANS)}

def unit_steps():
    out = []
    for s in range(UNITS + 2):
        if s < UNITS:
            out.append(("S", s))
        if 1 <= s <= UNITS:
            out.append(("T", s - 1))
    return out


W_USES = ([("ln", 1)] + [x for h in range(H0) for x in ([("q", h)] + ([("k", h // 2)] if h % 2 == 0 else []))]
          + [("v", j) for j in range(J)] + unit_steps()
          + [("oT", j) for j in range(J)] + [("out0", 0)]
          + [("ln", 2), ("gate0", 0)] + [("hid", n) for n in range(2 * E0)]
          + [("sg", 0), ("su", 0), ("sg", 1), ("su", 1)]
          + [("ln", 3), ("q1", 0), ("k1", 0), ("v1", 0), ("kv", 0), ("g", 0), ("out1", 0)]
          + [("ln", 4), ("gate1", 0), ("count", 0)])
O_USES = [("O", h) for h in range(H0)] + [("Y", e) for e in range(E0 + 1)]
C_USES = ([("lg", 0)] + [("bT", i) for i in range(TILES)] + [("y", 0)]
          + [x for o in range(OC) for x in (("main", o), ("cross", o))] + [("w2", 0)])
C_BANK = {"lg": 0, "bT": 1, "y": 0, "main": 0, "cross": 1, "w2": 0}


def place(uses, banks):
    seen = [0] * banks
    where = {}
    for n, u in enumerate(uses):
        b = C_BANK[u[0]] if uses is C_USES else n % banks
        seen[b] += 1
        where[u] = (b, seen[b])
    return where, seen


W_AT, W_PER = place(W_USES, 4)
O_AT, O_PER = place(O_USES, 2)
C_AT, C_PER = place(C_USES, 2)


FREED = {("lg", 0): ("lg_shifted", 1), ("y", 0): ("y_ready", 1), ("out0", 0): ("ln_var_ready", 2),
         ("gate0", 0): ("gate_shifted", 1), ("kv", 0): ("kv_state_ready", 1), ("g", 0): ("g_ready", 1),
         ("q1", 0): ("qkv1_ready", 1), ("k1", 0): ("qkv1_ready", 2), ("v1", 0): ("qkv1_ready", 3),
         ("out1", 0): ("h3_ready", 1), ("gate1", 0): ("gate_exp", 2)}
FREED |= {("bT", t): ("bandT_ready", t + 1) for t in range(TILES)}
FREED |= {("main", o): ("zneg_ready", o + 1) for o in range(OC)}
FREED |= {("cross", o): ("cross_terms_ready", o + 1) for o in range(OC)}
FREED |= {("ln", n): ("xT_ready", n) for n in range(1, 5)}
FREED |= {("q", h): ("q_ready", h + 1) for h in range(H0)}
FREED |= {("k", g): ("kv_ready", g + 1) for g in range(H0 // 2)}
FREED |= {("v", j): ("kv_ready", H0 // 2 + j + 1) for j in range(J)}
FREED |= {("S", u): ("p_ready", u + 1) for u in range(UNITS)}
FREED |= {("T", u): (("pt_ready_scalar", "pt_ready_vector")[u % 2], u // 2 + 1) for u in range(UNITS)}
FREED |= {("oT", j): ("oT_ready", j + 1) for j in range(J)}
FREED |= {("hid", n): ("hid_ready", n + 1) for n in range(2 * E0)}
FREED |= {(w, c): ("hid_ready", 2 * E0 + c + 1) for w in ("sg", "su") for c in range(2)}
FREED |= {("O", h): ("o_ready", h + 1) for h in range(H0)}
FREED |= {("Y", e): ("y_added", e + 1) for e in range(E0 + 1)}


def before_in_bank(uses, where):
    return {u: next((v for v in reversed(uses[:uses.index(u)]) if where[v][0] == where[u][0]), None) for u in uses}


W_PREV, O_PREV, C_PREV = (before_in_bank(u, w) for u, w in ((W_USES, W_AT), (O_USES, O_AT), (C_USES, C_AT)))


def build(nc, dram, out, per):
    ctx = ExitStack()
    seen, totals, named = {}, {}, {}

    def sb(name, shape, dt=F32):
        return ctx.enter_context(nc.sbuf_tensor(name, shape, dt))

    class Signal:

        def __init__(self, name, by=1, primed=0):
            self.h, self.name, self.by, self.primed = ctx.enter_context(nc.semaphore(name)), name, by, primed
            named[name] = self

        def up(self):
            seen[self.name] = seen.get(self.name, 0) + 1
            return self.by

        def at(self, b, k):
            return b * (per.get(self.name, 1) * self.by) + (k + self.primed) * self.by

    def batch_starts():
        seen.clear()

    def batch_ends():
        for name, n in seen.items():
            totals[name] = totals.get(name, 0) + n

    with ctx:
        ident = sb("ident", [128, 128])
        wlT = sb("wlT", [C, LK])
        tok_bl = sb("tok_bl", [TT, LK])
        tok_mask = sb("tok_mask", [TT, TILES, LK])
        tok_bias = sb("tok_bias", [C, 1])
        conv_b = sb("conv_b", [128, OC])
        w2T = sb("w2T", [128, OC, C])
        b2 = sb("b2", [A, C])
        wc_hi = sb("wc_hi", [C, OC, TAPS * 128], F16)
        wc_lo = sb("wc_lo", [C, OC, TAPS * 128], F16)
        gamma = sb("gamma", [C, 1])
        beta = sb("beta", [C, 1])
        wqT = sb("wqT", [C, H0, 2 * DH])
        wkT = sb("wkT", [C, H0 * DH])
        wvT = sb("wvT", [C, H0 * DH])
        q_b = sb("q_b", [128, H0])
        uv = sb("uv", [128, H0])
        k_b = sb("k_b", [128, H0 // 2])
        v_b = sb("v_b", [A, H0 * DH])
        woT = sb("woT", [128, 4, C])
        bo = sb("bo", [A, C])
        gate0T = sb("gate0T", [C, E0])
        w1T = sb("w1T", [C, E0 * F0])
        w2eT = sb("w2eT", [128, E0 * 2, C])
        sgT = sb("sgT", [C, F0])
        suT = sb("suT", [C, F0])
        sdT = sb("sdT", [128, 2, C])
        winT = sb("winT", [C, 3 * C])
        bin_col = sb("bin_col", [C, 3])
        bin_row = sb("bin_row", [A, 3 * C])
        kvmask = sb("kvmask", [C, C])
        wo1T = sb("wo1T", [C, C])
        bo1 = sb("bo1", [A, C])
        gate1T = sb("gate1T", [C, E1])
        gate1_b = sb("gate1_b", [A, E1])
        slot_base = sb("slot_base", [A, J, E1])
        before = sb("before", [A, 8, 8])
        tokens = sb("tokens", [A, J])
        tri = sb("tri", [A, 3, A], BF16)
        minus_half = sb("minus_half", [A, J])
        gate_dve = sb("gate_dve", [A, 1])

        x_win = sb("x_win", [TW, TILES, C])
        x_T = sb("x_T", [C, TP])
        lg = sb("lg", [TT, TILES, LK])
        lmax = sb("lmax", [TT, TILES * HEADS_T])
        lsum = sb("lsum", [TT, TILES * HEADS_T])
        band_selu = sb("band_selu", [128, TILES * BROW])
        band = band_selu[0:TT, :].rearrange("p (i n) -> p i n", i=TILES)
        selu = band_selu[:, 0:OC * TOK].rearrange("p (o t) -> p o t", o=OC)
        zc = band_selu[:, OC * TOK:(OC + 1) * TOK]
        bandT = sb("bandT", [TW, 2, HEADS_T * TT])
        y32 = sb("y32", [C, TP])
        y_hi = sb("y_hi", [C, TP], F16)
        y_lo = sb("y_lo", [C, TP], F16)
        z = sb("z", [128, TOK])
        zneg = sb("zneg", [128, TOK])
        h0 = sb("h0", [A, J * C])

        bn = sb("bn", [A, J, 6])
        mv = sb("mv", [A, J, 2])
        ve = sb("ve", [A, J])
        rstd = sb("rstd", [A, J])
        xh = sb("xh", [A, J, C])
        xT = sb("xT", [C, TOK])
        qv = sb("qv", [128, H0 * TOK + J * H0 * DH])
        Q = qv[:, 0:H0 * TOK].rearrange("p (h t) -> p h t", h=H0)
        V = qv[0:A, H0 * TOK:].rearrange("p (j n) -> p j n", j=J)
        HALF = TAPS * 64
        stage = [qv[:, 0:HALF], qv[:, HALF:2 * HALF]]
        KP = sb("KP", [128, H0, TOK])
        nmax = sb("nmax", [A, 2])
        psums = sb("psums", [A, H0, J])
        prec = sb("prec", [A, H0, J])
        p_k1 = sb("p_k1", [A, 2 * TOK])
        pT_v1 = sb("pT_v1", [A, 2 * TOK])
        Pm = p_k1[:, :].rearrange("p (u t) -> p u t", u=2)
        PT = pT_v1[:, :].rearrange("p (u t) -> p u t", u=2)
        k1, v1 = p_k1[:, 0:3 * C], pT_v1[:, 0:3 * C]
        tri_f = Pm[:, 0, :].rearrange("p (m a) -> p m a", m=3)
        O = sb("O", [A, J, H0 * DH])
        OT = sb("OT", [128, J, 4 * A])
        OTf = OT[:, :, :].rearrange("p j n -> p (j n)")
        peT, wposT = OTf[:, 0:TOK], OTf[:, TOK:TOK + H0 * DH]
        h1 = sb("h1", [A, J * C])
        h2 = sb("h2", [A, J * C])
        h0b = h2
        h3 = sb("h3", [A, J * C])
        gl = sb("gl", [A, J * 8])
        gmx = sb("gmx", [A, J])
        cmp_a = sb("cmp_a", [A, J * 8, 8])
        cmp_b = sb("cmp_b", [A, J * 8, 8])
        rank = sb("rank", [A, J * 8])
        gsum = sb("gsum", [A, J])
        comb = sb("comb", [A, J * 8])
        th = sb("th", [128, 2, TOK])
        hid = sb("hid", [128, 4, TOK])
        sgate = sb("sgate", [128, TOK])
        qT1 = sb("qT1", [C, J, A])
        kv = sb("kv", [C, C])
        G = sb("G", [C, C])
        rows = sb("rows", [A, J, ROW])
        sc = sb("sc", [A, J, E1])
        ss = sb("ss", [A, J * 8, 8])
        thi = sb("thi", [A, J * 8, 4])
        tlo = sb("tlo", [A, J * 8, 4])
        tmi = sb("tmi", [A, J * 8, 2])
        gpen = sb("gpen", [A, J * 8])
        top = sb("top", [A, J, 8])
        mr = sb("mr", [A, J, E1])
        sel = sb("sel", [A, J, E1], BF16)
        carry = sb("carry", [A, E1])
        pos = sb("pos", [A, J, E1])
        slot_i = sb("slot_i", [A, J * 8], U32)

        W = [ctx.enter_context(nc.psum_tensor(f"W{i}", [128, 512], F32)) for i in range(4)]
        Ob = [ctx.enter_context(nc.psum_tensor(f"Ob{i}", [128, 512], F32)) for i in range(2)]
        Cb = [ctx.enter_context(nc.psum_tensor(f"Cb{i}", [128, 512], F32)) for i in range(2)]

        s_tokw = ctx.enter_context(nc.semaphore("tok_weights_loaded"))
        s_curw = ctx.enter_context(nc.semaphore("layer_weights_loaded"))
        s_stage = [ctx.enter_context(nc.semaphore(f"conv_stage_loaded{i}")) for i in range(2)]
        s_zero = ctx.enter_context(nc.semaphore("band_zeroed"))
        s_held = ctx.enter_context(nc.semaphore("pool_held"))
        s_bandz = ctx.enter_context(nc.semaphore("band_dram_zeroed"))
        s_hi = ctx.enter_context(nc.semaphore("conv_hi_ready"))
        s_lo = ctx.enter_context(nc.semaphore("conv_lo_ready"))
        s_set = ctx.enter_context(nc.semaphore("setup_dve_step"))
        s_pos = ctx.enter_context(nc.semaphore("setup_pos_ready"))
        s_posu = ctx.enter_context(nc.semaphore("setup_pos_used"))
        s_setup = ctx.enter_context(nc.semaphore("setup_done"))

        w_full = [Signal(f"w_full{i}") for i in range(4)]
        o_full = [Signal(f"o_full{i}") for i in range(2)]
        c_full = [Signal(f"c_full{i}") for i in range(2)]
        x_loaded = Signal("x_loaded", 16)
        lg_sub = Signal("lg_shifted")
        lg_exp = Signal("lg_exp")
        taps_ready = Signal("tap_weights_ready")
        band_out = Signal("band_written", 16)
        band_in = Signal("band_loaded", 16)
        bandT_ready = Signal("bandT_ready")
        y_ready = Signal("y_ready")
        y_split = Signal("y_split")
        zc_ready = Signal("cross_terms_ready")
        zneg_ready = Signal("zneg_ready")
        zexp_ready = Signal("zexp_ready")
        selu_ready = Signal("selu_ready")
        step_n = Signal("dve_step_next")
        step_c = Signal("dve_step")
        ln_var = Signal("ln_var_ready")
        ln_rstd = Signal("ln_rstd_ready")
        xh_ready = Signal("xh_ready")
        xT_ready = Signal("xT_ready")
        q_ready = Signal("q_ready")
        kvp_ready = Signal("kv_ready")
        nmax_ready = Signal("nmax_ready")
        p_ready = Signal("p_ready")
        pt_ready_a = Signal("pt_ready_scalar")
        pt_ready_d = Signal("pt_ready_vector")
        pv_done = Signal("pv_done")
        o_ready = Signal("o_ready")
        oT_ready = Signal("oT_ready")
        gexp_in = Signal("gate_shifted")
        gexp_out = Signal("gate_exp")
        th_ready = Signal("tanh_ready")
        hid_ready = Signal("hid_ready")
        qkv1_ready = Signal("qkv1_ready")
        kv_ready = Signal("kv_state_ready")
        g_ready = Signal("g_ready")
        y_added = Signal("y_added")
        h3_ready = Signal("h3_ready")
        h3_stored = Signal("h3_stored", 16, primed=1)
        sel_ready = Signal("sel_ready")
        rows_ready = Signal("rows_ready")
        rows_sent = Signal("rows_sent", 16, primed=1)

        def freed(use):
            at, prev = next((a, p) for a, p in ((W_AT, W_PREV), (O_AT, O_PREV), (C_AT, C_PREV)) if use in a)
            if not prev[use]:
                return at[use][0], None, 0
            name, k = FREED[prev[use]]
            return at[use][0], named[name], k

        def pt_used(eng, b, u):
            h, j = u // J, u % J
            if j == J - 1:
                bank, nth = O_AT[("O", h)]
                eng.wait_ge(o_full[bank].h, o_full[bank].at(b, nth))
            else:
                eng.wait_ge(pv_done.h, pv_done.at(b, 2 * h + j + 1))

        xpad, xTp = dram["xpad"], dram["xTp"]
        band_d = nc.dram_tensor("band_dram", (TILES, TT, BROW), F32, kind="Internal").ap()
        slots_d = nc.dram_tensor("slots_dram", (SLOTS, ROW), F32, kind="Internal").ap()
        band_skew = bass.AP(tensor=band_d.tensor, offset=0,
                            ap=[[BROW + HEADS_T, TT], [TT * BROW, TILES], [1, LK]])
        band_rows = band_d.rearrange("i t n -> t i n")

        tok_loads = [(ident, dram["ident"]), (wlT, dram["wlT"]), (tok_bl, dram["tok_bl"].partition_broadcast(TT)),
                     (tok_mask, dram["tok_mask"]), (tok_bias, dram["tok_bias"]), (conv_b, dram["conv_b"]),
                     (w2T, dram["w2T"]), (b2, dram["b2"].partition_broadcast(A))]
        layer_loads = [(gamma, dram["gamma"]), (beta, dram["beta"]),
                       (wqT[:, :, 0:DH], dram["wqT"]), (wqT[:, :, DH:], dram["wqT"]), (wkT, dram["wkT"]),
                       (wvT, dram["wvT"]), (q_b[0:DH, :], dram["q_b"]), (q_b[DH:, :], dram["q_b"]),
                       (k_b, dram["k_b"]), (v_b, dram["v_b"].partition_broadcast(A)), (peT, dram["peT"]),
                       (wposT, dram["wposT"]), (woT, dram["woT"]), (bo, dram["bo"].partition_broadcast(A)),
                       (gate0T, dram["gate0T"]), (w1T, dram["w1T"]), (w2eT, dram["w2eT"]), (sgT, dram["sgT"]),
                       (suT, dram["suT"]), (sdT, dram["sdT"]), (winT, dram["winT"]), (bin_col, dram["bin_col"]),
                       (bin_row, dram["bin_row"].partition_broadcast(A)), (kvmask, dram["kvmask"]),
                       (wo1T, dram["wo1T"]), (bo1, dram["bo1"].partition_broadcast(A)), (gate1T, dram["gate1T"]),
                       (gate1_b, dram["gate1_b"].partition_broadcast(A)), (tokens, dram["tokens"]), (tri_f, dram["tri"])]
        layer_loads.append((uv, dram["uv"]))

        def ap(x):
            return x if isinstance(x, bass.AP) else x.ap()

        tail_f = wc_hi[:, :, :].rearrange("p a b -> p (a b)").bitcast(F32)
        used = [0]

        def carve(n):
            used[0] += n
            assert used[0] <= OC * TAPS * 64
            return tail_f[:, used[0] - n:used[0]]

        e_rows = [carve(2 * ROW).rearrange("p (c n) -> p c n", c=2) for _ in range(2)]
        e_w13 = [carve(2 * F1) for _ in range(2)]
        e_w2 = [carve(C)[0:F1, :] for _ in range(2)]
        e_xT = [carve(CAP) for _ in range(2)]
        e_th = [carve(CAP)[0:F1, :] for _ in range(2)]
        e_s = carve(CAP)[0:F1, :]
        e_h = [carve(CAP)[0:F1, :] for _ in range(2)]
        e_y = [carve(2 * C).rearrange("p (c n) -> p c n", c=2) for _ in range(2)]
        e_idx = [carve(2).bitcast(U32) for _ in range(2)]

        t_load = [Signal(f"t_loaded{i}", 16) for i in range(2)]
        t_xps = [Signal(f"t_x_turned{i}") for i in range(2)]
        t_xT = [Signal(f"t_xT_ready{i}") for i in range(2)]
        t_hps = [Signal(f"t_h_full{i}") for i in range(2)]
        t_th = [Signal(f"t_tanh{i}") for i in range(2)]
        t_s = Signal("t_step")
        t_h = [Signal(f"t_h_ready{i}") for i in range(2)]
        t_yps = [Signal(f"t_y_full{i}") for i in range(2)]
        t_y = [Signal(f"t_y_ready{i}", primed=0) for i in range(2)]
        t_out = [Signal(f"t_added{i}", 16, primed=1) for i in range(2)]

        block = ctx.enter_context(nc.Block())

        @block.sync
        def _(sp):
            for dst, src in tok_loads:
                sp.dma_start(ap(dst) if not isinstance(dst, bass.AP) else dst, src).then_inc(s_tokw, 16)

            def load_x(nb):
                if not isinstance(nb, int):
                    sp.wait_ge(c_full[0].h, c_full[0].at(nb - 1, C_AT[("y", 0)][1]))
                src = bass.AP(tensor=xpad.tensor, offset=nb * ((TP + 30) * C),
                              ap=[[C, TW], [TT * C, TILES], [1, C]])
                sp.dma_start(x_win[:, :, :], src).then_inc(x_loaded.h, x_loaded.up())
                sp.dma_start(x_T[:, :], xTp[nb]).then_inc(x_loaded.h, x_loaded.up())

            def bands(nb):
                sp.wait_ge(taps_ready.h, taps_ready.at(nb, 1))
                sp.dma_start(band_skew, lg[:, :, :]).then_inc(band_out.h, band_out.up())
                sp.wait_ge(band_out.h, band_out.at(nb, 1))
                sp.dma_start(band[:, :, :], band_rows).then_inc(band_in.h, band_in.up())

            batch_starts()
            load_x(0)
            for n in range(2 * OC):
                if n >= 2:
                    sp.wait_ge(s_lo, n - 1)
                sp.dma_start(stage[n % 2], dram["wc"][n // 2, :, (n % 2) * HALF:(n % 2 + 1) * HALF])\
                    .then_inc(s_stage[n % 2], 16)
                if n == 0:
                    sp.wait_ge(s_zero, 1)
                    sp.dma_start(band_rows, band[:, :, :]).then_inc(s_bandz, 16)
                    sp.wait_ge(s_bandz, 16)
                if n == 1:
                    bands(0)
            with sp.Fori(0, B - 1) as it:
                batch_starts()
                load_x(it + 1)
                bands(it + 1)
                batch_ends()

            def load_expert(pr, i):
                e = pr * 2 + i
                if not (isinstance(pr, int) and pr == 0):
                    sp.wait_ge(t_y[i].h, t_y[i].at(pr - 1, 1))
                sp.dma_start(e_rows[i], slots_e[e]).then_inc(t_load[i].h, t_load[i].up())
                sp.dma_start(e_w13[i][:, 0:F1], dram["w1e"][e]).then_inc(t_load[i].h, t_load[i].up())
                sp.dma_start(e_w13[i][:, F1:], dram["w3e"][e]).then_inc(t_load[i].h, t_load[i].up())
                sp.dma_start(e_w2[i], dram["w2e"][e]).then_inc(t_load[i].h, t_load[i].up())

            slots_e = slots_d.rearrange("(e c p) n -> e p c n", c=2, p=128)
            sp.wait_ge(rows_sent.h, rows_sent.at(B - 1, J * 8))
            sp.wait_ge(w_full[W_AT[("count", 0)][0]].h, w_full[W_AT[("count", 0)][0]].at(B - 1, W_AT[("count", 0)][1]))
            batch_starts()
            for i in range(2):
                load_expert(0, i)
            with sp.Fori(1, E1 // 2) as pr:
                batch_starts()
                for i in range(2):
                    load_expert(pr, i)
                batch_ends()

        @block.gpsimd
        def _(pool):
            pool.memset(minus_half[:, :], -0.5)
            pool.memset(band[:, :, :], 0.0).then_inc(s_zero, 1)
            pool.dma_start(slots_d.rearrange("(e s) n -> e (s n)", e=E1),
                           dram["empty_slots"].rearrange("s n -> (s n)").unsqueeze(0).to_broadcast((E1, CAP * ROW)))\
                .then_inc(rows_sent.h, 16)
            pool.dma_start(out[NTOK:, :], dram["empty_slots"][:, 0:C]).then_inc(h3_stored.h, 16)
            for sig, (dst, src) in zip(t_out, ((slot_base, dram["slot_base"]), (before, dram["before"]))):
                pool.dma_start(ap(dst), src).then_inc(sig.h, 16)
            pool.wait_ge(rows_sent.h, 16)
            pool.wait_ge(h3_stored.h, 16)

            def hold():
                pool.sem_inc(s_held, 1)

            def power(b, n):
                pool.wait_ge(ln_var.h, ln_var.at(b, n))
                pool.tensor_tensor(rstd[:, :], ve[:, :], minus_half[:, :], ALU.pow).then_inc(ln_rstd.h, ln_rstd.up())

            def send(b):
                pool.wait_ge(h3_ready.h, h3_ready.at(b, 1))
                src = h3[:, :]
                dst = bass.AP(tensor=out.tensor, offset=b * (TOK * C), ap=[[J * C, A], [1, J * C]])
                pool.dma_start(dst, src).then_inc(h3_stored.h, h3_stored.up())
                pool.wait_ge(rows_ready.h, rows_ready.at(b, 1))
                hold()
                for j in range(J):
                    for k in range(8):
                        pool.indirect_dma_start(
                            out=slots_d, out_offset=bass.IndirectOffsetOnAxis(ap=slot_i[:, j * 8 + k:j * 8 + k + 1], axis=0),
                            in_=rows[:, j, :], in_offset=None, bounds_check=SLOTS - 1, oob_is_err=False).then_inc(rows_sent.h, rows_sent.up())

            power(0, 1)
            with pool.Fori(0, B - 1) as it:
                batch_starts()
                for n in 2, 3, 4:
                    power(it, n)
                power(it + 1, 1)
                send(it)
                batch_ends()
            for n in 2, 3, 4:
                power(B - 1, n)
            send(B - 1)
            pool.wait_ge(h3_stored.h, h3_stored.at(B - 1, 1))
            pool.wait_ge(rows_sent.h, rows_sent.at(B - 1, J * 8))

            def add_rows(pr, i):
                pool.wait_ge(t_y[i].h, t_y[i].at(pr, 1))
                if i == 1:
                    pool.wait_ge(t_out[0].h, t_out[0].at(pr, 2))
                else:
                    pool.wait_ge(t_out[1].h, t_out[1].at(pr, 0))
                hold()
                for c in range(2):
                    pool.indirect_dma_start(
                        out=out, out_offset=bass.IndirectOffsetOnAxis(ap=e_idx[i][:, c:c + 1], axis=0),
                        in_=e_y[i][:, c, :], in_offset=None, bounds_check=NTOK + CAP - 1, oob_is_err=True,
                        compute_op=ALU.add).then_inc(t_out[i].h, t_out[i].up())

            with pool.Fori(0, E1 // 2) as pr:
                batch_starts()
                for i in range(2):
                    add_rows(pr, i)
                batch_ends()
            for s in t_out:
                pool.wait_ge(s.h, s.at(E1 // 2 - 1, 2))

        @block.tensor
        def _(pe):
            def mm(o, l, r, start=True, stop=True):
                return pe.matmul(o, l, r, start=start, stop=stop)

            def tok_logits(nb):
                i, was, nth = freed(("lg", 0))
                if was:
                    pe.wait_ge(was.h, was.at(nb, nth))
                pe.wait_ge(x_loaded.h, x_loaded.at(nb, 2))
                for t in range(TILES):
                    last = mm(Cb[i][0:TT, t * LK:(t + 1) * LK], x_T[:, t * TT:(t + 1) * TT], wlT[:, :])
                last.then_inc(c_full[i].h, c_full[i].up())

            def tok_mix(nb):
                pe.wait_ge(band_in.h, band_in.at(nb, 1))
                y, was, nth = freed(("y", 0))
                if was:
                    pe.wait_ge(was.h, was.at(nb, nth))
                for t in range(TILES + 1):
                    if t < TILES:
                        i, was, nth = freed(("bT", t))
                        if was:
                            pe.wait_ge(was.h, was.at(nb, nth))
                        for h in range(HEADS_T):
                            last = pe.transpose(Cb[i][0:TW, h * TT:(h + 1) * TT],
                                                band[:, t, h::HEADS_T], ident[0:TT, 0:TT])
                        last.then_inc(c_full[i].h, c_full[i].up())
                    if t >= 1:
                        u = t - 1
                        pe.wait_ge(bandT_ready.h, bandT_ready.at(nb, u + 1))
                        for h in range(HEADS_T):
                            last = mm(Cb[y][32 * h:32 * h + 32, u * TT:(u + 1) * TT],
                                      x_win[:, u, 32 * h:32 * h + 32], bandT[:, u % 2, h * TT:(h + 1) * TT])
                last.then_inc(c_full[y].h, c_full[y].up())

            def conv(nb, p):
                if nb is None:
                    return
                o, m0, m1 = FILL[p]
                if m0 == 0:
                    bank, was, nth = freed(("main", o))
                    if was:
                        pe.wait_ge(was.h, was.at(nb, nth))
                    bank, was, nth = freed(("cross", o))
                    if was:
                        pe.wait_ge(was.h, was.at(nb, nth))
                    if o == 0:
                        pe.wait_ge(y_split.h, y_split.at(nb, 1))
                    if isinstance(nb, int) and nb == 0:
                        pe.wait_ge(s_lo, 2 * o + 2)
                for m in range(m0, m1):
                    k, what = m // PASSES, m % PASSES
                    whi = wc_hi[:, o, k * 128:(k + 1) * 128]
                    wlo = wc_lo[:, o, k * 128:(k + 1) * 128]
                    yh, yl = y_hi[:, k:k + TOK], y_lo[:, k:k + TOK]
                    if what == 0:
                        last = mm(Cb[0][:, 0:TOK], whi, yh, start=(k == 0), stop=(k == TAPS - 1))
                        if k == TAPS - 1:
                            last.then_inc(c_full[0].h, c_full[0].up())
                    elif what == 1:
                        mm(Cb[1][:, 0:TOK], whi, yl, start=(k == 0), stop=False)
                    else:
                        last = mm(Cb[1][:, 0:TOK], wlo, yh, start=False, stop=(k == TAPS - 1))
                        if k == TAPS - 1:
                            last.then_inc(c_full[1].h, c_full[1].up())

            def tok_out(nb):
                i, was, nth = freed(("w2", 0))
                if was:
                    pe.wait_ge(was.h, was.at(nb, nth))
                pe.wait_ge(selu_ready.h, selu_ready.at(nb, OC))
                for j in range(J):
                    for o in range(OC):
                        last = mm(Cb[i][0:A, j * C:(j + 1) * C], selu[:, o, j::J], w2T[:, o, :],
                                  start=(o == 0), stop=(o == OC - 1))
                last.then_inc(c_full[i].h, c_full[i].up())

            def turn(b, n):
                pe.wait_ge(xh_ready.h, xh_ready.at(b, n))
                i, was, nth = freed(("ln", n))
                if was:
                    pe.wait_ge(was.h, was.at(b, nth))
                for j in range(J):
                    src = xh[:, j, :] if n < 4 else rows[:, j, 0:C]
                    last = pe.transpose(W[i][:, j * A:(j + 1) * A], src, ident[0:A, 0:A])
                last.then_inc(w_full[i].h, w_full[i].up())
                pe.wait_ge(xT_ready.h, xT_ready.at(b, n))

            def step(b, use, what, extra=None):
                i, was, nth = freed(use)
                if was:
                    pe.wait_ge(was.h, was.at(b, nth))
                what(W[i]).then_inc(w_full[i].h, w_full[i].up())

            def present(b, nb):
                turn(b, 1)
                if nb is not None:
                    tok_logits(nb)
                for h in range(H0):
                    step(b, ("q", h), lambda w: mm(w[:, 0:TOK], wqT[:, h, :], xT[:, :]))
                    if h % 2 == 0:
                        g = h // 2
                        step(b, ("k", g), lambda w: mm(w[:, 0:TOK], wkT[:, g * 128:(g + 1) * 128], xT[:, :]))
                for j in range(J):
                    step(b, ("v", j), lambda w: mm(w[0:A, :], xT[:, j * A:(j + 1) * A], wvT[:, :]))
                if nb is not None:
                    tok_mix(nb)
                pe.wait_ge(q_ready.h, q_ready.at(b, H0))
                pe.wait_ge(kvp_ready.h, kvp_ready.at(b, H0 // 2 + J))

                def turn_p(w, u):
                    for i in range(J):
                        last = pe.transpose(w[0:A, i * A:(i + 1) * A], Pm[:, u % 2, i * A:(i + 1) * A], ident[0:A, 0:A])
                    return last

                for s in range(UNITS + 2):
                    if s < UNITS:
                        h, j = s // J, s % J
                        step(b, ("S", s), lambda w: mm(w[0:A, 0:TOK], Q[:, h, j * A:(j + 1) * A], KP[:, h, :]))
                        conv(nb, s)
                    if 1 <= s <= UNITS:
                        u = s - 1
                        pe.wait_ge(p_ready.h, p_ready.at(b, u + 1))
                        step(b, ("T", u), lambda w: turn_p(w, u))
                    if s >= 2:
                        u = s - 2
                        h, j = u // J, u % J
                        if j == 0:
                            o, was, nth = freed(("O", h))
                            if was:
                                pe.wait_ge(was.h, was.at(b, nth))
                        pe.wait_ge((pt_ready_a, pt_ready_d)[u % 2].h, (pt_ready_a, pt_ready_d)[u % 2].at(b, u // 2 + 1))
                        for i in range(J):
                            last = mm(Ob[o][0:A, j * DH:(j + 1) * DH], PT[:, u % 2, i * A:(i + 1) * A],
                                      V[:, i, h * DH:(h + 1) * DH], start=(i == 0), stop=(i == J - 1))
                        pv = o_full[o] if j == J - 1 else pv_done
                        last.then_inc(pv.h, pv.up())

                pe.wait_ge(o_ready.h, o_ready.at(b, H0))
                for j in range(J):
                    i, was, nth = freed(("oT", j))
                    if was:
                        pe.wait_ge(was.h, was.at(b, nth))
                    for c in range(4):
                        last = pe.transpose(W[i][:, c * A:(c + 1) * A], O[:, j, c * 128:(c + 1) * 128], ident[0:A, 0:A])
                    last.then_inc(w_full[i].h, w_full[i].up())
                i, was, nth = freed(("out0", 0))
                if was:
                    pe.wait_ge(was.h, was.at(b, nth))
                for j in range(J):
                    pe.wait_ge(oT_ready.h, oT_ready.at(b, j + 1))
                    for c in range(4):
                        last = mm(W[i][0:A, j * C:(j + 1) * C], OT[:, j, c * A:(c + 1) * A], woT[:, c, :],
                                  start=(c == 0), stop=(c == 3))
                last.then_inc(w_full[i].h, w_full[i].up())

                turn(b, 2)

                def gate(w, width, wt):
                    for j in range(J):
                        last = mm(w[0:A, j * width:(j + 1) * width], xT[:, j * A:(j + 1) * A], wt[:, :])
                    return last
                step(b, ("gate0", 0), lambda w: gate(w, E0, gate0T))
                p = UNITS

                def mix(e):
                    pe.wait_ge(hid_ready.h, hid_ready.at(b, 2 * e + 2))
                    o, was, nth = freed(("Y", e))
                    if was:
                        pe.wait_ge(was.h, was.at(b, nth))
                    for j in range(J):
                        for c in range(2):
                            wt = w2eT[:, 2 * e + c, :] if e < E0 else sdT[:, c, :]
                            last = mm(Ob[o][0:A, j * C:(j + 1) * C], hid[:, 2 * (e % 2) + c, j * A:(j + 1) * A], wt,
                                      start=(c == 0), stop=(c == 1))
                    last.then_inc(o_full[o].h, o_full[o].up())

                for e in range(E0 + 1):
                    for c in range(2):
                        if e < E0:
                            n = 2 * e + c
                            step(b, ("hid", n), lambda w: mm(w[:, 0:TOK], w1T[:, n * 128:(n + 1) * 128], xT[:, :]))
                        else:
                            step(b, ("sg", c), lambda w: mm(w[:, 0:TOK], sgT[:, c * 128:(c + 1) * 128], xT[:, :]))
                            step(b, ("su", c), lambda w: mm(w[:, 0:TOK], suT[:, c * 128:(c + 1) * 128], xT[:, :]))
                        conv(nb, p)
                        p += 1
                    if e >= 1:
                        mix(e - 1)
                conv(nb, p)
                p += 1
                mix(E0)

                conv(nb, p)
                p += 1
                turn(b, 3)

                def three(w):
                    for j in range(J):
                        last = mm(w[:, j * A:(j + 1) * A], winT[:, j * C:(j + 1) * C], xT[:, 0:A])
                    return last
                step(b, ("q1", 0), three)
                step(b, ("k1", 0), lambda w: mm(w[0:A, 0:3 * C], xT[:, A:2 * A], winT[:, :]))
                step(b, ("v1", 0), lambda w: mm(w[0:A, 0:3 * C], xT[:, 2 * A:3 * A], winT[:, :]))
                conv(nb, p)
                p += 1
                pe.wait_ge(qkv1_ready.h, qkv1_ready.at(b, 3))

                def state(w):
                    for j in range(J):
                        last = mm(w[:, 0:C], v1[:, j * C:(j + 1) * C], k1[:, j * C:(j + 1) * C],
                                  start=(j == 0), stop=(j == J - 1))
                    return last
                step(b, ("kv", 0), state)
                conv(nb, p)
                p += 1
                pe.wait_ge(kv_ready.h, kv_ready.at(b, 1))
                step(b, ("g", 0), lambda w: mm(w[:, 0:C], kv[:, :], wo1T[:, :]))
                conv(nb, p)
                p += 1
                pe.wait_ge(g_ready.h, g_ready.at(b, 1))

                def outs(w):
                    for j in range(J):
                        last = mm(w[0:A, j * C:(j + 1) * C], qT1[:, j, :], G[:, :])
                    return last
                step(b, ("out1", 0), outs)
                conv(nb, p)
                p += 1

                turn(b, 4)
                step(b, ("gate1", 0), lambda w: gate(w, E1, gate1T))
                conv(nb, p)
                p += 1
                conv(nb, p)
                p += 1
                assert p == POINTS
                if nb is not None:
                    tok_out(nb)
                pe.wait_ge(sel_ready.h, sel_ready.at(b, 1))

                def counts(w):
                    for j in range(J + 1):
                        for q in range(J):
                            m = 2 if j == J else 1 if q < j else 0
                            last = mm(w[0:A, j * E1:(j + 1) * E1], tri[:, m, :], sel[:, q, :],
                                      start=(q == 0), stop=(q == J - 1))
                    return last
                step(b, ("count", 0), counts)

            pe.wait_ge(s_tokw, 16 * len(tok_loads))
            batch_starts()
            tok_logits(0)
            tok_mix(0)
            pe.wait_ge(s_curw, 16 * len(layer_loads))
            for g in range(H0 // 2):
                if g >= 2:
                    pe.wait_ge(s_posu, g - 1)
                mm(W[g % 2][:, 0:TOK], wposT[:, g * 128:(g + 1) * 128], peT).then_inc(s_pos, 1)
            for p in range(POINTS):
                conv(0, p)
            tok_out(0)
            pe.wait_ge(s_setup, 1)
            with pe.Fori(0, B - 1) as it:
                batch_starts()
                present(it, it + 1)
                batch_ends()
            present(B - 1, None)

            def expert_in(pr, i):
                pe.wait_ge(t_load[i].h, t_load[i].at(pr, 4))
                for c in range(2):
                    last = pe.transpose(W[i][:, c * 128:(c + 1) * 128], e_rows[i][:, c, 0:C], ident[:, :])
                last.then_inc(t_xps[i].h, t_xps[i].up())

            def expert_up(pr, i):
                pe.wait_ge(t_xT[i].h, t_xT[i].at(pr, 1))
                mm(W[2 + i][0:F1, 0:CAP], e_w13[i][:, 0:F1], e_xT[i])
                mm(Ob[i][0:F1, 0:CAP], e_w13[i][:, F1:], e_xT[i]).then_inc(t_hps[i].h, t_hps[i].up())

            def expert_down(pr, i):
                pe.wait_ge(t_h[i].h, t_h[i].at(pr, 1))
                for c in range(2):
                    last = mm(Cb[i][:, c * C:(c + 1) * C], e_h[i][:, c * 128:(c + 1) * 128], e_w2[i])
                last.then_inc(t_yps[i].h, t_yps[i].up())

            with pe.Fori(0, E1 // 2) as pr:
                batch_starts()
                for i in range(2):
                    expert_in(pr, i)
                for i in range(2):
                    expert_up(pr, i)
                for i in range(2):
                    expert_down(pr, i)
                batch_ends()

        @block.scalar
        def _(act):
            for dst, src in layer_loads:
                act.dma_start(ap(dst) if not isinstance(dst, bass.AP) else dst, src).then_inc(s_curw, 16)

            def tok_exp(nb):
                act.wait_ge(lg_sub.h, lg_sub.at(nb, 1))
                act.activation(lg[:, :, :], lg[:, :, :], ACT.Exp).then_inc(lg_exp.h, lg_exp.up())

            def tok_band(nb):
                for t in range(TILES):
                    i, nth = C_AT[("bT", t)]
                    act.wait_ge(c_full[i].h, c_full[i].at(nb, nth))
                    ins = act.activation(bandT[:, t % 2, :], Cb[i][0:TW, 0:HEADS_T * TT], ACT.Copy)
                    ins.then_inc(bandT_ready.h, bandT_ready.up())
                i, nth = C_AT[("y", 0)]
                act.wait_ge(c_full[i].h, c_full[i].at(nb, nth))
                ins = act.activation(y32[:, :], Cb[i][:, 0:TP], ACT.Identity, bias=tok_bias[:, 0:1])
                ins.then_inc(y_ready.h, y_ready.up())

            def conv_out(nb, p):
                if nb is None or p not in CHUNK_END:
                    return
                o = CHUNK_END[p]
                i, nth = C_AT[("cross", o)]
                act.wait_ge(c_full[i].h, c_full[i].at(nb, nth))
                if o >= 1 or not (isinstance(nb, int) and nb == 0):
                    act.wait_ge(zneg_ready.h, zneg_ready.at(nb, o))
                ins = act.activation(zc, Cb[i][:, 0:TOK], ACT.Identity, bias=conv_b[:, o:o + 1], scale=1.0 / LO)
                ins.then_inc(zc_ready.h, zc_ready.up())
                act.wait_ge(zneg_ready.h, zneg_ready.at(nb, o + 1))
                act.activation(zneg[:, :], zneg[:, :], ACT.Exp).then_inc(zexp_ready.h, zexp_ready.up())

            def tanh_in(b, use, n):
                i, nth = W_AT[use]
                act.wait_ge(w_full[i].h, w_full[i].at(b, nth))
                if n >= 2:
                    act.wait_ge(hid_ready.h, hid_ready.at(b, n - 1))
                act.activation(th[:, n % 2, :], W[i][:, 0:TOK], ACT.Tanh, scale=0.5).then_inc(th_ready.h, th_ready.up())

            def present(b, nb):
                if nb is not None:
                    tok_exp(nb)
                for h in range(H0):
                    i, nth = W_AT[("q", h)]
                    act.wait_ge(w_full[i].h, w_full[i].at(b, nth))
                    act.activation(Q[:, h, :], W[i][:, 0:TOK], ACT.Identity, bias=q_b[:, h:h + 1],
                                              scale=DH ** -0.5).then_inc(q_ready.h, q_ready.up())
                if nb is not None:
                    tok_band(nb)
                for s in range(UNITS + 1):
                    if s < UNITS:
                        i, nth = W_AT[("S", s)]
                        act.wait_ge(w_full[i].h, w_full[i].at(b, nth))
                        if s >= 2:
                            bank, nth = W_AT[("T", s - 2)]
                            act.wait_ge(w_full[bank].h, w_full[bank].at(b, nth))
                        act.wait_ge(nmax_ready.h, nmax_ready.at(b, s + 1))
                        act.activation(Pm[:, s % 2, :], W[i][0:A, 0:TOK], ACT.Exp,
                                                  bias=nmax[:, s % 2:s % 2 + 1],
                                                  accum_out=psums[:, s // J, s % J:s % J + 1]).then_inc(p_ready.h, p_ready.up())
                        conv_out(nb, s)
                    if s >= 1 and (s - 1) % 2 == 0:
                        u = s - 1
                        i, nth = W_AT[("T", u)]
                        act.wait_ge(w_full[i].h, w_full[i].at(b, nth))
                        if u >= 2:
                            pt_used(act, b, u - 2)
                        act.activation(PT[:, 0, :], W[i][0:A, 0:TOK], ACT.Copy).then_inc(pt_ready_a.h, pt_ready_a.up())
                for j in range(J):
                    i, nth = W_AT[("oT", j)]
                    act.wait_ge(w_full[i].h, w_full[i].at(b, nth))
                    act.activation(OT[:, j, :], W[i][:, 0:4 * A], ACT.Copy).then_inc(oT_ready.h, oT_ready.up())
                act.wait_ge(gexp_in.h, gexp_in.at(b, 1))
                act.activation(gl[:, :], gl[:, :], ACT.Exp).then_inc(gexp_out.h, gexp_out.up())
                p = UNITS
                for n in range(2 * (E0 + 1)):
                    tanh_in(b, ("hid", n) if n < 2 * E0 else ("sg", n - 2 * E0), n)
                    conv_out(nb, p)
                    p += 1
                for _ in range(5):
                    conv_out(nb, p)
                    p += 1
                conv_out(nb, p)
                p += 1
                i, nth = W_AT[("gate1", 0)]
                act.wait_ge(w_full[i].h, w_full[i].at(b, nth))
                act.activation(sc[:, :, :], W[i][0:A, 0:J * E1], ACT.Exp, scale=-1.0).then_inc(gexp_out.h, gexp_out.up())
                for _ in range(2):
                    conv_out(nb, p)
                    p += 1
                assert p == POINTS

            act.wait_ge(s_tokw, 16 * len(tok_loads))
            batch_starts()
            tok_exp(0)
            for n in range(2 * OC):
                act.wait_ge(s_stage[n % 2], 16 * (n // 2 + 1))
                act.activation(wc_hi[:, n // 2, (n % 2) * HALF:(n % 2 + 1) * HALF], stage[n % 2], ACT.Copy).then_inc(s_hi, 1)
                if n == 3:
                    tok_band(0)
            for p in range(POINTS):
                conv_out(0, p)
            act.wait_ge(s_setup, 1)
            with act.Fori(0, B - 1) as it:
                batch_starts()
                present(it, it + 1)
                batch_ends()
            present(B - 1, None)

            with act.Fori(0, E1 // 2) as pr:
                batch_starts()
                for i in range(2):
                    act.wait_ge(t_xps[i].h, t_xps[i].at(pr, 1))
                    act.activation(e_xT[i], W[i][:, 0:CAP], ACT.Copy).then_inc(t_xT[i].h, t_xT[i].up())
                for i in range(2):
                    act.wait_ge(t_hps[i].h, t_hps[i].at(pr, 1))
                    act.activation(e_th[i], W[2 + i][0:F1, 0:CAP], ACT.Tanh, scale=0.5).then_inc(t_th[i].h, t_th[i].up())
                batch_ends()

        @block.vector
        def _(dve):
            chain = [step_n, 0, 0]

            def link(ins):
                sig, b, k = chain
                ins.then_inc(sig.h, sig.up())
                chain[2] = k + 1
                dve.wait_ge(sig.h, sig.at(b, k + 1))

            def tok_softmax(nb):
                chain[:] = [step_n, nb, 0]
                i, nth = C_AT[("lg", 0)]
                dve.wait_ge(c_full[i].h, c_full[i].at(nb, nth))
                if not (isinstance(nb, int) and nb == 0):
                    dve.wait_ge(band_out.h, band_out.at(nb, 0))
                lgf = lg[:, :, :].rearrange("p i n -> p (i n)")
                ins = dve.tensor_tensor(lg[:, :, :], Cb[i][0:TT, 0:TILES * LK].rearrange("p (i n) -> p i n", i=TILES),
                                        tok_mask[:, :, :], ALU.add)
                link(ins)
                by_head = lg[:, :, :].rearrange("p i (k h) -> p i h k", h=HEADS_T)
                flat = lambda x: x[:, :].rearrange("p (i h) -> p i h", h=HEADS_T)
                spread = lambda x: flat(x).unsqueeze(3).to_broadcast((TT, TILES, HEADS_T, TAPS))
                link(dve.tensor_reduce(flat(lmax), by_head, AX.X, ALU.max))
                dve.tensor_tensor(by_head, by_head, spread(lmax), ALU.subtract).then_inc(lg_sub.h, lg_sub.up())
                dve.wait_ge(lg_exp.h, lg_exp.at(nb, 1))
                link(dve.tensor_reduce(flat(lsum), by_head, AX.X, ALU.add))
                link(dve.reciprocal(lsum[:, :], lsum[:, :]))
                dve.tensor_tensor(by_head, by_head, spread(lsum), ALU.mult).then_inc(taps_ready.h, taps_ready.up())
                return chain[2]

            def tok_split(nb, k):
                chain[:] = [step_n, nb, k]
                dve.wait_ge(y_ready.h, y_ready.at(nb, 1))
                link(dve.tensor_copy(y_hi[:, :], y32[:, :]))
                link(dve.tensor_tensor(y32[:, :], y32[:, :], y_hi[:, :], ALU.subtract))
                dve.tensor_scalar(y_lo[:, :], y32[:, :], LO, None, ALU.mult).then_inc(y_split.h, y_split.up())
                return chain[2]

            kn = [0]

            def conv_out(nb, p):
                if nb is None or p not in CHUNK_END:
                    return
                saved = list(chain)
                chain[:] = [step_n, nb, kn[0]]
                o = CHUNK_END[p]
                i, nth = C_AT[("main", o)]
                dve.wait_ge(c_full[i].h, c_full[i].at(nb, nth))
                dve.wait_ge(zc_ready.h, zc_ready.at(nb, o + 1))
                link(dve.tensor_tensor(z[:, :], Cb[i][:, 0:TOK], zc, ALU.add))
                dve.tensor_scalar(zneg[:, :], z[:, :], 0.0, None, ALU.min).then_inc(zneg_ready.h, zneg_ready.up())
                dve.wait_ge(zneg_ready.h, zneg_ready.at(nb, o + 1))
                link(dve.tensor_scalar(z[:, :], z[:, :], 0.0, ALPHA, ALU.max, ALU.subtract))
                dve.wait_ge(zexp_ready.h, zexp_ready.at(nb, o + 1))
                ins = dve.scalar_tensor_tensor(selu[:, o, :], zneg[:, :], ALPHA, z[:, :], ALU.mult, ALU.add)
                ins.then_inc(selu_ready.h, selu_ready.up())
                dve.wait_ge(selu_ready.h, selu_ready.at(nb, o + 1))
                kn[0] = chain[2]
                chain[:] = saved

            def tok_out(nb):
                i, nth = C_AT[("w2", 0)]
                dve.wait_ge(c_full[i].h, c_full[i].at(nb, nth))
                chain[:] = [step_n, nb, kn[0]]
                h = h0[:, :].rearrange("p (j c) -> p j c", j=J)
                link(dve.scalar_tensor_tensor(h, Cb[i][0:A, 0:J * C].rearrange("p (j c) -> p j c", j=J), LAMBDA,
                                              b2[:, :].unsqueeze(1).to_broadcast((A, J, C)), ALU.mult, ALU.add))

            def hold():
                dve.memset(gate_dve[:, :], 0.0)

            def norm(b, n, src):
                for j in range(J):
                    ins = dve.bn_stats(bn[:, j, :], src[:, j * C:(j + 1) * C])
                link(ins)
                hold()
                for j in range(J):
                    ins = dve.bn_aggr(mv[:, j, :], bn[:, j, :])
                link(ins)
                if n == 1:
                    ins = dve.tensor_scalar(ve[:, :], mv[:, :, 1], 1.0 + EPS, EPS * EPS, ALU.mult, ALU.add)
                else:
                    ins = dve.tensor_scalar(ve[:, :], mv[:, :, 1], EPS, None, ALU.add)
                ins.then_inc(ln_var.h, ln_var.up())
                dve.wait_ge(ln_rstd.h, ln_rstd.at(b, n))
                for j in range(J):
                    dst = xh[:, j, :] if n < 4 else rows[:, j, 0:C]
                    ins = dve.tensor_scalar(dst, src[:, j * C:(j + 1) * C], mv[:, j, 0:1], rstd[:, j:j + 1],
                                            ALU.subtract, ALU.mult)
                ins.then_inc(xh_ready.h, xh_ready.up())
                i, nth = W_AT[("ln", n)]
                dve.wait_ge(w_full[i].h, w_full[i].at(b, nth))
                if n == 1:
                    ins = dve.tensor_scalar(xT[:, :], W[i][:, 0:TOK], gamma[:, 0:1], beta[:, 0:1], ALU.mult, ALU.add)
                elif n == 3:
                    ins = dve.tensor_copy(xT[:, :].rearrange("c (a j) -> c j a", j=J),
                                          W[i][:, 0:TOK].rearrange("c (j a) -> c j a", j=J))
                else:
                    ins = dve.tensor_copy(xT[:, :], W[i][:, 0:TOK])
                ins.then_inc(xT_ready.h, xT_ready.up())

            def ranks(score):
                sview = score.rearrange("p (j g) -> p j g", g=8)
                ca = cmp_a[:, :, :].rearrange("p (j g) q -> p j g q", j=J)
                cb = cmp_b[:, :, :].rearrange("p (j g) q -> p j g q", j=J)
                other = sview.unsqueeze(2).to_broadcast((A, J, 8, 8))
                own = sview.unsqueeze(3).to_broadcast((A, J, 8, 8))
                low = before[:, :, :].unsqueeze(1).to_broadcast((A, J, 8, 8))
                dve.tensor_tensor(cb, other, own, ALU.is_gt)
                link(dve.tensor_tensor(ca, other, own, ALU.is_ge))
                link(dve.tensor_tensor(ca, ca, low, ALU.mult))
                link(dve.tensor_tensor(ca, ca, cb, ALU.max))
                link(dve.tensor_reduce(rank[:, :], cmp_a[:, :, :], AX.X, ALU.add))

            def present(b, nb):
                chain[:] = [step_c, b, 0]
                norm(b, 1, h0)
                kc = chain[2]
                if nb is not None:
                    kn[0] = tok_softmax(nb)
                chain[:] = [step_c, b, kc]
                for h in range(0, H0, 2):
                    g = h // 2
                    i, nth = W_AT[("k", g)]
                    dve.wait_ge(w_full[i].h, w_full[i].at(b, nth))
                    dve.tensor_scalar(KP[0:DH, h, :], W[i][0:DH, 0:TOK], k_b[0:DH, g:g + 1], None, ALU.add)
                    dve.tensor_scalar(KP[DH:, h + 1, :], W[i][DH:, 0:TOK], k_b[DH:, g:g + 1], None, ALU.add).then_inc(kvp_ready.h, kvp_ready.up())
                for j in range(J):
                    i, nth = W_AT[("v", j)]
                    dve.wait_ge(w_full[i].h, w_full[i].at(b, nth))
                    dve.tensor_tensor(V[:, j, :], W[i][0:A, :], v_b[:, :], ALU.add).then_inc(kvp_ready.h, kvp_ready.up())
                if nb is not None:
                    kn[0] = tok_split(nb, kn[0])
                chain[:] = [step_c, b, kc]
                for s in range(UNITS + 3):
                    if s < UNITS:
                        i, nth = W_AT[("S", s)]
                        dve.wait_ge(w_full[i].h, w_full[i].at(b, nth))
                        if s >= 2:
                            dve.wait_ge(p_ready.h, p_ready.at(b, s - 1))
                        dve.tensor_reduce(nmax[:, s % 2:s % 2 + 1], W[i][0:A, 0:TOK], AX.X, ALU.max,
                                                        negate=True).then_inc(nmax_ready.h, nmax_ready.up())
                    if 1 <= s <= UNITS and (s - 1) % 2 == 1:
                        u = s - 1
                        i, nth = W_AT[("T", u)]
                        dve.wait_ge(w_full[i].h, w_full[i].at(b, nth))
                        if u >= 2:
                            pt_used(dve, b, u - 2)
                        dve.tensor_copy(PT[:, 1, :], W[i][0:A, 0:TOK]).then_inc(pt_ready_d.h, pt_ready_d.up())
                    if s < UNITS:
                        conv_out(nb, s)
                    if s >= 4 and (s - 4) % J == J - 1 and (s - 4) // J < H0 - 1 or s == UNITS + 2:
                        h = (s - 4) // J if s < UNITS + 2 else H0 - 1
                        dve.wait_ge(p_ready.h, p_ready.at(b, J * h + J))
                        link(dve.reciprocal(prec[:, h, :], psums[:, h, :]))
                        i, nth = O_AT[("O", h)]
                        dve.wait_ge(o_full[i].h, o_full[i].at(b, nth))
                        dve.tensor_tensor(
                            O[:, :, h * DH:(h + 1) * DH], Ob[i][0:A, 0:J * DH].rearrange("p (j d) -> p j d", j=J),
                            prec[:, h, :].unsqueeze(2).to_broadcast((A, J, DH)), ALU.mult).then_inc(o_ready.h, o_ready.up())
                link(dve.tensor_tensor(h0b[:, :].rearrange("p (j c) -> p j c", j=J),
                                       h0[:, :].rearrange("p (j c) -> p j c", j=J),
                                       bo[:, :].unsqueeze(1).to_broadcast((A, J, C)), ALU.add))
                i, nth = W_AT[("out0", 0)]
                dve.wait_ge(w_full[i].h, w_full[i].at(b, nth))
                link(dve.tensor_tensor(h1[:, :], W[i][0:A, 0:J * C], h0b[:, :], ALU.add))

                norm(b, 2, h1)
                i, nth = W_AT[("gate0", 0)]
                dve.wait_ge(w_full[i].h, w_full[i].at(b, nth))
                link(dve.tensor_copy(gl[:, :], W[i][0:A, 0:J * E0]))
                ranks(gl[:, :])
                gl3 = gl[:, :].rearrange("p (j g) -> p j g", g=8)
                spread8 = lambda x: x[:, :].unsqueeze(2).to_broadcast((A, J, 8))
                link(dve.tensor_reduce(gmx[:, :], gl3, AX.X, ALU.max))
                dve.tensor_tensor(gl3, gl3, spread8(gmx), ALU.subtract).then_inc(gexp_in.h, gexp_in.up())
                dve.wait_ge(gexp_out.h, gexp_out.at(b, 1))
                link(dve.scalar_tensor_tensor(comb[:, :], rank[:, :], 2.0, gl[:, :], ALU.is_lt, ALU.mult))
                link(dve.tensor_reduce(gsum[:, :], comb[:, :].rearrange("p (j g) -> p j g", g=8), AX.X, ALU.add))
                link(dve.reciprocal(gsum[:, :], gsum[:, :]))
                c3 = comb[:, :].rearrange("p (j g) -> p j g", g=8)
                link(dve.scalar_tensor_tensor(c3, c3, 0.5, spread8(gsum), ALU.mult, ALU.mult))
                p = UNITS

                def mixed(e):
                    o, nth = O_AT[("Y", e)]
                    dve.wait_ge(o_full[o].h, o_full[o].at(b, nth))
                    src = h1 if e == 0 else h2
                    for j in range(J):
                        s = slice(j * C, (j + 1) * C)
                        scale = comb[:, j * 8 + e:j * 8 + e + 1] if e < E0 else 0.5
                        ins = dve.scalar_tensor_tensor(h2[:, s], Ob[o][0:A, s], scale, src[:, s], ALU.mult, ALU.add)
                    ins.then_inc(y_added.h, y_added.up())
                    dve.wait_ge(y_added.h, y_added.at(b, e + 1))

                for e in range(E0 + 1):
                    for c in range(2):
                        n = 2 * e + c
                        dst = hid[:, 2 * (e % 2) + c, :]
                        if e >= 2:
                            bank, nth = O_AT[("Y", e - 2)]
                            dve.wait_ge(o_full[bank].h, o_full[bank].at(b, nth))
                        dve.wait_ge(th_ready.h, th_ready.at(b, n + 1))
                        if e < E0:
                            i, nth = W_AT[("hid", n)]
                            dve.wait_ge(w_full[i].h, w_full[i].at(b, nth))
                            dve.scalar_tensor_tensor(dst, th[:, n % 2, :], 1.0, W[i][:, 0:TOK],
                                                                  ALU.add, ALU.mult).then_inc(hid_ready.h, hid_ready.up())
                        else:
                            i, nth = W_AT[("sg", c)]
                            dve.wait_ge(w_full[i].h, w_full[i].at(b, nth))
                            link(dve.scalar_tensor_tensor(sgate[:, :], th[:, n % 2, :], 1.0, W[i][:, 0:TOK],
                                                          ALU.add, ALU.mult))
                            i, nth = W_AT[("su", c)]
                            dve.wait_ge(w_full[i].h, w_full[i].at(b, nth))
                            dve.tensor_tensor(dst, W[i][:, 0:TOK], sgate[:, :], ALU.mult).then_inc(hid_ready.h, hid_ready.up())
                            dve.wait_ge(hid_ready.h, hid_ready.at(b, n + 1))
                        conv_out(nb, p)
                        p += 1
                    if e >= 1:
                        mixed(e - 1)
                conv_out(nb, p)
                p += 1
                mixed(E0)

                conv_out(nb, p)
                p += 1
                norm(b, 3, h2)
                i, nth = W_AT[("q1", 0)]
                dve.wait_ge(w_full[i].h, w_full[i].at(b, nth))
                dve.tensor_tensor(qT1[:, :, :], W[i][:, 0:TOK].rearrange("c (j a) -> c j a", j=J),
                                                bin_col[:, :].unsqueeze(2).to_broadcast((C, J, A)), ALU.add).then_inc(qkv1_ready.h, qkv1_ready.up())
                for name, dst in ("k1", k1), ("v1", v1):
                    i, nth = W_AT[(name, 0)]
                    dve.wait_ge(w_full[i].h, w_full[i].at(b, nth))
                    dve.tensor_tensor(dst, W[i][0:A, 0:3 * C], bin_row[:, :], ALU.add).then_inc(qkv1_ready.h, qkv1_ready.up())
                conv_out(nb, p)
                p += 1
                i, nth = W_AT[("kv", 0)]
                dve.wait_ge(w_full[i].h, w_full[i].at(b, nth))
                dve.tensor_tensor(kv[:, :], W[i][:, 0:C], kvmask[:, :], ALU.mult).then_inc(kv_ready.h, kv_ready.up())
                conv_out(nb, p)
                p += 1
                i, nth = W_AT[("g", 0)]
                dve.wait_ge(w_full[i].h, w_full[i].at(b, nth))
                dve.tensor_copy(G[:, :], W[i][:, 0:C]).then_inc(g_ready.h, g_ready.up())
                conv_out(nb, p)
                p += 1
                link(dve.tensor_tensor(h2[:, :].rearrange("p (j c) -> p j c", j=J),
                                       h2[:, :].rearrange("p (j c) -> p j c", j=J),
                                       bo1[:, :].unsqueeze(1).to_broadcast((A, J, C)), ALU.add))
                i, nth = W_AT[("out1", 0)]
                dve.wait_ge(w_full[i].h, w_full[i].at(b, nth))
                dve.wait_ge(h3_stored.h, h3_stored.at(b, 0))
                ins = dve.tensor_tensor(h3[:, :], W[i][0:A, 0:J * C], h2[:, :], ALU.add)
                ins.then_inc(h3_ready.h, h3_ready.up())
                dve.wait_ge(h3_ready.h, h3_ready.at(b, 1))
                conv_out(nb, p)
                p += 1

                dve.wait_ge(rows_sent.h, rows_sent.at(b, 0))
                norm(b, 4, h3)
                dve.wait_ge(gexp_out.h, gexp_out.at(b, 2))
                link(dve.tensor_scalar(sc[:, :, :], sc[:, :, :], 1.0, None, ALU.add))
                link(dve.reciprocal(sc[:, :, :], sc[:, :, :]))
                ss3 = ss[:, :, :].rearrange("p (j g) q -> p j (g q)", j=J)
                link(dve.tensor_tensor(ss3, sc[:, :, :], gate1_b[:, :].unsqueeze(1).to_broadcast((A, J, E1)), ALU.add))
                conv_out(nb, p)
                p += 1
                dve.tensor_tensor(tlo[:, :, :], ss[:, :, 0:4], ss[:, :, 4:8], ALU.min)
                link(dve.tensor_tensor(thi[:, :, :], ss[:, :, 0:4], ss[:, :, 4:8], ALU.max))
                for w in (2, 1):
                    dve.tensor_tensor(tmi[:, :, 0:w], thi[:, :, 0:w], thi[:, :, w:2 * w], ALU.min)
                    link(dve.tensor_tensor(tlo[:, :, 0:w], tlo[:, :, 0:w], tlo[:, :, w:2 * w], ALU.max))
                    link(dve.tensor_tensor(thi[:, :, 0:w], thi[:, :, 0:w], thi[:, :, w:2 * w], ALU.max))
                    link(dve.tensor_tensor(tlo[:, :, 0:w], tlo[:, :, 0:w], tmi[:, :, 0:w], ALU.max))
                link(dve.tensor_tensor(gl[:, :].unsqueeze(2), thi[:, :, 0:1], tlo[:, :, 0:1], ALU.add))
                ranks(gl[:, :])
                link(dve.tensor_scalar(gl[:, :], rank[:, :], 4.0, None, ALU.is_lt))
                dve.tensor_scalar(gpen[:, :], gl[:, :], 1.0, 1e30, ALU.subtract, ALU.mult)
                link(dve.tensor_tensor(ss[:, :, :], ss[:, :, :], gl[:, :].unsqueeze(2).to_broadcast((A, J * 8, 8)), ALU.mult))
                link(dve.tensor_tensor(ss[:, :, :], ss[:, :, :], gpen[:, :].unsqueeze(2).to_broadcast((A, J * 8, 8)), ALU.add))
                hold()
                for j in range(J):
                    ins = dve.max(top[:, j, :], ss3[:, j, :])
                link(ins)
                hold()
                for j in range(J):
                    ins = dve.match_replace(mr[:, j, :], top[:, j, :], ss3[:, j, :], -3e30)
                link(ins)
                dve.tensor_tensor(sel[:, :, :], mr[:, :, :], ss3, ALU.not_equal).then_inc(sel_ready.h, sel_ready.up())
                dve.wait_ge(sel_ready.h, sel_ready.at(b, 1))
                link(dve.tensor_tensor(sc[:, :, :], sc[:, :, :], sel[:, :, :], ALU.mult))
                link(dve.tensor_reduce(gsum[:, :], sc[:, :, :], AX.X, ALU.add))
                link(dve.reciprocal(gsum[:, :], gsum[:, :]))
                dve.scalar_tensor_tensor(rows[:, :, C:C + E1], sc[:, :, :], 2.5,
                                         gsum[:, :].unsqueeze(2).to_broadcast((A, J, E1)), ALU.mult, ALU.mult)
                link(dve.tensor_copy(rows[:, :, C + E1], tokens[:, :]))
                link(dve.tensor_scalar(tokens[:, :], tokens[:, :], float(TOK), None, ALU.add))
                conv_out(nb, p)
                p += 1
                assert p == POINTS
                kc = chain[2]
                if nb is not None:
                    tok_out(nb)
                chain[:] = [step_c, b, kc]
                i, nth = W_AT[("count", 0)]
                dve.wait_ge(w_full[i].h, w_full[i].at(b, nth))
                link(dve.tensor_tensor(pos[:, :, :], W[i][0:A, 0:J * E1].rearrange("p (j e) -> p j e", j=J),
                                       carry[:, :].unsqueeze(1).to_broadcast((A, J, E1)), ALU.add))
                link(dve.tensor_tensor(carry[:, :], W[i][0:A, J * E1:(J + 1) * E1], carry[:, :], ALU.add))
                link(dve.scalar_tensor_tensor(mr[:, :, :], pos[:, :, :], float(CAP), sel[:, :, :], ALU.is_lt, ALU.mult))
                link(dve.tensor_tensor(pos[:, :, :], slot_base[:, :, :], pos[:, :, :], ALU.subtract))
                link(dve.tensor_tensor(pos[:, :, :], pos[:, :, :], mr[:, :, :], ALU.mult))
                hold()
                for j in range(J):
                    ins = dve.max(top[:, j, :], pos[:, j, :])
                link(ins)
                dve.tensor_scalar(slot_i[:, :], top[:, :, :].rearrange("p j k -> p (j k)"), -1.0,
                                                float(SLOTS), ALU.mult, ALU.add).then_inc(rows_ready.h, rows_ready.up())

            n_set = [0]

            def done(ins):
                n_set[0] += 1
                ins.then_inc(s_set, 1)
                dve.wait_ge(s_set, n_set[0])

            done(dve.memset(carry[:, :], 0.0))
            dve.wait_ge(s_tokw, 16 * len(tok_loads))
            done(dve.tensor_tensor(tok_mask[:, :, :], tok_mask[:, :, :],
                                   tok_bl[:, :].unsqueeze(1).to_broadcast((TT, TILES, LK)), ALU.add))
            batch_starts()
            kn[0] = tok_softmax(0)

            def split_weights(n):
                half = slice((n % 2) * HALF, (n % 2 + 1) * HALF)
                dve.wait_ge(s_hi, n + 1)
                done(dve.tensor_tensor(stage[n % 2], stage[n % 2], wc_hi[:, n // 2, half], ALU.subtract))
                dve.tensor_scalar(wc_lo[:, n // 2, half], stage[n % 2], LO, None, ALU.mult).then_inc(s_lo, 1)
            for n in range(4):
                split_weights(n)
            kn[0] = tok_split(0, kn[0])
            for n in range(4, 2 * OC):
                split_weights(n)
            dve.wait_ge(s_curw, 16 * len(layer_loads))
            for sig in t_out:
                dve.wait_ge(sig.h, 16)
            done(dve.tensor_tensor(q_b[:, :], q_b[:, :], uv[:, :], ALU.add))
            done(dve.tensor_scalar(q_b[:, :], q_b[:, :], DH ** -0.5, None, ALU.mult))
            for g in range(H0 // 2):
                dve.wait_ge(s_pos, g + 1)
                dve.tensor_copy(KP[0:DH, 2 * g + 1, :], W[g % 2][0:DH, 0:TOK])
                dve.tensor_copy(KP[DH:, 2 * g, :], W[g % 2][DH:, 0:TOK]).then_inc(s_posu, 1)
            dve.tensor_copy(tri[:, :, :], tri_f).then_inc(s_setup, 1)
            for p in range(POINTS):
                conv_out(0, p)
            tok_out(0)
            with dve.Fori(0, B - 1) as it:
                batch_starts()
                present(it, it + 1)
                batch_ends()
            present(B - 1, None)

            with dve.Fori(0, E1 // 2) as pr:
                batch_starts()
                chain[:] = [t_s, pr, 0]
                for i in range(2):
                    dve.wait_ge(t_th[i].h, t_th[i].at(pr, 1))
                    link(dve.scalar_tensor_tensor(e_s, e_th[i], 1.0, W[2 + i][0:F1, 0:CAP], ALU.add, ALU.mult))
                    dve.tensor_tensor(e_h[i], Ob[i][0:F1, 0:CAP], e_s, ALU.mult).then_inc(t_h[i].h, t_h[i].up())
                    dve.wait_ge(t_h[i].h, t_h[i].at(pr, 1))
                for i in range(2):
                    dve.wait_ge(t_out[i].h, t_out[i].at(pr, 0))
                    dve.wait_ge(t_yps[i].h, t_yps[i].at(pr, 1))
                    dve.tensor_copy(e_idx[i], e_rows[i][:, :, C + E1])
                    for c in range(2):
                        w = e_rows[i][:, c, bass.ds(pr * 2 + (C + i), 1)]
                        ins = dve.tensor_scalar(e_y[i][:, c, :], Cb[i][:, c * C:(c + 1) * C], w, 0.5, ALU.mult, ALU.mult)
                    ins.then_inc(t_y[i].h, t_y[i].up())
                batch_ends()
    return totals


def pack(i):
    f = lambda a: np.ascontiguousarray(a)
    d = {}
    x = i["x"]
    pad = (TAPS - 1) // 2
    zrow = np.zeros((B, pad, C), np.float32)
    xpad = np.concatenate([zrow, x, np.zeros((B, TP - T, C), np.float32), zrow], axis=1)
    d["xpad"] = f(xpad)
    d["xTp"] = f(xpad[:, pad:pad + TP].transpose(0, 2, 1))
    by_tap = lambda w: w.reshape(HEADS_T, TAPS, -1).transpose(1, 0, 2).reshape(LK, -1)
    d["wlT"] = f(by_tap(i["L0_tok_Wl"]).T)
    d["tok_bl"] = f(by_tap(i["L0_tok_bl"])[:, 0])
    t = np.arange(TP)[:, None] + np.arange(TAPS)[None, :] - pad
    ok = (t >= 0) & (t < T)
    mask = np.where(ok, 0.0, -1e30).astype(np.float32).reshape(TILES, TT, TAPS)
    d["tok_mask"] = f(np.repeat(mask.transpose(1, 0, 2)[..., None], HEADS_T, axis=3).reshape(TT, TILES, LK))
    d["tok_bias"] = f(i["L0_tok_bias"][:, None])
    d["conv_b"] = f(i["L0_tok_bc"].reshape(OC, 128).T)
    d["w2T"] = f(i["L0_tok_W2"].T.reshape(OC, 128, C).transpose(1, 0, 2))
    d["b2"] = f(i["L0_tok_b2"])
    d["wc"] = f(i["L0_tok_Wc"].reshape(OC, 128, C, TAPS).transpose(0, 2, 3, 1).reshape(OC, C, TAPS * 128))
    d["gamma"], d["beta"] = f(i["L0_attn_gamma"][:, None]), f(i["L0_attn_beta"][:, None])
    wq, wk, wv = np.split(i["L0_attn_w_qkv"], 3, axis=0)
    bq, bk, bv = np.split(i["L0_attn_b_qkv"], 3)
    d["wqT"] = f(wq.T.reshape(C, H0, DH))
    d["wkT"], d["wvT"] = f(wk.T), f(wv.T)
    d["q_b"] = f(bq.reshape(H0, DH).T)
    d["k_b"] = f(bk.reshape(H0 // 2, 128).T)
    d["v_b"] = f(bv)
    u, v = i["L0_attn_u_bias"].T, i["L0_attn_v_bias"].T
    uv = np.empty((128, H0), np.float32)
    uv[:DH, 0::2], uv[DH:, 0::2], uv[:DH, 1::2], uv[DH:, 1::2] = u[:, 0::2], v[:, 0::2], v[:, 1::2], u[:, 1::2]
    d["uv"] = uv
    rel = np.arange(TOK, dtype=np.float32)[:, None] - np.arange(C, dtype=np.float32)[None, :]
    freq = np.exp(-np.arange(0, 2 * C, 2, dtype=np.float32) * np.float32(np.log(10000.0) / C)).astype(np.float32)
    angle = (rel * freq[None, :]).astype(np.float32)
    pe = np.where(np.arange(C)[None, :] % 2 == 0, np.cos(angle), np.sin(angle)).astype(np.float32)
    d["peT"] = f(pe.reshape(A, J, C).transpose(2, 1, 0).reshape(C, TOK))
    d["wposT"] = f(i["L0_attn_w_pos"].reshape(H0 // 2, 2, DH, C)[:, ::-1].reshape(H0 * DH, C).T)
    d["woT"] = f(i["L0_attn_w_out"].T.reshape(4, 128, C).transpose(1, 0, 2))
    d["bo"] = f(i["L0_attn_b_out"])
    d["gate0T"] = f(i["L0_ffn_gate_w"].T)
    d["w1T"] = f(i["L0_ffn_w1"].reshape(E0 * F0, C).T)
    d["w2eT"] = f(i["L0_ffn_w2"].transpose(0, 2, 1).reshape(E0 * 2, 128, C).transpose(1, 0, 2))
    d["sgT"], d["suT"] = f(i["L0_ffn_sg_gate"].T), f(i["L0_ffn_sg_up"].T)
    d["sdT"] = f(i["L0_ffn_sg_down"].T.reshape(2, 128, C).transpose(1, 0, 2))
    d["winT"] = f(i["L1_attn_w_in"].T)
    d["bin_col"] = f(i["L1_attn_b_in"].reshape(3, C).T)
    d["bin_row"] = f(i["L1_attn_b_in"])
    d["kvmask"] = np.kron(np.eye(8, dtype=np.float32), np.full((16, 16), 0.25, np.float32))
    d["wo1T"] = f(i["L1_attn_w_out"].T)
    d["bo1"] = f(i["L1_attn_b_out"])
    d["gate1T"] = f(i["L1_ffn_gate_w"].T)
    d["gate1_b"] = f(i["L1_ffn_gate_b"])
    d["w1e"], d["w3e"], d["w2e"] = f(i["L1_ffn_w1"]), f(i["L1_ffn_w3"]), f(i["L1_ffn_w2"])
    d["slot_base"] = np.broadcast_to(SLOTS - CAP * np.arange(E1, dtype=np.float32), (A, J, E1)).copy()
    n8 = np.arange(8)
    d["before"] = np.broadcast_to((n8[None, :] < n8[:, None]).astype(np.float32), (A, 8, 8)).copy()
    d["tokens"] = (np.arange(A)[:, None] * J + np.arange(J)[None, :]).astype(np.float32)
    a = np.arange(A)
    tri = np.stack([a[:, None] < a[None, :], a[:, None] <= a[None, :], np.ones((A, A), bool)], axis=1)
    d["tri"] = tri.astype(np.float32)
    d["ident"] = np.eye(128, dtype=np.float32)
    empty = np.zeros((CAP, ROW), np.float32)
    empty[:, C + E1] = NTOK + np.arange(CAP)
    d["empty_slots"] = empty
    return d


def kernel(**inputs):
    import concourse.bacc as bacc
    from concourse.bass_utils import run_bass_kernel_spmd

    arrays = {f"in_{k}": v for k, v in pack({k: np.asarray(v) for k, v in inputs.items()}).items()}

    def program(per):
        nc = bacc.Bacc("TRN2", target_bir_lowering=False, num_devices=1)
        dram = {k[3:]: nc.dram_tensor(k, v.shape, F32, kind="ExternalInput").ap() for k, v in arrays.items()}
        out = nc.dram_tensor("out", (NTOK + CAP, C), F32, kind="ExternalOutput").ap()
        return nc, build(nc, dram, out, per)

    _, per = program({})
    nc, again = program(per)
    assert again == per
    result = run_bass_kernel_spmd(nc, [arrays], core_ids=[0])
    return result.results[0]["out"][:NTOK].reshape(B, TOK, C)
```

```python
from contextlib import ExitStack

import numpy as np

import concourse.bass as bass
from concourse import mybir

F32 = mybir.dt.float32
F16 = mybir.dt.float16
BF16 = mybir.dt.bfloat16
U32 = mybir.dt.uint32
ALU = mybir.AluOpType
ACT = mybir.ActivationFunctionType
AX = mybir.AxisListType

B, T, C = 16, 375, 128
TAPS = 31
TOK = T - TAPS + 1
J = 3
A = TOK // J
HEADS_T = 4
LK = HEADS_T * TAPS
TILES = 4
TT = 94
TW = TT + TAPS - 1
TP = TILES * TT
BROW = TW * HEADS_T
HID = 512
OC = HID // 128
H0, DH = 8, 64
E0, F0 = 8, 256
E1, F1, CAP = 64, 64, 256
NTOK = B * TOK
ROW = C + E1 + 1
SLOTS = E1 * CAP
LO = 2048.0
ALPHA = 1.6732632423543772848170429916717
LAMBDA = 1.0507009873554804934193349852946
EPS = 1e-5
UNITS = H0 * J

PASSES = 3
CHUNK = TAPS * PASSES
NHID = 2 * (E0 + 1)
spread = lambda n, k: [n * (i + 1) // k - n * i // k for i in range(k)]
PLAN = [36, 6, 20] + spread(2 * CHUNK - 62, UNITS) + [6, 8, 36, 6] + spread(2 * CHUNK - 56, NHID - 2) + [0, 0, 0]
POINTS = len(PLAN)
assert sum(PLAN) == OC * CHUNK
CHUNK_END = {next(p for p in range(POINTS) if sum(PLAN[:p + 1]) >= (o + 1) * CHUNK): o for o in range(OC)}

LATE = ["ln3", "q1", "k1", "v1", "kv", "g", "out1", "ln4", "gate1", "count"]
LATE_UNIT = {2: "ln3", 3: "q1", 4: "k1", 5: "v1", 6: "kv", 7: "g", 8: "out1", 11: "ln4", 12: "gate1", 21: "count"}
TOK_USE = ["lg"] + [x for t in range(TILES) for x in (f"bT{t}", f"y{t}")]

def unit_steps():
    out = []
    for s in range(UNITS + 2):
        if s < UNITS:
            out.append(("S", s))
        if 1 <= s <= UNITS:
            out.append(("T", s - 1))
    return out


W_USES = ([("ln", 1)] + [x for h in range(H0) for x in ([("q", h)] + ([("k", h // 2)] if h % 2 == 0 else []))]
          + [("v", j) for j in range(J)] + unit_steps()
          + [("oT", j) for j in range(J)] + [("out0", 0)]
          + [("ln", 2), ("gate0", 0)] + [("hid", n) for n in range(2 * E0)]
          + [("sg", 0), ("su", 0), ("sg", 1), ("su", 1)])
O_USES = [("O", h) for h in range(H0)] + [("Y", e) for e in range(E0 + 1)]
C_USES = [x for o in range(OC) for x in (("main", o), ("cross", o))] + [("w2", 0)]
C_BANK = {"main": 0, "cross": 1, "w2": 0}


def place(uses, banks):
    seen = [0] * banks
    where = {}
    for n, u in enumerate(uses):
        b = C_BANK[u[0]] if uses is C_USES else n % banks
        seen[b] += 1
        where[u] = (b, seen[b])
    return where, seen


W_AT, W_PER = place(W_USES, 3)
O_AT, O_PER = place(O_USES, 2)
C_AT, C_PER = place(C_USES, 2)


FREED = {("out0", 0): ("ln_var_ready", 2), ("gate0", 0): ("gate_shifted", 1)}
FREED |= {("main", o): ("zneg_ready", o + 1) for o in range(OC)}
FREED |= {("cross", o): ("cross_terms_ready", o + 1) for o in range(OC)}
FREED |= {("ln", n): ("xT_ready", n) for n in (1, 2)}
FREED |= {("q", h): ("q_ready", h + 1) for h in range(H0)}
FREED |= {("k", g): ("kv_ready", g + 1) for g in range(H0 // 2)}
FREED |= {("v", j): ("kv_ready", H0 // 2 + j + 1) for j in range(J)}
FREED |= {("S", u): ("p_ready", u + 1) for u in range(UNITS)}
FREED |= {("T", u): (("pt_ready_scalar", "pt_ready_vector")[u % 2], u // 2 + 1) for u in range(UNITS)}
FREED |= {("oT", j): ("oT_ready", j + 1) for j in range(J)}
FREED |= {("hid", n): ("hid_ready", n + 1) for n in range(2 * E0)}
FREED |= {(w, c): ("hid_ready", 2 * E0 + c + 1) for w in ("sg", "su") for c in range(2)}
FREED |= {("O", h): ("o_ready", h + 1) for h in range(H0)}
FREED |= {("Y", e): ("y_added", e + 1) for e in range(E0 + 1)}


def before_in_bank(uses, where):
    return {u: next((v for v in reversed(uses[:uses.index(u)]) if where[v][0] == where[u][0]), None) for u in uses}


W_PREV, O_PREV, C_PREV = (before_in_bank(u, w) for u, w in ((W_USES, W_AT), (O_USES, O_AT), (C_USES, C_AT)))


def build(nc, dram, out, per):
    ctx = ExitStack()
    seen, totals, named = {}, {}, {}

    def sb(name, shape, dt=F32):
        return ctx.enter_context(nc.sbuf_tensor(name, shape, dt))

    class Signal:

        def __init__(self, name, by=1, primed=0):
            self.h, self.name, self.by, self.primed = ctx.enter_context(nc.semaphore(name)), name, by, primed
            named[name] = self

        def up(self):
            seen[self.name] = seen.get(self.name, 0) + 1
            return self.by

        def at(self, b, k):
            return b * (per.get(self.name, 1) * self.by) + (k + self.primed) * self.by

    def batch_starts():
        seen.clear()

    def batch_ends():
        for name, n in seen.items():
            totals[name] = totals.get(name, 0) + n

    with ctx:
        ident = sb("ident", [128, 128])
        wlT = sb("wlT", [C, LK])
        tok_bl = sb("tok_bl", [TT, LK])
        tok_mask = sb("tok_mask", [TT, TILES, LK])
        tok_bias = sb("tok_bias", [C, 1])
        conv_b = sb("conv_b", [128, OC])
        w2T = sb("w2T", [128, OC, C])
        b2 = sb("b2", [A, C])
        wc_hi = sb("wc_hi", [C, OC, TAPS * 128], F16)
        wc_lo = sb("wc_lo", [C, OC, TAPS * 128], F16)
        gamma = sb("gamma", [C, 1])
        beta = sb("beta", [C, 1])
        wqT = sb("wqT", [C, H0, 2 * DH])
        wkT = sb("wkT", [C, H0 * DH])
        wvT = sb("wvT", [C, H0 * DH])
        q_b = sb("q_b", [128, H0])
        uv = sb("uv", [128, H0])
        k_b = sb("k_b", [128, H0 // 2])
        v_b = sb("v_b", [A, H0 * DH])
        woT = sb("woT", [128, 4, C])
        bo = sb("bo", [A, C])
        gate0T = sb("gate0T", [C, E0])
        w1T = sb("w1T", [C, E0 * F0])
        w2eT = sb("w2eT", [128, E0 * 2, C])
        sgT = sb("sgT", [C, F0])
        suT = sb("suT", [C, F0])
        sdT = sb("sdT", [128, 2, C])
        winT = sb("winT", [C, 3 * C])
        bin_col = sb("bin_col", [C, 3])
        bin_row = sb("bin_row", [A, 3 * C])
        kvmask = sb("kvmask", [C, C])
        wo1T = sb("wo1T", [C, C])
        bo1 = sb("bo1", [A, C])
        gate1T = sb("gate1T", [C, E1])
        gate1_b = sb("gate1_b", [A, E1])
        slot_base = sb("slot_base", [A, J, E1])
        before = sb("before", [A, 8, 8])
        tokens = sb("tokens", [A, J])
        tri = sb("tri", [A, 3, A], BF16)
        minus_half = sb("minus_half", [A, J])
        gate_dve = sb("gate_dve", [A, 1])

        x_win = sb("x_win", [TW, TILES, C])
        x_T = sb("x_T", [C, TP])
        lg = sb("lg", [TT, TILES, LK])
        lmax = sb("lmax", [TT, TILES * HEADS_T])
        lsum = sb("lsum", [TT, TILES * HEADS_T])
        band = sb("band", [TT, 2, BROW])
        selu = sb("selu", [128, OC, TOK])
        zc = sb("zc", [128, TOK])
        bandT = sb("bandT", [TW, HEADS_T * TT])
        y32 = sb("y32", [C, TP])
        y_hi = sb("y_hi", [C, TP], F16)
        y_lo = sb("y_lo", [C, TP], F16)
        z = sb("z", [128, TOK])
        zneg = sb("zneg", [128, TOK])
        h0 = sb("h0", [A, J * C])

        bn = [sb(f"bn{g}", [A, J, 6]) for g in range(2)]
        mv = [sb(f"mv{g}", [A, J, 2]) for g in range(2)]
        ve = [sb(f"ve{g}", [A, J]) for g in range(2)]
        rstd = [sb(f"rstd{g}", [A, J]) for g in range(2)]
        xh = [sb(f"xh{g}", [A, J, C]) for g in range(2)]
        xTs = [sb(f"xT{g}", [C, TOK]) for g in range(2)]
        xT = xTs[0]
        qv = sb("qv", [128, H0 * TOK + J * H0 * DH])
        Q = qv[:, 0:H0 * TOK].rearrange("p (h t) -> p h t", h=H0)
        V = qv[0:A, H0 * TOK:].rearrange("p (j n) -> p j n", j=J)
        HALF = TAPS * 64
        stage = [qv[:, 0:HALF], qv[:, HALF:2 * HALF]]
        KP = sb("KP", [128, H0, TOK])
        nmax = sb("nmax", [A, 2])
        psums = sb("psums", [A, H0, J])
        prec = sb("prec", [A, H0, J])
        Pm = sb("Pm", [A, 2, TOK])
        PT = sb("PT", [A, 2, TOK])
        k1 = sb("k1", [A, 3 * C])
        v1 = sb("v1", [A, 3 * C])
        tri_f = Pm[:, 0, :].rearrange("p (m a) -> p m a", m=3)
        O = sb("O", [A, J, H0 * DH])
        hid = sb("hid", [128, 4, TOK])
        hidf = hid[:, :, :].rearrange("p j n -> p (j n)")
        OT = hidf.rearrange("p (j n) -> p j n", j=J)
        peT, wposT = hidf[:, 0:TOK], hidf[:, TOK:TOK + H0 * DH]
        h1 = sb("h1", [A, J * C])
        h2 = sb("h2", [A, J * C])
        h0b = h2
        h3 = sb("h3", [A, J * C])
        gl = sb("gl", [A, J * 8])
        gmx = sb("gmx", [A, J])
        cmp_a = sb("cmp_a", [A, J * 8, 8])
        cmp_b = sb("cmp_b", [A, J * 8, 8])
        rank = sb("rank", [A, J * 8])
        gsum = sb("gsum", [A, J])
        comb = sb("comb", [A, J * 8])
        th = sb("th", [128, 2, TOK])
        sgate = sb("sgate", [128, TOK])
        qT1 = sb("qT1", [C, J, A])
        kv = sb("kv", [C, C])
        G = sb("G", [C, C])
        rows = sb("rows", [A, J, ROW])
        sc = sb("sc", [A, J, E1])
        ss = sb("ss", [A, J * 8, 8])
        thi = sb("thi", [A, J * 8, 4])
        tlo = sb("tlo", [A, J * 8, 4])
        tmi = sb("tmi", [A, J * 8, 2])
        gpen = sb("gpen", [A, J * 8])
        top = sb("top", [A, J, 8])
        mr = sb("mr", [A, J, E1])
        sel = sb("sel", [A, J, E1], BF16)
        carry = sb("carry", [A, E1])
        pos = sb("pos", [A, J, E1])
        slot_i = sb("slot_i", [A, J * 8], U32)

        W = [ctx.enter_context(nc.psum_tensor(f"W{i}", [128, 512], F32)) for i in range(3)]
        L = ctx.enter_context(nc.psum_tensor("L", [128, 512], F32))
        Ob = [ctx.enter_context(nc.psum_tensor(f"Ob{i}", [128, 512], F32)) for i in range(2)]
        Cb = [ctx.enter_context(nc.psum_tensor(f"Cb{i}", [128, 512], F32)) for i in range(2)]

        s_tokw = ctx.enter_context(nc.semaphore("tok_weights_loaded"))
        s_curw = ctx.enter_context(nc.semaphore("layer_weights_loaded"))
        s_stage = [ctx.enter_context(nc.semaphore(f"conv_stage_loaded{i}")) for i in range(2)]
        s_zero = ctx.enter_context(nc.semaphore("band_zeroed"))
        s_held = ctx.enter_context(nc.semaphore("pool_held"))
        s_bandz = ctx.enter_context(nc.semaphore("band_dram_zeroed"))
        s_hi = ctx.enter_context(nc.semaphore("conv_hi_ready"))
        s_lo = ctx.enter_context(nc.semaphore("conv_lo_ready"))
        s_set = ctx.enter_context(nc.semaphore("setup_dve_step"))
        s_pos = ctx.enter_context(nc.semaphore("setup_pos_ready"))
        s_posu = ctx.enter_context(nc.semaphore("setup_pos_used"))
        s_setup = ctx.enter_context(nc.semaphore("setup_done"))

        w_full = [Signal(f"w_full{i}") for i in range(3)]
        late_full = Signal("late_full")
        tok_full = Signal("tok_full")
        o_full = [Signal(f"o_full{i}") for i in range(2)]
        c_full = [Signal(f"c_full{i}") for i in range(2)]
        x_loaded = Signal("x_loaded", 16)
        lg_sub = Signal("lg_shifted")
        lg_exp = Signal("lg_exp")
        taps_ready = Signal("tap_weights_ready")
        band_out = Signal("band_written", 16)
        band_in = [Signal(f"band_loaded{i}", 16) for i in range(2)]
        bandT_ready = Signal("bandT_ready")
        y_ready = Signal("y_ready")
        y_split = Signal("y_split")
        zc_ready = Signal("cross_terms_ready")
        zneg_ready = Signal("zneg_ready")
        zexp_ready = Signal("zexp_ready")
        h0_ready = Signal("h0_ready")
        selu_ready = Signal("selu_ready")
        step_main = Signal("dve_step_main")
        step_late = Signal("dve_step_late")
        step_conv = Signal("dve_step_conv")
        step_tok = Signal("dve_step_tok")
        ln_var = [Signal("ln_var_ready"), Signal("late_var_ready")]
        ln_rstd = [Signal("ln_rstd_ready"), Signal("late_rstd_ready")]
        xh_ready = [Signal("xh_ready"), Signal("late_xh_ready")]
        xT_ready = [Signal("xT_ready"), Signal("late_xT_ready")]
        q_ready = Signal("q_ready")
        kvp_ready = Signal("kv_ready")
        nmax_ready = Signal("nmax_ready")
        p_ready = Signal("p_ready")
        pt_ready_a = Signal("pt_ready_scalar")
        pt_ready_d = Signal("pt_ready_vector")
        pv_done = Signal("pv_done")
        o_ready = Signal("o_ready")
        oT_ready = Signal("oT_ready")
        gexp_in = Signal("gate_shifted")
        gexp_out = Signal("gate_exp")
        th_ready = Signal("tanh_ready")
        hid_ready = Signal("hid_ready")
        qkv1_ready = Signal("qkv1_ready")
        kv_ready = Signal("kv_state_ready")
        g_ready = Signal("g_ready")
        y_added = Signal("y_added")
        gate1_exp = Signal("gate1_exp")
        counted = Signal("counts_added")
        h3_ready = Signal("h3_ready")
        h3_stored = Signal("h3_stored", 16, primed=1)
        sel_ready = Signal("sel_ready")
        rows_ready = Signal("rows_ready")
        rows_sent = Signal("rows_sent", 16, primed=1)

        def freed(use):
            at, prev = next((a, p) for a, p in ((W_AT, W_PREV), (O_AT, O_PREV), (C_AT, C_PREV)) if use in a)
            if not prev[use]:
                return at[use][0], None, 0
            name, k = FREED[prev[use]]
            return at[use][0], named[name], k

        def pt_used(eng, b, u):
            h, j = u // J, u % J
            if j == J - 1:
                bank, nth = O_AT[("O", h)]
                eng.wait_ge(o_full[bank].h, o_full[bank].at(b, nth))
            else:
                eng.wait_ge(pv_done.h, pv_done.at(b, 2 * h + j + 1))

        xpad, xTp = dram["xpad"], dram["xTp"]
        band_d = nc.dram_tensor("band_dram", (TILES, TT, BROW), F32, kind="Internal").ap()
        slots_d = nc.dram_tensor("slots_dram", (SLOTS, ROW), F32, kind="Internal").ap()
        band_skew = bass.AP(tensor=band_d.tensor, offset=0,
                            ap=[[BROW + HEADS_T, TT], [TT * BROW, TILES], [1, LK]])
        band_rows = band_d.rearrange("i t n -> t i n")

        tok_loads = [(ident, dram["ident"]), (wlT, dram["wlT"]), (tok_bl, dram["tok_bl"].partition_broadcast(TT)),
                     (tok_mask, dram["tok_mask"]), (tok_bias, dram["tok_bias"]), (conv_b, dram["conv_b"]),
                     (w2T, dram["w2T"]), (b2, dram["b2"].partition_broadcast(A))]
        layer_loads = [(beta, dram["beta"]),
                       (wqT[:, :, 0:DH], dram["wqT"]), (wqT[:, :, DH:], dram["wqT"]), (wkT, dram["wkT"]),
                       (wvT, dram["wvT"]), (q_b[0:DH, :], dram["q_b"]), (q_b[DH:, :], dram["q_b"]),
                       (k_b, dram["k_b"]), (v_b, dram["v_b"].partition_broadcast(A)), (peT, dram["peT"]),
                       (wposT, dram["wposT"]), (woT, dram["woT"]), (bo, dram["bo"].partition_broadcast(A)),
                       (gate0T, dram["gate0T"]), (w1T, dram["w1T"]), (w2eT, dram["w2eT"]), (sgT, dram["sgT"]),
                       (suT, dram["suT"]), (sdT, dram["sdT"]), (winT, dram["winT"]), (bin_col, dram["bin_col"]),
                       (bin_row, dram["bin_row"].partition_broadcast(A)), (kvmask, dram["kvmask"]),
                       (wo1T, dram["wo1T"]), (bo1, dram["bo1"].partition_broadcast(A)), (gate1T, dram["gate1T"]),
                       (gate1_b, dram["gate1_b"].partition_broadcast(A)), (tri_f, dram["tri"])]
        layer_loads.append((uv, dram["uv"]))

        def ap(x):
            return x if isinstance(x, bass.AP) else x.ap()

        tail_f = wc_hi[:, :, :].rearrange("p a b -> p (a b)").bitcast(F32)
        used = [0]

        def carve(n):
            used[0] += n
            assert used[0] <= OC * TAPS * 64
            return tail_f[:, used[0] - n:used[0]]

        e_rows = [carve(2 * ROW).rearrange("p (c n) -> p c n", c=2) for _ in range(4)]
        e_w13 = [carve(2 * F1) for _ in range(4)]
        e_w2 = [carve(C)[0:F1, :] for _ in range(4)]
        e_y = [carve(2 * C).rearrange("p (c n) -> p c n", c=2) for _ in range(4)]
        e_idx = [carve(2).bitcast(U32) for _ in range(4)]
        e_xT = [carve(CAP) for _ in range(2)]
        e_th = [carve(CAP)[0:F1, :] for _ in range(2)]
        e_s = carve(CAP)[0:F1, :]
        e_h = [carve(CAP)[0:F1, :] for _ in range(2)]

        t_load = [Signal(f"t_loaded{i}", 16) for i in range(4)]
        t_xps = [Signal(f"t_x_turned{i}") for i in range(4)]
        t_xT = [Signal(f"t_xT_ready{i}") for i in range(4)]
        t_hps = [Signal(f"t_h_full{i}") for i in range(4)]
        t_th = [Signal(f"t_tanh{i}") for i in range(4)]
        t_s = Signal("t_step")
        t_h = [Signal(f"t_h_ready{i}") for i in range(4)]
        t_yps = [Signal(f"t_y_full{i}") for i in range(4)]
        t_y = [Signal(f"t_y_ready{i}") for i in range(4)]
        t_out = [Signal(f"t_added{i}", 16, primed=1) for i in range(4)]
        t_sum = ctx.enter_context(nc.semaphore("sums_joined"))
        odd_d = nc.dram_tensor("odd_sum_dram", (NTOK + CAP, C), F32, kind="Internal").ap()
        sums = [out, odd_d]

        block = ctx.enter_context(nc.Block())

        @block.sync
        def _(sp):
            for dst, src in tok_loads:
                sp.dma_start(ap(dst) if not isinstance(dst, bass.AP) else dst, src).then_inc(s_tokw, 16)

            def load_x(tb):
                if not (isinstance(tb, int) and tb == 0):
                    sp.wait_ge(tok_full.h, tok_full.at(tb - 1, len(TOK_USE)))
                src = bass.AP(tensor=xpad.tensor, offset=tb * ((TP + 30) * C),
                              ap=[[C, TW], [TT * C, TILES], [1, C]])
                sp.dma_start(x_win[:, :, :], src).then_inc(x_loaded.h, x_loaded.up())
                sp.dma_start(x_T[:, :], xTp[tb]).then_inc(x_loaded.h, x_loaded.up())

            def bands(tb, tiles=range(TILES)):
                if 0 in tiles:
                    sp.wait_ge(taps_ready.h, taps_ready.at(tb, 1))
                    sp.dma_start(band_skew, lg[:, :, :]).then_inc(band_out.h, band_out.up())
                    sp.wait_ge(band_out.h, band_out.at(tb, 1))
                for t in tiles:
                    if t >= 2:
                        sp.wait_ge(tok_full.h, tok_full.at(tb, 1 + TOK_USE.index(f"bT{t - 2}")))
                    sp.dma_start(band[:, t % 2, :], band_rows[:, t, :])\
                        .then_inc(band_in[t % 2].h, band_in[t % 2].up())

            batch_starts()
            load_x(0)
            for n in range(2 * OC):
                if n >= 2:
                    sp.wait_ge(s_lo, n - 1)
                sp.dma_start(stage[n % 2], dram["wc"][n // 2, :, (n % 2) * HALF:(n % 2 + 1) * HALF])\
                    .then_inc(s_stage[n % 2], 16)
                if n == 0:
                    sp.wait_ge(s_zero, 1)
                    for t in range(0, TILES, 2):
                        sp.dma_start(band_rows[:, t:t + 2, :], band[:, :, :]).then_inc(s_bandz, 16)
                    sp.wait_ge(s_bandz, 32)
                if n == 1:
                    bands(0, range(2))
                if n == 3:
                    bands(0, range(2, TILES))
            for tb in 1, 2:
                load_x(tb)
                bands(tb)
            with sp.Fori(1, B - 1) as it:
                batch_starts()
                load_x(it + 2)
                bands(it + 2)
                batch_ends()

            def load_expert(pr, i):
                e = pr * 4 + i
                if not (isinstance(pr, int) and pr == 0):
                    sp.wait_ge(t_y[i].h, t_y[i].at(pr - 1, 1))
                sp.dma_start(e_rows[i], slots_e[e]).then_inc(t_load[i].h, t_load[i].up())
                sp.dma_start(e_w13[i][:, 0:F1], dram["w1e"][e]).then_inc(t_load[i].h, t_load[i].up())
                sp.dma_start(e_w13[i][:, F1:], dram["w3e"][e]).then_inc(t_load[i].h, t_load[i].up())
                sp.dma_start(e_w2[i], dram["w2e"][e]).then_inc(t_load[i].h, t_load[i].up())

            slots_e = slots_d.rearrange("(e c p) n -> e p c n", c=2, p=128)
            sp.wait_ge(rows_sent.h, rows_sent.at(B - 1, J * 8))
            batch_starts()
            for i in range(4):
                load_expert(0, i)
            with sp.Fori(1, E1 // 4) as pr:
                batch_starts()
                for i in range(4):
                    load_expert(pr, i)
                batch_ends()

        @block.gpsimd
        def _(pool):
            pool.memset(minus_half[:, :], -0.5)
            pool.memset(band[:, :, :], 0.0).then_inc(s_zero, 1)
            pool.dma_start(slots_d.rearrange("(e s) n -> e (s n)", e=E1),
                           dram["empty_slots"].rearrange("s n -> (s n)").unsqueeze(0).to_broadcast((E1, CAP * ROW)))\
                .then_inc(rows_sent.h, 16)
            pool.dma_start(out[NTOK:, :], dram["empty_slots"][:, 0:C]).then_inc(h3_stored.h, 16)
            nz = NTOK // CAP * CAP
            zeros = dram["empty_slots"][:, 0:C]
            pool.dma_start(odd_d[0:nz, :].rearrange("(r s) c -> r s c", s=CAP),
                           zeros.unsqueeze(0).to_broadcast((nz // CAP, CAP, C))).then_inc(t_sum, 16)
            pool.dma_start(odd_d[nz:, :], dram["empty_slots"].rearrange("s n -> (s n)")[0:C]
                           .unsqueeze(0).to_broadcast((NTOK + CAP - nz, C))).then_inc(t_sum, 16)
            for sig, (dst, src) in zip(t_out, ((slot_base, dram["slot_base"]), (before, dram["before"]),
                                               (tokens, dram["tokens"]), (gamma, dram["gamma"]))):
                pool.dma_start(ap(dst), src).then_inc(sig.h, 16)
            pool.wait_ge(rows_sent.h, 16)
            pool.wait_ge(h3_stored.h, 16)

            def hold():
                pool.sem_inc(s_held, 1)

            def power(b, n, g):
                pool.wait_ge(ln_var[g].h, ln_var[g].at(b, n))
                pool.tensor_tensor(rstd[g][:, :], ve[g][:, :], minus_half[:, :], ALU.pow)\
                    .then_inc(ln_rstd[g].h, ln_rstd[g].up())

            def send(b):
                pool.wait_ge(h3_ready.h, h3_ready.at(b, 1))
                src = h3[:, :]
                dst = bass.AP(tensor=out.tensor, offset=b * (TOK * C), ap=[[J * C, A], [1, J * C]])
                pool.dma_start(dst, src).then_inc(h3_stored.h, h3_stored.up())
                pool.wait_ge(rows_ready.h, rows_ready.at(b, 1))
                hold()
                for j in range(J):
                    for k in range(8):
                        pool.indirect_dma_start(
                            out=slots_d, out_offset=bass.IndirectOffsetOnAxis(ap=slot_i[:, j * 8 + k:j * 8 + k + 1], axis=0),
                            in_=rows[:, j, :], in_offset=None, bounds_check=SLOTS - 1, oob_is_err=False).then_inc(rows_sent.h, rows_sent.up())

            def present(b, lb):
                power(b, 1, 0)
                if lb is not None:
                    power(lb, 1, 1)
                    power(lb, 2, 1)
                power(b, 2, 0)
                if lb is not None:
                    send(lb)

            present(0, None)
            with pool.Fori(1, B - 1) as it:
                batch_starts()
                present(it, it - 1)
                batch_ends()
            present(B - 1, B - 2)
            power(B - 1, 1, 1)
            power(B - 1, 2, 1)
            send(B - 1)
            pool.wait_ge(h3_stored.h, h3_stored.at(B - 1, 1))
            pool.wait_ge(rows_sent.h, rows_sent.at(B - 1, J * 8))
            pool.wait_ge(t_sum, 32)

            def add_rows(pr, i):
                pool.wait_ge(t_y[i].h, t_y[i].at(pr, 1))
                if i >= 2:
                    pool.wait_ge(t_out[i - 2].h, t_out[i - 2].at(pr, 2))
                else:
                    pool.wait_ge(t_out[i + 2].h, t_out[i + 2].at(pr, 0))
                hold()
                for c in range(2):
                    pool.indirect_dma_start(
                        out=sums[i % 2], out_offset=bass.IndirectOffsetOnAxis(ap=e_idx[i][:, c:c + 1], axis=0),
                        in_=e_y[i][:, c, :], in_offset=None, bounds_check=NTOK + CAP - 1, oob_is_err=True,
                        compute_op=ALU.add).then_inc(t_out[i].h, t_out[i].up())

            with pool.Fori(0, E1 // 4) as pr:
                batch_starts()
                for i in range(4):
                    add_rows(pr, i)
                batch_ends()
            for i in range(4):
                pool.wait_ge(t_out[i].h, t_out[i].at(E1 // 4 - 1, 2))
            wide = 2048
            flat = lambda x: x[0:NTOK, :].rearrange("t c -> (t c)").rearrange("(r n) -> r n", n=wide)
            pool.dma_start(flat(out), flat(odd_d), accum_op=ALU.add, max_dma_last_dim=4 * wide).then_inc(t_sum, 16)
            pool.wait_ge(t_sum, 48)

        @block.tensor
        def _(pe):
            def mm(o, l, r, start=True, stop=True):
                return pe.matmul(o, l, r, start=start, stop=stop)

            def tok_logits(tb):
                if not (isinstance(tb, int) and tb == 0):
                    pe.wait_ge(y_ready.h, y_ready.at(tb - 1, TILES))
                pe.wait_ge(x_loaded.h, x_loaded.at(tb, 2))
                for t in range(TILES):
                    last = mm(L[0:TT, t * LK:(t + 1) * LK], x_T[:, t * TT:(t + 1) * TT], wlT[:, :])
                last.then_inc(tok_full.h, tok_full.up())

            def tok_mix(tb, n, lb):
                t = n // 2
                if n % 2 == 0:
                    pe.wait_ge(band_in[t % 2].h, band_in[t % 2].at(tb, t // 2 + 1))
                    if t >= 1:
                        pe.wait_ge(y_ready.h, y_ready.at(tb, t))
                    elif lb is not None:
                        pe.wait_ge(counted.h, counted.at(lb, 1))
                    else:
                        pe.wait_ge(lg_sub.h, lg_sub.at(tb, 1))
                    for h in range(HEADS_T):
                        last = pe.transpose(L[0:TW, h * TT:(h + 1) * TT], band[:, t % 2, h::HEADS_T], ident[0:TT, 0:TT])
                else:
                    pe.wait_ge(bandT_ready.h, bandT_ready.at(tb, t + 1))
                    for h in range(HEADS_T):
                        last = mm(L[32 * h:32 * h + 32, 0:TT], x_win[:, t, 32 * h:32 * h + 32],
                                  bandT[:, h * TT:(h + 1) * TT])
                last.then_inc(tok_full.h, tok_full.up())

            def conv(nb, p):
                if nb is None:
                    return
                for g in range(sum(PLAN[:p]), sum(PLAN[:p + 1])):
                    o, m = g // CHUNK, g % CHUNK
                    if m == 0:
                        if o == 0:
                            pe.wait_ge(y_split.h, y_split.at(nb, 1))
                            if not (isinstance(nb, int) and nb == 0):
                                pe.wait_ge(h0_ready.h, h0_ready.at(nb - 1, 1))
                        else:
                            pe.wait_ge(zneg_ready.h, zneg_ready.at(nb, o))
                        if isinstance(nb, int) and nb == 0:
                            pe.wait_ge(s_lo, 2 * o + 2)
                    k, what = m // PASSES, m % PASSES
                    whi = wc_hi[:, o, k * 128:(k + 1) * 128]
                    wlo = wc_lo[:, o, k * 128:(k + 1) * 128]
                    yh, yl = y_hi[:, k:k + TOK], y_lo[:, k:k + TOK]
                    if what == 0:
                        last = mm(Cb[0][:, 0:TOK], whi, yh, start=(k == 0), stop=(k == TAPS - 1))
                        if k == TAPS - 1:
                            last.then_inc(c_full[0].h, c_full[0].up())
                    elif what == 1:
                        mm(Cb[1][:, 0:TOK], whi, yl, start=(k == 0), stop=False)
                    else:
                        last = mm(Cb[1][:, 0:TOK], wlo, yh, start=False, stop=(k == TAPS - 1))
                        if k == TAPS - 1:
                            last.then_inc(c_full[1].h, c_full[1].up())

            def tok_out(nb):
                i, was, nth = freed(("w2", 0))
                if was:
                    pe.wait_ge(was.h, was.at(nb, nth))
                pe.wait_ge(selu_ready.h, selu_ready.at(nb, OC))
                for j in range(J):
                    for o in range(OC):
                        last = mm(Cb[i][0:A, j * C:(j + 1) * C], selu[:, o, j::J], w2T[:, o, :],
                                  start=(o == 0), stop=(o == OC - 1))
                last.then_inc(c_full[i].h, c_full[i].up())

            def turn(b, n):
                pe.wait_ge(xh_ready[0].h, xh_ready[0].at(b, n))
                i, was, nth = freed(("ln", n))
                if was:
                    pe.wait_ge(was.h, was.at(b, nth))
                for j in range(J):
                    last = pe.transpose(W[i][:, j * A:(j + 1) * A], xh[0][:, j, :], ident[0:A, 0:A])
                last.then_inc(w_full[i].h, w_full[i].up())

            def gate(w, width, wt, x):
                for j in range(J):
                    last = mm(w[0:A, j * width:(j + 1) * width], x[:, j * A:(j + 1) * A], wt[:, :])
                return last

            def late(b, unit, tb):
                if b is None or unit not in LATE_UNIT:
                    return
                use, x = LATE_UNIT[unit], xTs[1]
                if use == "ln3":
                    if tb is not None:
                        pe.wait_ge(lg_sub.h, lg_sub.at(tb, 1))
                    elif isinstance(b, int) and b == B - 1:
                        pe.wait_ge(counted.h, counted.at(b - 1, 1))
                    else:
                        pe.wait_ge(y_ready.h, y_ready.at(B, TILES))
                    pe.wait_ge(xh_ready[1].h, xh_ready[1].at(b, 1))
                    for j in range(J):
                        last = pe.transpose(L[:, j * A:(j + 1) * A], xh[1][:, j, :], ident[0:A, 0:A])
                elif use == "q1":
                    pe.wait_ge(xT_ready[1].h, xT_ready[1].at(b, 1))
                    for j in range(J):
                        last = mm(L[:, j * A:(j + 1) * A], winT[:, j * C:(j + 1) * C], x[:, 0:A])
                elif use == "k1":
                    pe.wait_ge(qkv1_ready.h, qkv1_ready.at(b, 1))
                    last = mm(L[0:A, 0:3 * C], x[:, A:2 * A], winT[:, :])
                elif use == "v1":
                    pe.wait_ge(qkv1_ready.h, qkv1_ready.at(b, 2))
                    last = mm(L[0:A, 0:3 * C], x[:, 2 * A:3 * A], winT[:, :])
                elif use == "kv":
                    pe.wait_ge(qkv1_ready.h, qkv1_ready.at(b, 3))
                    for j in range(J):
                        last = mm(L[:, 0:C], v1[:, j * C:(j + 1) * C], k1[:, j * C:(j + 1) * C],
                                  start=(j == 0), stop=(j == J - 1))
                elif use == "g":
                    pe.wait_ge(kv_ready.h, kv_ready.at(b, 1))
                    last = mm(L[:, 0:C], kv[:, :], wo1T[:, :])
                elif use == "out1":
                    pe.wait_ge(g_ready.h, g_ready.at(b, 1))
                    for j in range(J):
                        last = mm(L[0:A, j * C:(j + 1) * C], qT1[:, j, :], G[:, :])
                elif use == "ln4":
                    pe.wait_ge(xh_ready[1].h, xh_ready[1].at(b, 2))
                    for j in range(J):
                        last = pe.transpose(L[:, j * A:(j + 1) * A], rows[:, j, 0:C], ident[0:A, 0:A])
                elif use == "gate1":
                    pe.wait_ge(xT_ready[1].h, xT_ready[1].at(b, 2))
                    last = gate(L, E1, gate1T, x)
                else:
                    pe.wait_ge(sel_ready.h, sel_ready.at(b, 1))
                    for j in range(J + 1):
                        for q in range(J):
                            m = 2 if j == J else 1 if q < j else 0
                            last = mm(L[0:A, j * E1:(j + 1) * E1], tri[:, m, :], sel[:, q, :],
                                      start=(q == 0), stop=(q == J - 1))
                last.then_inc(late_full.h, late_full.up())

            def step(b, use, what, extra=None):
                i, was, nth = freed(use)
                if was:
                    pe.wait_ge(was.h, was.at(b, nth))
                what(W[i]).then_inc(w_full[i].h, w_full[i].up())

            def present(b, nb, tb, lb):
                if tb is not None:
                    tok_logits(tb)
                conv(nb, 0)
                turn(b, 1)
                conv(nb, 1)
                pe.wait_ge(xT_ready[0].h, xT_ready[0].at(b, 1))
                for h in range(H0):
                    step(b, ("q", h), lambda w: mm(w[:, 0:TOK], wqT[:, h, :], xT[:, :]))
                    if h % 2 == 0:
                        g = h // 2
                        step(b, ("k", g), lambda w: mm(w[:, 0:TOK], wkT[:, g * 128:(g + 1) * 128], xT[:, :]))
                for j in range(J):
                    step(b, ("v", j), lambda w: mm(w[0:A, :], xT[:, j * A:(j + 1) * A], wvT[:, :]))
                conv(nb, 2)
                pe.wait_ge(q_ready.h, q_ready.at(b, H0))
                pe.wait_ge(kvp_ready.h, kvp_ready.at(b, H0 // 2 + J))

                def turn_p(w, u):
                    for i in range(J):
                        last = pe.transpose(w[0:A, i * A:(i + 1) * A], Pm[:, u % 2, i * A:(i + 1) * A], ident[0:A, 0:A])
                    return last

                for s in range(UNITS + 2):
                    if s < UNITS:
                        h, j = s // J, s % J
                        step(b, ("S", s), lambda w: mm(w[0:A, 0:TOK], Q[:, h, j * A:(j + 1) * A], KP[:, h, :]))
                        late(lb, s, tb)
                        conv(nb, 3 + s)
                    if 1 <= s <= UNITS:
                        u = s - 1
                        pe.wait_ge(p_ready.h, p_ready.at(b, u + 1))
                        step(b, ("T", u), lambda w: turn_p(w, u))
                    if s >= 2:
                        u = s - 2
                        h, j = u // J, u % J
                        if j == 0:
                            o, was, nth = freed(("O", h))
                            if was:
                                pe.wait_ge(was.h, was.at(b, nth))
                        pe.wait_ge((pt_ready_a, pt_ready_d)[u % 2].h, (pt_ready_a, pt_ready_d)[u % 2].at(b, u // 2 + 1))
                        for i in range(J):
                            last = mm(Ob[o][0:A, j * DH:(j + 1) * DH], PT[:, u % 2, i * A:(i + 1) * A],
                                      V[:, i, h * DH:(h + 1) * DH], start=(i == 0), stop=(i == J - 1))
                        pv = o_full[o] if j == J - 1 else pv_done
                        last.then_inc(pv.h, pv.up())

                p = 3 + UNITS
                conv(nb, p)
                pe.wait_ge(o_ready.h, o_ready.at(b, H0))
                for j in range(J):
                    i, was, nth = freed(("oT", j))
                    if was:
                        pe.wait_ge(was.h, was.at(b, nth))
                    for c in range(4):
                        last = pe.transpose(W[i][:, c * A:(c + 1) * A], O[:, j, c * 128:(c + 1) * 128], ident[0:A, 0:A])
                    last.then_inc(w_full[i].h, w_full[i].up())
                conv(nb, p + 1)
                i, was, nth = freed(("out0", 0))
                if was:
                    pe.wait_ge(was.h, was.at(b, nth))
                for j in range(J):
                    pe.wait_ge(oT_ready.h, oT_ready.at(b, j + 1))
                    for c in range(4):
                        last = mm(W[i][0:A, j * C:(j + 1) * C], OT[:, j, c * A:(c + 1) * A], woT[:, c, :],
                                  start=(c == 0), stop=(c == 3))
                last.then_inc(w_full[i].h, w_full[i].up())

                conv(nb, p + 2)
                turn(b, 2)
                conv(nb, p + 3)
                p += 4
                pe.wait_ge(xT_ready[0].h, xT_ready[0].at(b, 2))
                step(b, ("gate0", 0), lambda w: gate(w, E0, gate0T, xT))

                def mix(e):
                    pe.wait_ge(hid_ready.h, hid_ready.at(b, 2 * e + 2))
                    o, was, nth = freed(("Y", e))
                    if was:
                        pe.wait_ge(was.h, was.at(b, nth))
                    for j in range(J):
                        for c in range(2):
                            wt = w2eT[:, 2 * e + c, :] if e < E0 else sdT[:, c, :]
                            last = mm(Ob[o][0:A, j * C:(j + 1) * C], hid[:, 2 * (e % 2) + c, j * A:(j + 1) * A], wt,
                                      start=(c == 0), stop=(c == 1))
                    last.then_inc(o_full[o].h, o_full[o].up())

                for e in range(E0 + 1):
                    for c in range(2):
                        if e < E0:
                            n = 2 * e + c
                            step(b, ("hid", n), lambda w: mm(w[:, 0:TOK], w1T[:, n * 128:(n + 1) * 128], xT[:, :]))
                        else:
                            step(b, ("sg", c), lambda w: mm(w[:, 0:TOK], sgT[:, c * 128:(c + 1) * 128], xT[:, :]))
                            step(b, ("su", c), lambda w: mm(w[:, 0:TOK], suT[:, c * 128:(c + 1) * 128], xT[:, :]))
                        n = 2 * e + c
                        if tb is not None and n % 2 == 0 and n < 4 * TILES:
                            tok_mix(tb, n // 2, lb)
                        conv(nb, p)
                        p += 1
                    if e >= 1:
                        mix(e - 1)
                conv(nb, p)
                p += 1
                mix(E0)
                assert p == POINTS
                if nb is not None:
                    tok_out(nb)

            pe.wait_ge(s_tokw, 16 * len(tok_loads))
            batch_starts()
            tok_logits(0)
            for n in range(2 * TILES):
                tok_mix(0, n, None)
            pe.wait_ge(s_curw, 16 * len(layer_loads))
            for g in range(H0 // 2):
                if g >= 2:
                    pe.wait_ge(s_posu, g - 1)
                mm(W[g % 2][:, 0:TOK], wposT[:, g * 128:(g + 1) * 128], peT).then_inc(s_pos, 1)
            tok_logits(1)
            for p in range(POINTS):
                conv(0, p)
                if p >= 3 + UNITS and p < 3 + UNITS + 2 * TILES:
                    tok_mix(1, p - 3 - UNITS, None)
            tok_out(0)
            pe.wait_ge(s_setup, 1)
            present(0, 1, 2, None)
            with pe.Fori(1, B - 1) as it:
                batch_starts()
                present(it, it + 1, it + 2, it - 1)
                batch_ends()
            present(B - 1, None, None, B - 2)
            for s in range(UNITS):
                late(B - 1, s, None)

            turn_bank, h_bank, up_bank, y_bank = W[0:2], Ob, Cb, [W[2], L]

            def expert_in(pr, i):
                pe.wait_ge(t_load[i].h, t_load[i].at(pr, 4))
                for c in range(2):
                    last = pe.transpose(turn_bank[i % 2][:, c * 128:(c + 1) * 128], e_rows[i][:, c, 0:C], ident[:, :])
                last.then_inc(t_xps[i].h, t_xps[i].up())

            def expert_up(pr, i):
                pe.wait_ge(t_xT[i].h, t_xT[i].at(pr, 1))
                mm(h_bank[i % 2][0:F1, 0:CAP], e_w13[i][:, 0:F1], e_xT[i % 2])
                mm(up_bank[i % 2][0:F1, 0:CAP], e_w13[i][:, F1:], e_xT[i % 2]).then_inc(t_hps[i].h, t_hps[i].up())

            def expert_down(pr, i):
                pe.wait_ge(t_h[i].h, t_h[i].at(pr, 1))
                if i >= 2:
                    pe.wait_ge(t_y[i - 2].h, t_y[i - 2].at(pr, 1))
                for c in range(2):
                    last = mm(y_bank[i % 2][:, c * C:(c + 1) * C], e_h[i % 2][:, c * 128:(c + 1) * 128], e_w2[i])
                last.then_inc(t_yps[i].h, t_yps[i].up())

            with pe.Fori(0, E1 // 4) as pr:
                batch_starts()
                expert_in(pr, 0)
                expert_in(pr, 1)
                expert_up(pr, 0)
                expert_up(pr, 1)
                expert_in(pr, 2)
                expert_in(pr, 3)
                expert_down(pr, 0)
                expert_down(pr, 1)
                expert_up(pr, 2)
                expert_up(pr, 3)
                expert_down(pr, 2)
                expert_down(pr, 3)
                batch_ends()

        @block.scalar
        def _(act):
            for dst, src in layer_loads:
                act.dma_start(ap(dst) if not isinstance(dst, bass.AP) else dst, src).then_inc(s_curw, 16)

            def tok_exp(nb):
                act.wait_ge(lg_sub.h, lg_sub.at(nb, 1))
                act.activation(lg[:, :, :], lg[:, :, :], ACT.Exp).then_inc(lg_exp.h, lg_exp.up())

            def tok_band(tb, n):
                act.wait_ge(tok_full.h, tok_full.at(tb, 2 + n))
                t = n // 2
                if n % 2 == 0:
                    act.activation(bandT[:, :], L[0:TW, 0:HEADS_T * TT], ACT.Copy)\
                        .then_inc(bandT_ready.h, bandT_ready.up())
                else:
                    act.activation(y32[:, t * TT:(t + 1) * TT], L[:, 0:TT], ACT.Identity, bias=tok_bias[:, 0:1])\
                        .then_inc(y_ready.h, y_ready.up())

            def conv_out(nb, p):
                if nb is None or p not in CHUNK_END:
                    return
                o = CHUNK_END[p]
                i, nth = C_AT[("cross", o)]
                act.wait_ge(c_full[i].h, c_full[i].at(nb, nth))
                if o >= 1 or not (isinstance(nb, int) and nb == 0):
                    act.wait_ge(zneg_ready.h, zneg_ready.at(nb, o))
                ins = act.activation(zc[:, :], Cb[i][:, 0:TOK], ACT.Identity, bias=conv_b[:, o:o + 1], scale=1.0 / LO)
                ins.then_inc(zc_ready.h, zc_ready.up())
                act.wait_ge(zneg_ready.h, zneg_ready.at(nb, o + 1))
                act.activation(zneg[:, :], zneg[:, :], ACT.Exp).then_inc(zexp_ready.h, zexp_ready.up())

            def late(b, unit):
                if b is None or LATE_UNIT.get(unit) != "gate1":
                    return
                act.wait_ge(late_full.h, late_full.at(b, 1 + LATE.index("gate1")))
                act.activation(sc[:, :, :], L[0:A, 0:J * E1], ACT.Exp, scale=-1.0).then_inc(gate1_exp.h, gate1_exp.up())

            def tanh_in(b, use, n):
                i, nth = W_AT[use]
                act.wait_ge(w_full[i].h, w_full[i].at(b, nth))
                if n >= 2:
                    act.wait_ge(hid_ready.h, hid_ready.at(b, n - 1))
                act.activation(th[:, n % 2, :], W[i][:, 0:TOK], ACT.Tanh, scale=0.5).then_inc(th_ready.h, th_ready.up())

            def present(b, nb, tb, lb):
                for h in range(H0):
                    i, nth = W_AT[("q", h)]
                    act.wait_ge(w_full[i].h, w_full[i].at(b, nth))
                    act.activation(Q[:, h, :], W[i][:, 0:TOK], ACT.Identity, bias=q_b[:, h:h + 1],
                                              scale=DH ** -0.5).then_inc(q_ready.h, q_ready.up())
                if tb is not None:
                    tok_exp(tb)
                for s in range(UNITS + 1):
                    if s < UNITS:
                        i, nth = W_AT[("S", s)]
                        act.wait_ge(w_full[i].h, w_full[i].at(b, nth))
                        if s >= 2:
                            bank, nth = W_AT[("T", s - 2)]
                            act.wait_ge(w_full[bank].h, w_full[bank].at(b, nth))
                        act.wait_ge(nmax_ready.h, nmax_ready.at(b, s + 1))
                        act.activation(Pm[:, s % 2, :], W[i][0:A, 0:TOK], ACT.Exp,
                                                  bias=nmax[:, s % 2:s % 2 + 1],
                                                  accum_out=psums[:, s // J, s % J:s % J + 1]).then_inc(p_ready.h, p_ready.up())
                        late(lb, s)
                        conv_out(nb, 3 + s)
                    if s >= 1 and (s - 1) % 2 == 0:
                        u = s - 1
                        i, nth = W_AT[("T", u)]
                        act.wait_ge(w_full[i].h, w_full[i].at(b, nth))
                        if u >= 2:
                            pt_used(act, b, u - 2)
                        act.activation(PT[:, 0, :], W[i][0:A, 0:TOK], ACT.Copy).then_inc(pt_ready_a.h, pt_ready_a.up())
                for j in range(J):
                    i, nth = W_AT[("oT", j)]
                    act.wait_ge(w_full[i].h, w_full[i].at(b, nth))
                    act.activation(OT[:, j, :], W[i][:, 0:4 * A], ACT.Copy).then_inc(oT_ready.h, oT_ready.up())
                act.wait_ge(gexp_in.h, gexp_in.at(b, 1))
                act.activation(gl[:, :], gl[:, :], ACT.Exp).then_inc(gexp_out.h, gexp_out.up())
                p = 3 + UNITS + 4
                for n in range(NHID):
                    tanh_in(b, ("hid", n) if n < 2 * E0 else ("sg", n - 2 * E0), n)
                    if tb is not None and n % 2 == 0 and n < 4 * TILES:
                        tok_band(tb, n // 2)
                    conv_out(nb, p)
                    p += 1

            act.wait_ge(s_tokw, 16 * len(tok_loads))
            batch_starts()
            tok_exp(0)
            for n in range(2 * OC):
                act.wait_ge(s_stage[n % 2], 16 * (n // 2 + 1))
                act.activation(wc_hi[:, n // 2, (n % 2) * HALF:(n % 2 + 1) * HALF], stage[n % 2], ACT.Copy).then_inc(s_hi, 1)
                if n == 3:
                    for m in range(2 * TILES):
                        tok_band(0, m)
            tok_exp(1)
            for p in range(POINTS):
                conv_out(0, p)
                if p >= 3 + UNITS and p < 3 + UNITS + 2 * TILES:
                    tok_band(1, p - 3 - UNITS)
            act.wait_ge(s_setup, 1)
            present(0, 1, 2, None)
            with act.Fori(1, B - 1) as it:
                batch_starts()
                present(it, it + 1, it + 2, it - 1)
                batch_ends()
            present(B - 1, None, None, B - 2)
            for s in range(UNITS):
                late(B - 1, s)

            def expert_xT(pr, i):
                act.wait_ge(t_xps[i].h, t_xps[i].at(pr, 1))
                act.activation(e_xT[i % 2], W[i % 2][:, 0:CAP], ACT.Copy).then_inc(t_xT[i].h, t_xT[i].up())

            def expert_tanh(pr, i):
                act.wait_ge(t_hps[i].h, t_hps[i].at(pr, 1))
                act.activation(e_th[i % 2], Ob[i % 2][0:F1, 0:CAP], ACT.Tanh, scale=0.5).then_inc(t_th[i].h, t_th[i].up())

            with act.Fori(0, E1 // 4) as pr:
                batch_starts()
                for i in 0, 2:
                    expert_xT(pr, i)
                    expert_xT(pr, i + 1)
                    expert_tanh(pr, i)
                    expert_tanh(pr, i + 1)
                batch_ends()

        @block.vector
        def _(dve):
            chain = [step_main, 0]
            steps = {}

            def turn_to(sig, b, first=False):
                chain[:] = [sig, b]
                if first:
                    steps[sig.name] = 0

            def link(ins):
                sig, b = chain
                ins.then_inc(sig.h, sig.up())
                steps[sig.name] += 1
                dve.wait_ge(sig.h, sig.at(b, steps[sig.name]))

            def tok_softmax(nb):
                turn_to(step_tok, nb, first=True)
                dve.wait_ge(tok_full.h, tok_full.at(nb, 1))
                if not (isinstance(nb, int) and nb == 0):
                    dve.wait_ge(band_out.h, band_out.at(nb, 0))
                lgf = lg[:, :, :].rearrange("p i n -> p (i n)")
                ins = dve.tensor_tensor(lg[:, :, :], L[0:TT, 0:TILES * LK].rearrange("p (i n) -> p i n", i=TILES),
                                        tok_mask[:, :, :], ALU.add)
                link(ins)
                by_head = lg[:, :, :].rearrange("p i (k h) -> p i h k", h=HEADS_T)
                flat = lambda x: x[:, :].rearrange("p (i h) -> p i h", h=HEADS_T)
                spread = lambda x: flat(x).unsqueeze(3).to_broadcast((TT, TILES, HEADS_T, TAPS))
                link(dve.tensor_reduce(flat(lmax), by_head, AX.X, ALU.max))
                dve.tensor_tensor(by_head, by_head, spread(lmax), ALU.subtract).then_inc(lg_sub.h, lg_sub.up())
                dve.wait_ge(lg_exp.h, lg_exp.at(nb, 1))
                link(dve.tensor_reduce(flat(lsum), by_head, AX.X, ALU.add))
                link(dve.reciprocal(lsum[:, :], lsum[:, :]))
                dve.tensor_tensor(by_head, by_head, spread(lsum), ALU.mult).then_inc(taps_ready.h, taps_ready.up())

            def tok_split(nb):
                turn_to(step_tok, nb)
                dve.wait_ge(y_ready.h, y_ready.at(nb, TILES))
                link(dve.tensor_copy(y_hi[:, :], y32[:, :]))
                link(dve.tensor_tensor(y32[:, :], y32[:, :], y_hi[:, :], ALU.subtract))
                dve.tensor_scalar(y_lo[:, :], y32[:, :], LO, None, ALU.mult).then_inc(y_split.h, y_split.up())

            def conv_out(nb, p):
                if nb is None or p not in CHUNK_END:
                    return
                saved = list(chain)
                o = CHUNK_END[p]
                turn_to(step_conv, nb, first=(o == 0))
                i, nth = C_AT[("main", o)]
                dve.wait_ge(c_full[i].h, c_full[i].at(nb, nth))
                dve.wait_ge(zc_ready.h, zc_ready.at(nb, o + 1))
                link(dve.tensor_tensor(z[:, :], Cb[i][:, 0:TOK], zc[:, :], ALU.add))
                dve.tensor_scalar(zneg[:, :], z[:, :], 0.0, None, ALU.min).then_inc(zneg_ready.h, zneg_ready.up())
                dve.wait_ge(zneg_ready.h, zneg_ready.at(nb, o + 1))
                link(dve.tensor_scalar(z[:, :], z[:, :], 0.0, ALPHA, ALU.max, ALU.subtract))
                dve.wait_ge(zexp_ready.h, zexp_ready.at(nb, o + 1))
                ins = dve.scalar_tensor_tensor(selu[:, o, :], zneg[:, :], ALPHA, z[:, :], ALU.mult, ALU.add)
                ins.then_inc(selu_ready.h, selu_ready.up())
                dve.wait_ge(selu_ready.h, selu_ready.at(nb, o + 1))
                chain[:] = saved

            def tok_out(nb):
                i, nth = C_AT[("w2", 0)]
                dve.wait_ge(c_full[i].h, c_full[i].at(nb, nth))
                h = h0[:, :].rearrange("p (j c) -> p j c", j=J)
                dve.scalar_tensor_tensor(h, Cb[i][0:A, 0:J * C].rearrange("p (j c) -> p j c", j=J), LAMBDA,
                                         b2[:, :].unsqueeze(1).to_broadcast((A, J, C)), ALU.mult, ALU.add)\
                    .then_inc(h0_ready.h, h0_ready.up())
                dve.wait_ge(h0_ready.h, h0_ready.at(nb, 1))

            def hold():
                dve.memset(gate_dve[:, :], 0.0)

            def norm_stats(b, n, src, g):
                for j in range(J):
                    ins = dve.bn_stats(bn[g][:, j, :], src[:, j * C:(j + 1) * C])
                link(ins)
                hold()
                for j in range(J):
                    ins = dve.bn_aggr(mv[g][:, j, :], bn[g][:, j, :])
                link(ins)
                if n == 1 and g == 0:
                    ins = dve.tensor_scalar(ve[g][:, :], mv[g][:, :, 1], 1.0 + EPS, EPS * EPS, ALU.mult, ALU.add)
                else:
                    ins = dve.tensor_scalar(ve[g][:, :], mv[g][:, :, 1], EPS, None, ALU.add)
                ins.then_inc(ln_var[g].h, ln_var[g].up())

            def norm_rows(b, n, src, g):
                dve.wait_ge(ln_rstd[g].h, ln_rstd[g].at(b, n))
                for j in range(J):
                    dst = rows[:, j, 0:C] if (n, g) == (2, 1) else xh[g][:, j, :]
                    ins = dve.tensor_scalar(dst, src[:, j * C:(j + 1) * C], mv[g][:, j, 0:1], rstd[g][:, j:j + 1],
                                            ALU.subtract, ALU.mult)
                ins.then_inc(xh_ready[g].h, xh_ready[g].up())

            def norm(b, n, src):
                norm_stats(b, n, src, 0)
                norm_rows(b, n, src, 0)
                i, nth = W_AT[("ln", n)]
                dve.wait_ge(w_full[i].h, w_full[i].at(b, nth))
                if n == 1:
                    ins = dve.tensor_scalar(xT[:, :], W[i][:, 0:TOK], gamma[:, 0:1], beta[:, 0:1], ALU.mult, ALU.add)
                else:
                    ins = dve.tensor_copy(xT[:, :], W[i][:, 0:TOK])
                ins.then_inc(xT_ready[0].h, xT_ready[0].up())

            def ranks(score):
                sview = score.rearrange("p (j g) -> p j g", g=8)
                ca = cmp_a[:, :, :].rearrange("p (j g) q -> p j g q", j=J)
                cb = cmp_b[:, :, :].rearrange("p (j g) q -> p j g q", j=J)
                other = sview.unsqueeze(2).to_broadcast((A, J, 8, 8))
                own = sview.unsqueeze(3).to_broadcast((A, J, 8, 8))
                low = before[:, :, :].unsqueeze(1).to_broadcast((A, J, 8, 8))
                dve.tensor_tensor(cb, other, own, ALU.is_gt)
                link(dve.tensor_tensor(ca, other, own, ALU.is_ge))
                link(dve.tensor_tensor(ca, ca, low, ALU.mult))
                link(dve.tensor_tensor(ca, ca, cb, ALU.max))
                link(dve.tensor_reduce(rank[:, :], cmp_a[:, :, :], AX.X, ALU.add))

            def late(b, unit):
                if b is None:
                    return
                saved = list(chain)
                turn_to(step_late, b, first=(unit == 0))
                use = LATE_UNIT.get(unit)
                if use:
                    dve.wait_ge(late_full.h, late_full.at(b, 1 + LATE.index(use)))
                ss3 = ss[:, :, :].rearrange("p (j g) q -> p j (g q)", j=J)
                if unit == 0:
                    norm_stats(b, 1, h2, 1)
                elif unit == 1:
                    norm_rows(b, 1, h2, 1)
                elif use == "ln3":
                    dve.tensor_copy(xTs[1][:, :].rearrange("c (a j) -> c j a", j=J),
                                    L[:, 0:TOK].rearrange("c (j a) -> c j a", j=J))\
                        .then_inc(xT_ready[1].h, xT_ready[1].up())
                elif use == "q1":
                    dve.tensor_tensor(qT1[:, :, :], L[:, 0:TOK].rearrange("c (j a) -> c j a", j=J),
                                      bin_col[:, :].unsqueeze(2).to_broadcast((C, J, A)), ALU.add)\
                        .then_inc(qkv1_ready.h, qkv1_ready.up())
                elif use in ("k1", "v1"):
                    dst = k1 if use == "k1" else v1
                    dve.tensor_tensor(dst[:, :], L[0:A, 0:3 * C], bin_row[:, :], ALU.add)\
                        .then_inc(qkv1_ready.h, qkv1_ready.up())
                elif use == "kv":
                    dve.tensor_tensor(kv[:, :], L[:, 0:C], kvmask[:, :], ALU.mult).then_inc(kv_ready.h, kv_ready.up())
                elif use == "g":
                    dve.tensor_copy(G[:, :], L[:, 0:C]).then_inc(g_ready.h, g_ready.up())
                    h2v = h2[:, :].rearrange("p (j c) -> p j c", j=J)
                    link(dve.tensor_tensor(h2v, h2v, bo1[:, :].unsqueeze(1).to_broadcast((A, J, C)), ALU.add))
                elif use == "out1":
                    dve.wait_ge(h3_stored.h, h3_stored.at(b, 0))
                    dve.tensor_tensor(h3[:, :], L[0:A, 0:J * C], h2[:, :], ALU.add).then_inc(h3_ready.h, h3_ready.up())
                elif unit == 9:
                    dve.wait_ge(h3_ready.h, h3_ready.at(b, 1))
                    norm_stats(b, 2, h3, 1)
                elif unit == 10:
                    dve.wait_ge(rows_sent.h, rows_sent.at(b, 0))
                    norm_rows(b, 2, h3, 1)
                elif use == "ln4":
                    dve.tensor_copy(xTs[1][:, :], L[:, 0:TOK]).then_inc(xT_ready[1].h, xT_ready[1].up())
                elif unit == 13:
                    dve.wait_ge(gate1_exp.h, gate1_exp.at(b, 1))
                    link(dve.tensor_scalar(sc[:, :, :], sc[:, :, :], 1.0, None, ALU.add))
                    link(dve.reciprocal(sc[:, :, :], sc[:, :, :]))
                    link(dve.tensor_tensor(ss3, sc[:, :, :], gate1_b[:, :].unsqueeze(1).to_broadcast((A, J, E1)), ALU.add))
                elif unit == 14:
                    dve.tensor_tensor(tlo[:, :, :], ss[:, :, 0:4], ss[:, :, 4:8], ALU.min)
                    link(dve.tensor_tensor(thi[:, :, :], ss[:, :, 0:4], ss[:, :, 4:8], ALU.max))
                    for w in (2, 1):
                        dve.tensor_tensor(tmi[:, :, 0:w], thi[:, :, 0:w], thi[:, :, w:2 * w], ALU.min)
                        link(dve.tensor_tensor(tlo[:, :, 0:w], tlo[:, :, 0:w], tlo[:, :, w:2 * w], ALU.max))
                        link(dve.tensor_tensor(thi[:, :, 0:w], thi[:, :, 0:w], thi[:, :, w:2 * w], ALU.max))
                        link(dve.tensor_tensor(tlo[:, :, 0:w], tlo[:, :, 0:w], tmi[:, :, 0:w], ALU.max))
                    link(dve.tensor_tensor(gl[:, :].unsqueeze(2), thi[:, :, 0:1], tlo[:, :, 0:1], ALU.add))
                elif unit == 15:
                    ranks(gl[:, :])
                elif unit == 16:
                    link(dve.tensor_scalar(gl[:, :], rank[:, :], 4.0, None, ALU.is_lt))
                    dve.tensor_scalar(gpen[:, :], gl[:, :], 1.0, 1e30, ALU.subtract, ALU.mult)
                    link(dve.tensor_tensor(ss[:, :, :], ss[:, :, :], gl[:, :].unsqueeze(2).to_broadcast((A, J * 8, 8)), ALU.mult))
                    link(dve.tensor_tensor(ss[:, :, :], ss[:, :, :], gpen[:, :].unsqueeze(2).to_broadcast((A, J * 8, 8)), ALU.add))
                elif unit == 17:
                    hold()
                    for j in range(J):
                        ins = dve.max(top[:, j, :], ss3[:, j, :])
                    link(ins)
                elif unit == 18:
                    hold()
                    for j in range(J):
                        ins = dve.match_replace(mr[:, j, :], top[:, j, :], ss3[:, j, :], -3e30)
                    link(ins)
                    dve.tensor_tensor(sel[:, :, :], mr[:, :, :], ss3, ALU.not_equal).then_inc(sel_ready.h, sel_ready.up())
                    dve.wait_ge(sel_ready.h, sel_ready.at(b, 1))
                elif unit == 19:
                    link(dve.tensor_tensor(sc[:, :, :], sc[:, :, :], sel[:, :, :], ALU.mult))
                    link(dve.tensor_reduce(gsum[:, :], sc[:, :, :], AX.X, ALU.add))
                    link(dve.reciprocal(gsum[:, :], gsum[:, :]))
                    dve.scalar_tensor_tensor(rows[:, :, C:C + E1], sc[:, :, :], 2.5,
                                             gsum[:, :].unsqueeze(2).to_broadcast((A, J, E1)), ALU.mult, ALU.mult)
                    link(dve.tensor_copy(rows[:, :, C + E1], tokens[:, :]))
                    link(dve.tensor_scalar(tokens[:, :], tokens[:, :], float(TOK), None, ALU.add))
                elif use == "count":
                    link(dve.tensor_tensor(pos[:, :, :], L[0:A, 0:J * E1].rearrange("p (j e) -> p j e", j=J),
                                           carry[:, :].unsqueeze(1).to_broadcast((A, J, E1)), ALU.add))
                    dve.tensor_tensor(carry[:, :], L[0:A, J * E1:(J + 1) * E1], carry[:, :], ALU.add)\
                        .then_inc(counted.h, counted.up())
                    link(dve.scalar_tensor_tensor(mr[:, :, :], pos[:, :, :], float(CAP), sel[:, :, :], ALU.is_lt, ALU.mult))
                    link(dve.tensor_tensor(pos[:, :, :], slot_base[:, :, :], pos[:, :, :], ALU.subtract))
                    link(dve.tensor_tensor(pos[:, :, :], pos[:, :, :], mr[:, :, :], ALU.mult))
                elif unit == 22:
                    hold()
                    for j in range(J):
                        ins = dve.max(top[:, j, :], pos[:, j, :])
                    link(ins)
                    dve.tensor_scalar(slot_i[:, :], top[:, :, :].rearrange("p j k -> p (j k)"), -1.0,
                                                    float(SLOTS), ALU.mult, ALU.add).then_inc(rows_ready.h, rows_ready.up())
                chain[:] = saved

            def present(b, nb, tb, lb):
                turn_to(step_main, b, first=True)
                norm(b, 1, h0)
                for h in range(0, H0, 2):
                    g = h // 2
                    i, nth = W_AT[("k", g)]
                    dve.wait_ge(w_full[i].h, w_full[i].at(b, nth))
                    dve.tensor_scalar(KP[0:DH, h, :], W[i][0:DH, 0:TOK], k_b[0:DH, g:g + 1], None, ALU.add)
                    dve.tensor_scalar(KP[DH:, h + 1, :], W[i][DH:, 0:TOK], k_b[DH:, g:g + 1], None, ALU.add).then_inc(kvp_ready.h, kvp_ready.up())
                for j in range(J):
                    i, nth = W_AT[("v", j)]
                    dve.wait_ge(w_full[i].h, w_full[i].at(b, nth))
                    dve.tensor_tensor(V[:, j, :], W[i][0:A, :], v_b[:, :], ALU.add).then_inc(kvp_ready.h, kvp_ready.up())
                if tb is not None:
                    tok_softmax(tb)
                turn_to(step_main, b)
                for s in range(UNITS + 3):
                    if s < UNITS:
                        i, nth = W_AT[("S", s)]
                        dve.wait_ge(w_full[i].h, w_full[i].at(b, nth))
                        if s >= 2:
                            dve.wait_ge(p_ready.h, p_ready.at(b, s - 1))
                        dve.tensor_reduce(nmax[:, s % 2:s % 2 + 1], W[i][0:A, 0:TOK], AX.X, ALU.max,
                                                        negate=True).then_inc(nmax_ready.h, nmax_ready.up())
                        late(lb, s)
                    if 1 <= s <= UNITS and (s - 1) % 2 == 1:
                        u = s - 1
                        i, nth = W_AT[("T", u)]
                        dve.wait_ge(w_full[i].h, w_full[i].at(b, nth))
                        if u >= 2:
                            pt_used(dve, b, u - 2)
                        dve.tensor_copy(PT[:, 1, :], W[i][0:A, 0:TOK]).then_inc(pt_ready_d.h, pt_ready_d.up())
                    if s < UNITS:
                        conv_out(nb, 3 + s)
                    if s >= 4 and (s - 4) % J == J - 1 and (s - 4) // J < H0 - 1 or s == UNITS + 2:
                        h = (s - 4) // J if s < UNITS + 2 else H0 - 1
                        dve.wait_ge(p_ready.h, p_ready.at(b, J * h + J))
                        link(dve.reciprocal(prec[:, h, :], psums[:, h, :]))
                        i, nth = O_AT[("O", h)]
                        dve.wait_ge(o_full[i].h, o_full[i].at(b, nth))
                        dve.tensor_tensor(
                            O[:, :, h * DH:(h + 1) * DH], Ob[i][0:A, 0:J * DH].rearrange("p (j d) -> p j d", j=J),
                            prec[:, h, :].unsqueeze(2).to_broadcast((A, J, DH)), ALU.mult).then_inc(o_ready.h, o_ready.up())
                link(dve.tensor_tensor(h0b[:, :].rearrange("p (j c) -> p j c", j=J),
                                       h0[:, :].rearrange("p (j c) -> p j c", j=J),
                                       bo[:, :].unsqueeze(1).to_broadcast((A, J, C)), ALU.add))
                i, nth = W_AT[("out0", 0)]
                dve.wait_ge(w_full[i].h, w_full[i].at(b, nth))
                link(dve.tensor_tensor(h1[:, :], W[i][0:A, 0:J * C], h0b[:, :], ALU.add))

                norm(b, 2, h1)
                i, nth = W_AT[("gate0", 0)]
                dve.wait_ge(w_full[i].h, w_full[i].at(b, nth))
                link(dve.tensor_copy(gl[:, :], W[i][0:A, 0:J * E0]))
                ranks(gl[:, :])
                gl3 = gl[:, :].rearrange("p (j g) -> p j g", g=8)
                spread8 = lambda x: x[:, :].unsqueeze(2).to_broadcast((A, J, 8))
                link(dve.tensor_reduce(gmx[:, :], gl3, AX.X, ALU.max))
                dve.tensor_tensor(gl3, gl3, spread8(gmx), ALU.subtract).then_inc(gexp_in.h, gexp_in.up())
                dve.wait_ge(gexp_out.h, gexp_out.at(b, 1))
                link(dve.scalar_tensor_tensor(comb[:, :], rank[:, :], 2.0, gl[:, :], ALU.is_lt, ALU.mult))
                link(dve.tensor_reduce(gsum[:, :], comb[:, :].rearrange("p (j g) -> p j g", g=8), AX.X, ALU.add))
                link(dve.reciprocal(gsum[:, :], gsum[:, :]))
                c3 = comb[:, :].rearrange("p (j g) -> p j g", g=8)
                link(dve.scalar_tensor_tensor(c3, c3, 0.5, spread8(gsum), ALU.mult, ALU.mult))
                p = 3 + UNITS + 4

                def mixed(e):
                    o, nth = O_AT[("Y", e)]
                    dve.wait_ge(o_full[o].h, o_full[o].at(b, nth))
                    src = h1 if e == 0 else h2
                    for j in range(J):
                        s = slice(j * C, (j + 1) * C)
                        scale = comb[:, j * 8 + e:j * 8 + e + 1] if e < E0 else 0.5
                        ins = dve.scalar_tensor_tensor(h2[:, s], Ob[o][0:A, s], scale, src[:, s], ALU.mult, ALU.add)
                    ins.then_inc(y_added.h, y_added.up())
                    dve.wait_ge(y_added.h, y_added.at(b, e + 1))

                for e in range(E0 + 1):
                    for c in range(2):
                        n = 2 * e + c
                        dst = hid[:, 2 * (e % 2) + c, :]
                        if e >= 2:
                            bank, nth = O_AT[("Y", e - 2)]
                            dve.wait_ge(o_full[bank].h, o_full[bank].at(b, nth))
                        dve.wait_ge(th_ready.h, th_ready.at(b, n + 1))
                        if e < E0:
                            i, nth = W_AT[("hid", n)]
                            dve.wait_ge(w_full[i].h, w_full[i].at(b, nth))
                            dve.scalar_tensor_tensor(dst, th[:, n % 2, :], 1.0, W[i][:, 0:TOK],
                                                                  ALU.add, ALU.mult).then_inc(hid_ready.h, hid_ready.up())
                        else:
                            i, nth = W_AT[("sg", c)]
                            dve.wait_ge(w_full[i].h, w_full[i].at(b, nth))
                            link(dve.scalar_tensor_tensor(sgate[:, :], th[:, n % 2, :], 1.0, W[i][:, 0:TOK],
                                                          ALU.add, ALU.mult))
                            i, nth = W_AT[("su", c)]
                            dve.wait_ge(w_full[i].h, w_full[i].at(b, nth))
                            dve.tensor_tensor(dst, W[i][:, 0:TOK], sgate[:, :], ALU.mult).then_inc(hid_ready.h, hid_ready.up())
                            dve.wait_ge(hid_ready.h, hid_ready.at(b, n + 1))
                        conv_out(nb, p)
                        p += 1
                        if n == NHID - 2 and tb is not None:
                            tok_split(tb)
                            turn_to(step_main, b)
                    if e >= 1:
                        mixed(e - 1)
                conv_out(nb, p)
                p += 1
                mixed(E0)
                assert p == POINTS
                if nb is not None:
                    tok_out(nb)

            n_set = [0]

            def done(ins):
                n_set[0] += 1
                ins.then_inc(s_set, 1)
                dve.wait_ge(s_set, n_set[0])

            done(dve.memset(carry[:, :], 0.0))
            dve.wait_ge(s_tokw, 16 * len(tok_loads))
            done(dve.tensor_tensor(tok_mask[:, :, :], tok_mask[:, :, :],
                                   tok_bl[:, :].unsqueeze(1).to_broadcast((TT, TILES, LK)), ALU.add))
            batch_starts()
            tok_softmax(0)

            def split_weights(n):
                half = slice((n % 2) * HALF, (n % 2 + 1) * HALF)
                dve.wait_ge(s_hi, n + 1)
                done(dve.tensor_tensor(stage[n % 2], stage[n % 2], wc_hi[:, n // 2, half], ALU.subtract))
                dve.tensor_scalar(wc_lo[:, n // 2, half], stage[n % 2], LO, None, ALU.mult).then_inc(s_lo, 1)
            for n in range(4):
                split_weights(n)
            tok_split(0)
            for n in range(4, 2 * OC):
                split_weights(n)
            dve.wait_ge(s_curw, 16 * len(layer_loads))
            for sig in t_out:
                dve.wait_ge(sig.h, 16)
            done(dve.tensor_tensor(q_b[:, :], q_b[:, :], uv[:, :], ALU.add))
            done(dve.tensor_scalar(q_b[:, :], q_b[:, :], DH ** -0.5, None, ALU.mult))
            for g in range(H0 // 2):
                dve.wait_ge(s_pos, g + 1)
                dve.tensor_copy(KP[0:DH, 2 * g + 1, :], W[g % 2][0:DH, 0:TOK])
                dve.tensor_copy(KP[DH:, 2 * g, :], W[g % 2][DH:, 0:TOK]).then_inc(s_posu, 1)
            dve.tensor_copy(tri[:, :, :], tri_f).then_inc(s_setup, 1)
            tok_softmax(1)
            for p in range(POINTS):
                conv_out(0, p)
            tok_split(1)
            tok_out(0)
            present(0, 1, 2, None)
            with dve.Fori(1, B - 1) as it:
                batch_starts()
                present(it, it + 1, it + 2, it - 1)
                batch_ends()
            present(B - 1, None, None, B - 2)
            for s in range(UNITS):
                late(B - 1, s)

            def expert_h(pr, i):
                k = i % 2
                dve.wait_ge(t_th[i].h, t_th[i].at(pr, 1))
                link(dve.scalar_tensor_tensor(e_s, e_th[k], 1.0, Ob[k][0:F1, 0:CAP], ALU.add, ALU.mult))
                dve.tensor_tensor(e_h[k], Cb[k][0:F1, 0:CAP], e_s, ALU.mult).then_inc(t_h[i].h, t_h[i].up())
                dve.wait_ge(t_h[i].h, t_h[i].at(pr, 1))

            def expert_y(pr, i):
                dve.wait_ge(t_out[i].h, t_out[i].at(pr, 0))
                dve.wait_ge(t_yps[i].h, t_yps[i].at(pr, 1))
                dve.tensor_copy(e_idx[i], e_rows[i][:, :, C + E1])
                y = (W[2], L)[i % 2]
                for c in range(2):
                    w = e_rows[i][:, c, bass.ds(pr * 4 + (C + i), 1)]
                    ins = dve.tensor_scalar(e_y[i][:, c, :], y[:, c * C:(c + 1) * C], w, 0.5, ALU.mult, ALU.mult)
                ins.then_inc(t_y[i].h, t_y[i].up())

            with dve.Fori(0, E1 // 4) as pr:
                batch_starts()
                turn_to(t_s, pr, first=True)
                for i in 0, 2:
                    expert_h(pr, i)
                    expert_h(pr, i + 1)
                    expert_y(pr, i)
                    expert_y(pr, i + 1)
                batch_ends()
    return totals


def pack(i):
    f = lambda a: np.ascontiguousarray(a)
    d = {}
    x = i["x"]
    pad = (TAPS - 1) // 2
    x = np.concatenate([x, np.zeros((1, T, C), np.float32)], axis=0)
    zrow = np.zeros((B + 1, pad, C), np.float32)
    xpad = np.concatenate([zrow, x, np.zeros((B + 1, TP - T, C), np.float32), zrow], axis=1)
    d["xpad"] = f(xpad)
    d["xTp"] = f(xpad[:, pad:pad + TP].transpose(0, 2, 1))
    by_tap = lambda w: w.reshape(HEADS_T, TAPS, -1).transpose(1, 0, 2).reshape(LK, -1)
    d["wlT"] = f(by_tap(i["L0_tok_Wl"]).T)
    d["tok_bl"] = f(by_tap(i["L0_tok_bl"])[:, 0])
    t = np.arange(TP)[:, None] + np.arange(TAPS)[None, :] - pad
    ok = (t >= 0) & (t < T)
    mask = np.where(ok, 0.0, -1e30).astype(np.float32).reshape(TILES, TT, TAPS)
    d["tok_mask"] = f(np.repeat(mask.transpose(1, 0, 2)[..., None], HEADS_T, axis=3).reshape(TT, TILES, LK))
    d["tok_bias"] = f(i["L0_tok_bias"][:, None])
    d["conv_b"] = f(i["L0_tok_bc"].reshape(OC, 128).T)
    d["w2T"] = f(i["L0_tok_W2"].T.reshape(OC, 128, C).transpose(1, 0, 2))
    d["b2"] = f(i["L0_tok_b2"])
    d["wc"] = f(i["L0_tok_Wc"].reshape(OC, 128, C, TAPS).transpose(0, 2, 3, 1).reshape(OC, C, TAPS * 128))
    d["gamma"], d["beta"] = f(i["L0_attn_gamma"][:, None]), f(i["L0_attn_beta"][:, None])
    wq, wk, wv = np.split(i["L0_attn_w_qkv"], 3, axis=0)
    bq, bk, bv = np.split(i["L0_attn_b_qkv"], 3)
    d["wqT"] = f(wq.T.reshape(C, H0, DH))
    d["wkT"], d["wvT"] = f(wk.T), f(wv.T)
    d["q_b"] = f(bq.reshape(H0, DH).T)
    d["k_b"] = f(bk.reshape(H0 // 2, 128).T)
    d["v_b"] = f(bv)
    u, v = i["L0_attn_u_bias"].T, i["L0_attn_v_bias"].T
    uv = np.empty((128, H0), np.float32)
    uv[:DH, 0::2], uv[DH:, 0::2], uv[:DH, 1::2], uv[DH:, 1::2] = u[:, 0::2], v[:, 0::2], v[:, 1::2], u[:, 1::2]
    d["uv"] = uv
    rel = np.arange(TOK, dtype=np.float32)[:, None] - np.arange(C, dtype=np.float32)[None, :]
    freq = np.exp(-np.arange(0, 2 * C, 2, dtype=np.float32) * np.float32(np.log(10000.0) / C)).astype(np.float32)
    angle = (rel * freq[None, :]).astype(np.float32)
    pe = np.where(np.arange(C)[None, :] % 2 == 0, np.cos(angle), np.sin(angle)).astype(np.float32)
    d["peT"] = f(pe.reshape(A, J, C).transpose(2, 1, 0).reshape(C, TOK))
    d["wposT"] = f(i["L0_attn_w_pos"].reshape(H0 // 2, 2, DH, C)[:, ::-1].reshape(H0 * DH, C).T)
    d["woT"] = f(i["L0_attn_w_out"].T.reshape(4, 128, C).transpose(1, 0, 2))
    d["bo"] = f(i["L0_attn_b_out"])
    d["gate0T"] = f(i["L0_ffn_gate_w"].T)
    d["w1T"] = f(i["L0_ffn_w1"].reshape(E0 * F0, C).T)
    d["w2eT"] = f(i["L0_ffn_w2"].transpose(0, 2, 1).reshape(E0 * 2, 128, C).transpose(1, 0, 2))
    d["sgT"], d["suT"] = f(i["L0_ffn_sg_gate"].T), f(i["L0_ffn_sg_up"].T)
    d["sdT"] = f(i["L0_ffn_sg_down"].T.reshape(2, 128, C).transpose(1, 0, 2))
    d["winT"] = f(i["L1_attn_w_in"].T)
    d["bin_col"] = f(i["L1_attn_b_in"].reshape(3, C).T)
    d["bin_row"] = f(i["L1_attn_b_in"])
    d["kvmask"] = np.kron(np.eye(8, dtype=np.float32), np.full((16, 16), 0.25, np.float32))
    d["wo1T"] = f(i["L1_attn_w_out"].T)
    d["bo1"] = f(i["L1_attn_b_out"])
    d["gate1T"] = f(i["L1_ffn_gate_w"].T)
    d["gate1_b"] = f(i["L1_ffn_gate_b"])
    d["w1e"], d["w3e"], d["w2e"] = f(i["L1_ffn_w1"]), f(i["L1_ffn_w3"]), f(i["L1_ffn_w2"])
    d["slot_base"] = np.broadcast_to(SLOTS - CAP * np.arange(E1, dtype=np.float32), (A, J, E1)).copy()
    n8 = np.arange(8)
    d["before"] = np.broadcast_to((n8[None, :] < n8[:, None]).astype(np.float32), (A, 8, 8)).copy()
    d["tokens"] = (np.arange(A)[:, None] * J + np.arange(J)[None, :]).astype(np.float32)
    a = np.arange(A)
    tri = np.stack([a[:, None] < a[None, :], a[:, None] <= a[None, :], np.ones((A, A), bool)], axis=1)
    d["tri"] = tri.astype(np.float32)
    d["ident"] = np.eye(128, dtype=np.float32)
    empty = np.zeros((CAP, ROW), np.float32)
    empty[:, C + E1] = NTOK + np.arange(CAP)
    d["empty_slots"] = empty
    return d


def kernel(**inputs):
    import concourse.bacc as bacc
    from concourse.bass_utils import run_bass_kernel_spmd

    arrays = {f"in_{k}": v for k, v in pack({k: np.asarray(v) for k, v in inputs.items()}).items()}

    def program(per):
        nc = bacc.Bacc("TRN2", target_bir_lowering=False, num_devices=1)
        dram = {k[3:]: nc.dram_tensor(k, v.shape, F32, kind="ExternalInput").ap() for k, v in arrays.items()}
        out = nc.dram_tensor("out", (NTOK + CAP, C), F32, kind="ExternalOutput").ap()
        return nc, build(nc, dram, out, per)

    _, per = program({})
    nc, again = program(per)
    assert again == per
    result = run_bass_kernel_spmd(nc, [arrays], core_ids=[0])
    return result.results[0]["out"][:NTOK].reshape(B, TOK, C)
```

```python
from contextlib import ExitStack

import numpy as np

import concourse.bass as bass
from concourse import mybir

F32 = mybir.dt.float32
F16 = mybir.dt.float16
BF16 = mybir.dt.bfloat16
U32 = mybir.dt.uint32
ALU = mybir.AluOpType
ACT = mybir.ActivationFunctionType
AX = mybir.AxisListType

B, T, C = 16, 375, 128
TAPS = 31
TOK = T - TAPS + 1
J = 3
A = TOK // J
HEADS_T = 4
LK = HEADS_T * TAPS
TILES = 4
TT = 94
TW = TT + TAPS - 1
TP = TILES * TT
BROW = TW * HEADS_T
HID = 512
OC = HID // 128
H0, DH = 8, 64
E0, F0 = 8, 256
E1, F1, CAP = 64, 64, 256
NTOK = B * TOK
ROW = C + E1 + 1
SLOTS = E1 * CAP
CS = 2048.0
WS = 16.0
ALPHA = 1.6732632423543772848170429916717
LAMBDA = 1.0507009873554804934193349852946
EPS = 1e-5
UNITS = H0 * J
NE = 8

PASSES = 3
CHUNK = TAPS * PASSES
NHID = 2 * (E0 + 1)
spread = lambda n, k: [n * (i + 1) // k - n * i // k for i in range(k)]
PLAN = ([29, 13, 20] + spread(CHUNK - 62, 6) + spread(CHUNK, UNITS - 6)
        + [10, 8, 48, 6] + spread(CHUNK - 72, 3) + spread(CHUNK, NHID - 5) + [0, 0, 0])
POINTS = len(PLAN)
assert sum(PLAN) == OC * CHUNK
assert all((o + 1) * CHUNK in [sum(PLAN[:p]) for p in range(POINTS + 1)] for o in range(OC))
CHUNK_END = {next(p for p in range(POINTS) if sum(PLAN[:p + 1]) >= (o + 1) * CHUNK): o for o in range(OC)}

LATE = ["ln3", "q1", "k1", "v1", "kv", "g", "out1", "ln4", "gate1", "count"]
LATE_UNIT = {3: "ln3", 4: "q1", 5: "k1", 6: "v1", 7: "kv", 8: "g", 9: "out1", 13: "ln4", 14: "gate1", 22: "count"}
TOK_USE = ["lg"] + [x for t in range(TILES) for x in (f"bT{t}", f"y{t}")]

def unit_steps():
    out = []
    for s in range(UNITS + 2):
        if s < UNITS:
            out.append(("S", s))
        if 1 <= s <= UNITS:
            out.append(("T", s - 1))
    return out


W_USES = ([("ln", 1)] + [x for h in range(H0) for x in ([("q", h)] + ([("k", h // 2)] if h % 2 == 0 else []))]
          + [("v", j) for j in range(J)] + unit_steps()
          + [("oT", j) for j in range(J)] + [("out0", 0)]
          + [("ln", 2), ("gate0", 0)] + [("hid", n) for n in range(2 * E0)]
          + [("sg", 0), ("su", 0), ("sg", 1), ("su", 1)])
O_USES = [("O", h) for h in range(H0)] + [("Y", e) for e in range(E0 + 1)]
C_USES = [("conv", o) for o in range(OC)] + [("w2", 0)]


def place(uses, banks):
    seen = [0] * banks
    where = {}
    for n, u in enumerate(uses):
        b = n % banks
        seen[b] += 1
        where[u] = (b, seen[b])
    return where, seen


W_AT, W_PER = place(W_USES, 3)
O_AT, O_PER = place(O_USES, 2)
C_AT, C_PER = place(C_USES, 2)


FREED = {("out0", 0): ("ln_var_ready", 2), ("gate0", 0): ("gate_shifted", 1)}
FREED |= {("conv", o): ("zneg_ready", o + 1) for o in range(OC)}
FREED |= {("ln", n): ("xT_ready", n) for n in (1, 2)}
FREED |= {("q", h): ("q_ready", h + 1) for h in range(H0)}
FREED |= {("k", g): ("kv_ready", g + 1) for g in range(H0 // 2)}
FREED |= {("v", j): ("kv_ready", H0 // 2 + j + 1) for j in range(J)}
FREED |= {("S", u): ("p_ready", u + 1) for u in range(UNITS)}
FREED |= {("T", u): (("pt_ready_scalar", "pt_ready_vector")[u % 2], u // 2 + 1) for u in range(UNITS)}
FREED |= {("oT", j): ("oT_ready", j + 1) for j in range(J)}
FREED |= {("hid", n): ("hid_ready", n + 1) for n in range(2 * E0)}
FREED |= {(w, c): ("hid_ready", 2 * E0 + c + 1) for w in ("sg", "su") for c in range(2)}
FREED |= {("O", h): ("o_ready", h + 1) for h in range(H0)}
FREED |= {("Y", e): ("y_added", e + 1) for e in range(E0 + 1)}


def before_in_bank(uses, where):
    return {u: next((v for v in reversed(uses[:uses.index(u)]) if where[v][0] == where[u][0]), None) for u in uses}


W_PREV, O_PREV, C_PREV = (before_in_bank(u, w) for u, w in ((W_USES, W_AT), (O_USES, O_AT), (C_USES, C_AT)))


def build(nc, dram, out, per):
    ctx = ExitStack()
    seen, totals, named = {}, {}, {}

    def sb(name, shape, dt=F32):
        return ctx.enter_context(nc.sbuf_tensor(name, shape, dt))

    class Signal:

        def __init__(self, name, by=1, primed=0):
            self.h, self.name, self.by, self.primed = ctx.enter_context(nc.semaphore(name)), name, by, primed
            named[name] = self

        def up(self):
            seen[self.name] = seen.get(self.name, 0) + 1
            return self.by

        def at(self, b, k):
            return b * (per.get(self.name, 1) * self.by) + (k + self.primed) * self.by

    def batch_starts():
        seen.clear()

    def batch_ends():
        for name, n in seen.items():
            totals[name] = totals.get(name, 0) + n

    with ctx:
        ident = sb("ident", [128, 128])
        wlT = sb("wlT", [C, LK])
        tok_bl = sb("tok_bl", [TT, LK])
        tok_mask = sb("tok_mask", [TT, TILES, LK])
        tok_bias = sb("tok_bias", [C, 1])
        conv_b = sb("conv_b", [128, OC])
        w2T = sb("w2T", [128, OC, C])
        b2 = sb("b2", [A, C])
        wc_hi = sb("wc_hi", [C, OC, TAPS * 128], F16)
        wc_lo = sb("wc_lo", [C, OC, TAPS * 128], F16)
        gamma = sb("gamma", [C, 1])
        beta = sb("beta", [C, 1])
        WIDE = 2 * H0 * DH
        LAYER_W = H0 * DH * 2 + E0 * F0 + 2 * F0
        w_hl = sb("w_hl", [C, 2, WIDE + LAYER_W], F16)

        def weight(part, first, n):
            at = {"q": 0, "k": WIDE, "v": WIDE + H0 * DH, "w1": WIDE + 2 * H0 * DH,
                  "sg": WIDE + 2 * H0 * DH + E0 * F0, "su": WIDE + 2 * H0 * DH + E0 * F0 + F0}[part] + first
            return [w_hl[:, i, at:at + n] for i in range(2)]
        q_b = sb("q_b", [128, H0])
        uv = sb("uv", [128, H0])
        k_b = sb("k_b", [128, H0 // 2])
        v_b = sb("v_b", [128, 4])
        woT = sb("woT", [128, 4, C])
        bo = sb("bo", [A, C])
        gate0T = sb("gate0T", [C, E0])
        w2eT = sb("w2eT", [128, E0 * 2, C])
        sdT = sb("sdT", [128, 2, C])
        winT = sb("winT", [C, 3 * C])
        bin_col = sb("bin_col", [C, 3])
        bin_row = sb("bin_row", [A, 3 * C])
        kvmask = sb("kvmask", [C, C])
        wo1T = sb("wo1T", [C, C])
        bo1 = sb("bo1", [A, C])
        gate1T = sb("gate1T", [C, E1])
        gate1_b = sb("gate1_b", [A, E1])
        slot_base = sb("slot_base", [A, J, E1])
        tokens = sb("tokens", [A, J])
        tri = sb("tri", [A, 3, A], BF16)
        minus_half = sb("minus_half", [A, J])
        gate_dve = sb("gate_dve", [A, 1])

        x_win = sb("x_win", [TW, TILES, C])
        x_T = sb("x_T", [C, TP])
        lg = sb("lg", [TT, TILES, LK])
        lmax = sb("lmax", [TT, TILES * HEADS_T])
        lsum = sb("lsum", [TT, TILES * HEADS_T])
        band = sb("band", [TT, 2, BROW])
        selu = sb("selu", [128, OC, TOK])
        bandT = sb("bandT", [TW, HEADS_T * TT])
        y32 = sb("y32", [C, TP])
        y_hi = sb("y_hi", [C, TP], F16)
        y_lo = sb("y_lo", [C, TP], F16)
        z = sb("z", [128, TOK])
        zneg = sb("zneg", [128, TOK])
        h0 = sb("h0", [A, J * C])

        bn = [sb(f"bn{g}", [A, J, 6]) for g in range(2)]
        mv = [sb(f"mv{g}", [A, J, 2]) for g in range(2)]
        ve = [sb(f"ve{g}", [A, J]) for g in range(2)]
        rstd = [sb(f"rstd{g}", [A, J]) for g in range(2)]
        xh = [sb(f"xh{g}", [A, J, C]) for g in range(2)]
        xTs = [sb(f"xT{g}", [C, TOK]) for g in range(2)]
        xT = xTs[0]
        x_hl = sb("x_hl", [C, 2, TOK], F16)
        qv = sb("qv", [128, H0 * TOK + J * H0 * DH])
        Q = qv[:, 0:H0 * TOK].rearrange("p (h t) -> p h t", h=H0)
        V = qv[0:A, H0 * TOK:].rearrange("p (j n) -> p j n", j=J)
        HALF = TAPS * 64
        stage = [qv[:, 0:HALF], qv[:, HALF:2 * HALF]]
        w_stage = qv[:, 0:H0 * DH + LAYER_W]
        KP = sb("KP", [128, H0, TOK])
        nmax = sb("nmax", [A, 2])
        psums = sb("psums", [A, H0, J])
        prec = sb("prec", [A, H0, J])
        Pm = sb("Pm", [A, 2, TOK])
        PT = sb("PT", [A, 2, TOK])
        k1 = sb("k1", [A, 3 * C])
        v1 = sb("v1", [A, 3 * C])
        tri_f = Pm[:, 0, :].rearrange("p (m a) -> p m a", m=3)
        O = sb("O", [A, J, H0 * DH])
        hid = sb("hid", [128, 4, TOK])
        hidf = hid[:, :, :].rearrange("p j n -> p (j n)")
        OT = hidf.rearrange("p (j n) -> p j n", j=J)
        peT, wposT = hidf[:, 0:TOK], hidf[:, TOK:TOK + H0 * DH]
        h1 = sb("h1", [A, J * C])
        h2 = sb("h2", [A, J * C])
        h0b = h2
        h3 = sb("h3", [A, J * C])
        gl = sb("gl", [A, J * 8])
        gmx = sb("gmx", [A, J])
        best = sb("best", [A, J, 8])
        rest = sb("rest", [A, J * 8])
        chosen = sb("chosen", [A, J * 8])
        gsum = sb("gsum", [A, J])
        comb = sb("comb", [A, J * 8])
        th = sb("th", [128, 2, TOK])
        sgate = sb("sgate", [128, TOK])
        qT1 = sb("qT1", [C, J, A])
        kv = sb("kv", [C, C])
        G = sb("G", [C, C])
        rows = sb("rows", [A, J, ROW])
        sc = sb("sc", [A, J, E1])
        ss = sb("ss", [A, J * 8, 8])
        thi = sb("thi", [A, J * 8, 4])
        tlo = sb("tlo", [A, J * 8, 4])
        tmi = sb("tmi", [A, J * 8, 2])
        gpen = sb("gpen", [A, J * 8])
        top = sb("top", [A, J, 8])
        mr = sb("mr", [A, J, E1])
        sel = sb("sel", [A, J, E1], BF16)
        carry = sb("carry", [A, E1])
        pos = sb("pos", [A, J, E1])
        slot_i = sb("slot_i", [A, J * 8], U32)

        W = [ctx.enter_context(nc.psum_tensor(f"W{i}", [128, 512], F32)) for i in range(3)]
        L = ctx.enter_context(nc.psum_tensor("L", [128, 512], F32))
        Ob = [ctx.enter_context(nc.psum_tensor(f"Ob{i}", [128, 512], F32)) for i in range(2)]
        Cb = [ctx.enter_context(nc.psum_tensor(f"Cb{i}", [128, 512], F32)) for i in range(2)]

        s_tokw = ctx.enter_context(nc.semaphore("tok_weights_loaded"))
        s_curw = ctx.enter_context(nc.semaphore("layer_weights_loaded"))
        s_stage = [ctx.enter_context(nc.semaphore(f"conv_stage_loaded{i}")) for i in range(2)]
        s_zero = ctx.enter_context(nc.semaphore("band_zeroed"))
        s_held = ctx.enter_context(nc.semaphore("pool_held"))
        s_bandz = ctx.enter_context(nc.semaphore("band_dram_zeroed"))
        s_hi = ctx.enter_context(nc.semaphore("conv_hi_ready"))
        s_lo = ctx.enter_context(nc.semaphore("conv_lo_ready"))
        s_set = ctx.enter_context(nc.semaphore("setup_dve_step"))
        s_pos = ctx.enter_context(nc.semaphore("setup_pos_ready"))
        s_posu = ctx.enter_context(nc.semaphore("setup_pos_used"))
        s_setup = ctx.enter_context(nc.semaphore("setup_done"))
        s_split = ctx.enter_context(nc.semaphore("split_weights_loaded"))
        s_whi = ctx.enter_context(nc.semaphore("layer_hi_ready"))
        s_vb = ctx.enter_context(nc.semaphore("value_bias_projected"))

        w_full = [Signal(f"w_full{i}") for i in range(3)]
        late_full = Signal("late_full")
        tok_full = Signal("tok_full")
        o_full = [Signal(f"o_full{i}") for i in range(2)]
        c_full = [Signal(f"c_full{i}") for i in range(2)]
        x_loaded = Signal("x_loaded", 16)
        lg_sub = Signal("lg_shifted")
        lg_exp = Signal("lg_exp")
        taps_ready = Signal("tap_weights_ready")
        band_out = Signal("band_written", 16)
        band_in = [Signal(f"band_loaded{i}", 16) for i in range(2)]
        bandT_ready = Signal("bandT_ready")
        y_ready = Signal("y_ready")
        y_split = Signal("y_split")
        zneg_ready = Signal("zneg_ready")
        zexp_ready = Signal("zexp_ready")
        h0_ready = Signal("h0_ready")
        selu_ready = Signal("selu_ready")
        step_main = Signal("dve_step_main")
        step_late = Signal("dve_step_late")
        step_conv = Signal("dve_step_conv")
        step_tok = Signal("dve_step_tok")
        ln_var = [Signal("ln_var_ready"), Signal("late_var_ready")]
        ln_rstd = [Signal("ln_rstd_ready"), Signal("late_rstd_ready")]
        x_split = Signal("x_split")
        xh_ready = [Signal("xh_ready"), Signal("late_xh_ready")]
        xT_ready = [Signal("xT_ready"), Signal("late_xT_ready")]
        q_ready = Signal("q_ready")
        kvp_ready = Signal("kv_ready")
        nmax_ready = Signal("nmax_ready")
        p_ready = Signal("p_ready")
        pt_ready_a = Signal("pt_ready_scalar")
        pt_ready_d = Signal("pt_ready_vector")
        pv_done = Signal("pv_done")
        o_ready = Signal("o_ready")
        oT_ready = Signal("oT_ready")
        gexp_in = Signal("gate_shifted")
        gexp_out = Signal("gate_exp")
        th_ready = Signal("tanh_ready")
        hid_ready = Signal("hid_ready")
        qkv1_ready = Signal("qkv1_ready")
        kv_ready = Signal("kv_state_ready")
        g_ready = Signal("g_ready")
        y_added = Signal("y_added")
        gate1_exp = Signal("gate1_exp")
        counted = Signal("counts_added")
        h3_ready = Signal("h3_ready")
        h3_stored = Signal("h3_stored", 16, primed=1)
        sel_ready = Signal("sel_ready")
        rows_ready = Signal("rows_ready")
        rows_sent = Signal("rows_sent", 16, primed=1)

        def freed(use):
            at, prev = next((a, p) for a, p in ((W_AT, W_PREV), (O_AT, O_PREV), (C_AT, C_PREV)) if use in a)
            if not prev[use]:
                return at[use][0], None, 0
            name, k = FREED[prev[use]]
            return at[use][0], named[name], k

        def pt_used(eng, b, u):
            h, j = u // J, u % J
            if j == J - 1:
                bank, nth = O_AT[("O", h)]
                eng.wait_ge(o_full[bank].h, o_full[bank].at(b, nth))
            else:
                eng.wait_ge(pv_done.h, pv_done.at(b, 2 * h + j + 1))

        xpad, xTp = dram["xpad"], dram["xTp"]
        band_d = nc.dram_tensor("band_dram", (TILES, TT, BROW), F32, kind="Internal").ap()
        slots_d = nc.dram_tensor("slots_dram", (SLOTS, ROW), F32, kind="Internal").ap()
        band_skew = bass.AP(tensor=band_d.tensor, offset=0,
                            ap=[[BROW + HEADS_T, TT], [TT * BROW, TILES], [1, LK]])
        band_rows = band_d.rearrange("i t n -> t i n")

        tok_loads = [(ident, dram["ident"]), (wlT, dram["wlT"]), (tok_bl, dram["tok_bl"].partition_broadcast(TT)),
                     (tok_mask, dram["tok_mask"]), (tok_bias, dram["tok_bias"]), (conv_b, dram["conv_b"]),
                     (w2T, dram["w2T"]), (b2, dram["b2"].partition_broadcast(A))]
        layer_loads = [(beta, dram["beta"]),
                       (q_b[0:DH, :], dram["q_b"]), (q_b[DH:, :], dram["q_b"]),
                       (k_b, dram["k_b"]), (v_b, dram["v_b"]), (peT, dram["peT"]),
                       (wposT, dram["wposT"]), (woT, dram["woT"]), (bo, dram["bo"].partition_broadcast(A)),
                       (gate0T, dram["gate0T"]), (w2eT, dram["w2eT"]),
                       (sdT, dram["sdT"]), (winT, dram["winT"]),
                       (bin_row, dram["bin_row"].partition_broadcast(A)),
                       (bo1, dram["bo1"].partition_broadcast(A)),
                       (gate1_b, dram["gate1_b"].partition_broadcast(A)), (tri_f, dram["tri"])]

        prime_loads = [(slot_base, dram["slot_base"]), (uv, dram["uv"]), (tokens, dram["tokens"]),
                       (gamma, dram["gamma"]), (kvmask, dram["kvmask"]), (wo1T, dram["wo1T"]),
                       (gate1T, dram["gate1T"]), (bin_col, dram["bin_col"])]

        def ap(x):
            return x if isinstance(x, bass.AP) else x.ap()

        areas = [w[:, :, :].rearrange("p a b -> p (a b)").bitcast(F32) for w in (wc_hi, wc_lo)]
        used = [0, 0]

        def carve(area, n):
            used[area] += n
            assert used[area] <= OC * TAPS * 64
            return areas[area][:, used[area] - n:used[area]]

        e_rows = [carve(0, 2 * ROW).rearrange("p (c n) -> p c n", c=2) for _ in range(NE)]
        e_w13 = [carve(0, 2 * F1) for _ in range(NE)]
        e_w2 = [carve(0, C)[0:F1, :] for _ in range(NE)]
        e_y = [carve(1, 2 * C).rearrange("p (c n) -> p c n", c=2) for _ in range(NE)]
        e_idx = [carve(1, 2).bitcast(U32) for _ in range(NE)]
        e_xT = [carve(1, CAP) for _ in range(2)]
        e_th = [carve(1, CAP)[0:F1, :] for _ in range(4)]
        e_s = carve(1, CAP)[0:F1, :]
        e_h = [carve(1, CAP)[0:F1, :] for _ in range(4)]

        t_load = [Signal(f"t_loaded{i}", 16) for i in range(NE)]
        t_xps = [Signal(f"t_x_turned{i}") for i in range(NE)]
        t_xT = [Signal(f"t_xT_ready{i}") for i in range(NE)]
        t_hps = [Signal(f"t_h_full{i}") for i in range(NE)]
        t_th = [Signal(f"t_tanh{i}") for i in range(NE)]
        t_s = Signal("t_step")
        t_h = [Signal(f"t_h_ready{i}") for i in range(NE)]
        t_yps = [Signal(f"t_y_full{i}") for i in range(NE)]
        t_y = [Signal(f"t_y_ready{i}") for i in range(NE)]
        t_out = [Signal(f"t_added{i}", 16, primed=1) for i in range(NE)]
        t_sum = ctx.enter_context(nc.semaphore("sums_joined"))
        sum_rows = -(-(NTOK + CAP) // CAP) * CAP
        odd_d = nc.dram_tensor("odd_sum_dram", (sum_rows, C), F32, kind="Internal").ap()
        sums = [out, odd_d]

        q_twice = w_stage[:, 0:H0 * DH].rearrange("p (h d) -> p h d", h=H0).unsqueeze(2)\
            .to_broadcast((C, H0, 2, DH))

        up_bank = Ob + Cb

        block = ctx.enter_context(nc.Block())

        @block.sync
        def _(sp):
            for dst, src in tok_loads:
                sp.dma_start(ap(dst) if not isinstance(dst, bass.AP) else dst, src).then_inc(s_tokw, 16)

            def load_x(tb):
                if not (isinstance(tb, int) and tb == 0):
                    sp.wait_ge(tok_full.h, tok_full.at(tb - 1, len(TOK_USE)))
                src = bass.AP(tensor=xpad.tensor, offset=tb * ((TP + 30) * C),
                              ap=[[C, TW], [TT * C, TILES], [1, C]])
                sp.dma_start(x_win[:, :, :], src).then_inc(x_loaded.h, x_loaded.up())
                sp.dma_start(x_T[:, :], xTp[tb]).then_inc(x_loaded.h, x_loaded.up())

            def bands(tb, tiles=range(TILES)):
                if 0 in tiles:
                    sp.wait_ge(taps_ready.h, taps_ready.at(tb, 1))
                    sp.dma_start(band_skew, lg[:, :, :]).then_inc(band_out.h, band_out.up())
                    sp.wait_ge(band_out.h, band_out.at(tb, 1))
                for t in tiles:
                    if t >= 2:
                        sp.wait_ge(tok_full.h, tok_full.at(tb, 1 + TOK_USE.index(f"bT{t - 2}")))
                    sp.dma_start(band[:, t % 2, :], band_rows[:, t, :])\
                        .then_inc(band_in[t % 2].h, band_in[t % 2].up())

            batch_starts()
            load_x(0)
            for n in range(2 * OC):
                if n >= 2:
                    sp.wait_ge(s_lo, n - 1)
                sp.dma_start(stage[n % 2], dram["wc"][n // 2, :, (n % 2) * HALF:(n % 2 + 1) * HALF])\
                    .then_inc(s_stage[n % 2], 16)
                if n == 0:
                    sp.wait_ge(s_zero, 1)
                    for t in range(0, TILES, 2):
                        sp.dma_start(band_rows[:, t:t + 2, :], band[:, :, :]).then_inc(s_bandz, 16)
                    sp.wait_ge(s_bandz, 32)
                if n == 1:
                    bands(0, range(2))
                if n == 3:
                    bands(0, range(2, TILES))
            for tb in 1, 2:
                load_x(tb)
                if tb == 1:
                    sp.wait_ge(s_lo, 2 * OC)
                    at = 0
                    for name in "wqT", "wkT", "wvT", "w1T", "sgT", "suT":
                        n = dram[name].shape[1]
                        sp.dma_start(w_stage[:, at:at + n], dram[name]).then_inc(s_split, 16)
                        at += n
                bands(tb)
            with sp.Fori(1, B - 1) as it:
                batch_starts()
                load_x(it + 2)
                bands(it + 2)
                batch_ends()

            def load_expert(pr, i):
                e = pr * NE + i
                if not (isinstance(pr, int) and pr == 0):
                    sp.wait_ge(t_y[i].h, t_y[i].at(pr - 1, 1))
                sp.dma_start(e_rows[i], slots_e[e]).then_inc(t_load[i].h, t_load[i].up())
                sp.dma_start(e_w13[i][:, 0:F1], dram["w1e"][e]).then_inc(t_load[i].h, t_load[i].up())
                sp.dma_start(e_w13[i][:, F1:], dram["w3e"][e]).then_inc(t_load[i].h, t_load[i].up())
                sp.dma_start(e_w2[i], dram["w2e"][e]).then_inc(t_load[i].h, t_load[i].up())

            slots_e = slots_d.rearrange("(e c p) n -> e p c n", c=2, p=128)
            sp.wait_ge(rows_sent.h, rows_sent.at(B - 1, J * 8))
            batch_starts()
            for i in range(NE):
                load_expert(0, i)
            with sp.Fori(1, E1 // NE) as pr:
                batch_starts()
                for i in range(NE):
                    load_expert(pr, i)
                batch_ends()

        @block.gpsimd
        def _(pool):
            pool.memset(minus_half[:, :], -0.5)
            pool.memset(band[:, :, :], 0.0).then_inc(s_zero, 1)
            for sig, (dst, src) in zip(t_out, prime_loads):
                pool.dma_start(ap(dst), src).then_inc(sig.h, 16)
            pool.dma_start(out[NTOK:, :], dram["empty_slots"][:, 0:C]).then_inc(h3_stored.h, 16)
            pool.wait_ge(s_lo, 2 * OC)
            pool.dma_start(slots_d.rearrange("(e s) n -> e (s n)", e=E1),
                           dram["empty_slots"].rearrange("s n -> (s n)").unsqueeze(0).to_broadcast((E1, CAP * ROW)))\
                .then_inc(rows_sent.h, 16)
            pool.dma_start(odd_d.rearrange("(r s) c -> r (s c)", s=CAP),
                           dram["zero_rows"].unsqueeze(0).to_broadcast((sum_rows // CAP, CAP * C))).then_inc(t_sum, 16)

            def hold():
                pool.sem_inc(s_held, 1)

            def power(b, n, g):
                pool.wait_ge(ln_var[g].h, ln_var[g].at(b, n))
                pool.tensor_tensor(rstd[g][:, :], ve[g][:, :], minus_half[:, :], ALU.pow)\
                    .then_inc(ln_rstd[g].h, ln_rstd[g].up())

            def send(b):
                pool.wait_ge(h3_ready.h, h3_ready.at(b, 1))
                src = h3[:, :]
                dst = bass.AP(tensor=out.tensor, offset=b * (TOK * C), ap=[[J * C, A], [1, J * C]])
                pool.dma_start(dst, src).then_inc(h3_stored.h, h3_stored.up())
                pool.wait_ge(rows_ready.h, rows_ready.at(b, 1))
                hold()
                for j in range(J):
                    for k in range(8):
                        pool.indirect_dma_start(
                            out=slots_d, out_offset=bass.IndirectOffsetOnAxis(ap=slot_i[:, j * 8 + k:j * 8 + k + 1], axis=0),
                            in_=rows[:, j, :], in_offset=None, bounds_check=SLOTS - 1, oob_is_err=False).then_inc(rows_sent.h, rows_sent.up())

            def present(b, lb):
                power(b, 1, 0)
                if lb is not None:
                    power(lb, 1, 1)
                    power(lb, 2, 1)
                power(b, 2, 0)
                if lb is not None:
                    send(lb)

            present(0, None)
            pool.wait_ge(rows_sent.h, 16)
            pool.wait_ge(h3_stored.h, 16)
            with pool.Fori(1, B - 1) as it:
                batch_starts()
                present(it, it - 1)
                batch_ends()
            present(B - 1, B - 2)
            power(B - 1, 1, 1)
            power(B - 1, 2, 1)
            send(B - 1)
            pool.wait_ge(h3_stored.h, h3_stored.at(B - 1, 1))
            pool.wait_ge(rows_sent.h, rows_sent.at(B - 1, J * 8))
            pool.wait_ge(t_sum, 16)

            def add_rows(pr, i):
                pool.wait_ge(t_y[i].h, t_y[i].at(pr, 1))
                if i >= 2:
                    pool.wait_ge(t_out[i - 2].h, t_out[i - 2].at(pr, 2))
                else:
                    pool.wait_ge(t_out[i + NE - 2].h, t_out[i + NE - 2].at(pr, 0))
                hold()
                for c in range(2):
                    pool.indirect_dma_start(
                        out=sums[i % 2], out_offset=bass.IndirectOffsetOnAxis(ap=e_idx[i][:, c:c + 1], axis=0),
                        in_=e_y[i][:, c, :], in_offset=None, bounds_check=NTOK + CAP - 1, oob_is_err=True,
                        compute_op=ALU.add).then_inc(t_out[i].h, t_out[i].up())

            with pool.Fori(0, E1 // NE) as pr:
                batch_starts()
                for i in range(NE):
                    add_rows(pr, i)
                batch_ends()
            for i in range(NE):
                pool.wait_ge(t_out[i].h, t_out[i].at(E1 // NE - 1, 2))
            wide = 2048
            flat = lambda x: x[0:NTOK, :].rearrange("t c -> (t c)").rearrange("(r n) -> r n", n=wide)
            pool.dma_start(flat(out), flat(odd_d), accum_op=ALU.add, max_dma_last_dim=4 * wide).then_inc(t_sum, 16)
            pool.wait_ge(t_sum, 32)

        @block.tensor
        def _(pe):
            def mm(o, l, r, start=True, stop=True):
                return pe.matmul(o, l, r, start=start, stop=stop)

            def tok_logits(tb):
                if not (isinstance(tb, int) and tb == 0):
                    pe.wait_ge(y_ready.h, y_ready.at(tb - 1, TILES))
                pe.wait_ge(x_loaded.h, x_loaded.at(tb, 2))
                for t in range(TILES):
                    last = mm(L[0:TT, t * LK:(t + 1) * LK], x_T[:, t * TT:(t + 1) * TT], wlT[:, :])
                last.then_inc(tok_full.h, tok_full.up())

            def tok_mix(tb, n, lb):
                t = n // 2
                if n % 2 == 0:
                    pe.wait_ge(band_in[t % 2].h, band_in[t % 2].at(tb, t // 2 + 1))
                    if t >= 1:
                        pe.wait_ge(y_ready.h, y_ready.at(tb, t))
                    elif lb is not None:
                        pe.wait_ge(counted.h, counted.at(lb, 1))
                    else:
                        pe.wait_ge(lg_sub.h, lg_sub.at(tb, 1))
                    for h in range(HEADS_T):
                        last = pe.transpose(L[0:TW, h * TT:(h + 1) * TT], band[:, t % 2, h::HEADS_T], ident[0:TT, 0:TT])
                else:
                    pe.wait_ge(bandT_ready.h, bandT_ready.at(tb, t + 1))
                    for h in range(HEADS_T):
                        last = mm(L[32 * h:32 * h + 32, 0:TT], x_win[:, t, 32 * h:32 * h + 32],
                                  bandT[:, h * TT:(h + 1) * TT])
                last.then_inc(tok_full.h, tok_full.up())

            def conv(nb, p):
                if nb is None:
                    return
                for g in range(sum(PLAN[:p]), sum(PLAN[:p + 1])):
                    o, m = g // CHUNK, g % CHUNK
                    if m == 0:
                        if o == 0:
                            pe.wait_ge(y_split.h, y_split.at(nb, 1))
                            if not (isinstance(nb, int) and nb == 0):
                                pe.wait_ge(h0_ready.h, h0_ready.at(nb - 1, 1))
                        i, was, nth = freed(("conv", o))
                        if was:
                            pe.wait_ge(was.h, was.at(nb, nth))
                        if isinstance(nb, int) and nb == 0:
                            pe.wait_ge(s_lo, 2 * o + 2)
                    k, what = m // PASSES, m % PASSES
                    w = (wc_hi, wc_hi, wc_lo)[what][:, o, k * 128:(k + 1) * 128]
                    y = (y_hi, y_lo, y_hi)[what][:, k:k + TOK]
                    last = mm(Cb[o % 2][:, 0:TOK], w, y, start=(m == 0), stop=(m == CHUNK - 1))
                    if m == CHUNK - 1:
                        last.then_inc(c_full[o % 2].h, c_full[o % 2].up())

            def tok_out(nb):
                i, was, nth = freed(("w2", 0))
                if was:
                    pe.wait_ge(was.h, was.at(nb, nth))
                pe.wait_ge(selu_ready.h, selu_ready.at(nb, OC))
                for j in range(J):
                    for o in range(OC):
                        last = mm(Cb[i][0:A, j * C:(j + 1) * C], selu[:, o, j::J], w2T[:, o, :],
                                  start=(o == 0), stop=(o == OC - 1))
                last.then_inc(c_full[i].h, c_full[i].up())

            def mm3(o, l, r):
                mm(o, l[0], r[0], start=True, stop=False)
                mm(o, l[0], r[1], start=False, stop=False)
                return mm(o, l[1], r[0], start=False, stop=True)

            x_halves = [x_hl[:, i, :] for i in range(2)]

            def turn(b, n):
                pe.wait_ge(xh_ready[0].h, xh_ready[0].at(b, n))
                i, was, nth = freed(("ln", n))
                if was:
                    pe.wait_ge(was.h, was.at(b, nth))
                for j in range(J):
                    last = pe.transpose(W[i][:, j * A:(j + 1) * A], xh[0][:, j, :], ident[0:A, 0:A])
                last.then_inc(w_full[i].h, w_full[i].up())

            def gate(w, width, wt, x):
                for j in range(J):
                    last = mm(w[0:A, j * width:(j + 1) * width], x[:, j * A:(j + 1) * A], wt[:, :])
                return last

            def late(b, unit, tb):
                if b is None or unit not in LATE_UNIT:
                    return
                use, x = LATE_UNIT[unit], xTs[1]
                if use == "ln3":
                    if tb is not None:
                        pe.wait_ge(lg_sub.h, lg_sub.at(tb, 1))
                    elif isinstance(b, int) and b == B - 1:
                        pe.wait_ge(counted.h, counted.at(b - 1, 1))
                    else:
                        pe.wait_ge(y_ready.h, y_ready.at(B, TILES))
                    pe.wait_ge(xh_ready[1].h, xh_ready[1].at(b, 1))
                    for j in range(J):
                        last = pe.transpose(L[:, j * A:(j + 1) * A], xh[1][:, j, :], ident[0:A, 0:A])
                elif use == "q1":
                    pe.wait_ge(xT_ready[1].h, xT_ready[1].at(b, 1))
                    for j in range(J):
                        last = mm(L[:, j * A:(j + 1) * A], winT[:, j * C:(j + 1) * C], x[:, 0:A])
                elif use == "k1":
                    pe.wait_ge(qkv1_ready.h, qkv1_ready.at(b, 1))
                    last = mm(L[0:A, 0:3 * C], x[:, A:2 * A], winT[:, :])
                elif use == "v1":
                    pe.wait_ge(qkv1_ready.h, qkv1_ready.at(b, 2))
                    last = mm(L[0:A, 0:3 * C], x[:, 2 * A:3 * A], winT[:, :])
                elif use == "kv":
                    pe.wait_ge(qkv1_ready.h, qkv1_ready.at(b, 3))
                    for j in range(J):
                        last = mm(L[:, 0:C], v1[:, j * C:(j + 1) * C], k1[:, j * C:(j + 1) * C],
                                  start=(j == 0), stop=(j == J - 1))
                elif use == "g":
                    pe.wait_ge(kv_ready.h, kv_ready.at(b, 1))
                    last = mm(L[:, 0:C], kv[:, :], wo1T[:, :])
                elif use == "out1":
                    pe.wait_ge(g_ready.h, g_ready.at(b, 1))
                    for j in range(J):
                        last = mm(L[0:A, j * C:(j + 1) * C], qT1[:, j, :], G[:, :])
                elif use == "ln4":
                    pe.wait_ge(xh_ready[1].h, xh_ready[1].at(b, 2))
                    for j in range(J):
                        last = pe.transpose(L[:, j * A:(j + 1) * A], rows[:, j, 0:C], ident[0:A, 0:A])
                elif use == "gate1":
                    pe.wait_ge(xT_ready[1].h, xT_ready[1].at(b, 2))
                    last = gate(L, E1, gate1T, x)
                else:
                    pe.wait_ge(sel_ready.h, sel_ready.at(b, 1))
                    for j in range(J + 1):
                        for q in range(J):
                            m = 2 if j == J else 1 if q < j else 0
                            last = mm(L[0:A, j * E1:(j + 1) * E1], tri[:, m, :], sel[:, q, :],
                                      start=(q == 0), stop=(q == J - 1))
                last.then_inc(late_full.h, late_full.up())

            def step(b, use, what):
                i, was, nth = freed(use)
                if was:
                    pe.wait_ge(was.h, was.at(b, nth))
                what(W[i]).then_inc(w_full[i].h, w_full[i].up())

            def present(b, nb, tb, lb):
                if tb is not None:
                    tok_logits(tb)
                conv(nb, 0)
                turn(b, 1)
                conv(nb, 1)
                pe.wait_ge(x_split.h, x_split.at(b, 1))
                for h in range(H0):
                    step(b, ("q", h), lambda w: mm3(w[:, 0:TOK], weight("q", h * 128, 128), x_halves))
                    if h % 2 == 0:
                        g = h // 2
                        step(b, ("k", g), lambda w: mm3(w[:, 0:TOK], weight("k", g * 128, 128), x_halves))
                for j in range(J):
                    step(b, ("v", j), lambda w: mm3(w[0:A, :], [x[:, j * A:(j + 1) * A] for x in x_halves],
                                                    weight("v", 0, H0 * DH)))
                conv(nb, 2)
                pe.wait_ge(q_ready.h, q_ready.at(b, H0))
                pe.wait_ge(kvp_ready.h, kvp_ready.at(b, H0 // 2 + J))

                def turn_p(w, u):
                    for i in range(J):
                        last = pe.transpose(w[0:A, i * A:(i + 1) * A], Pm[:, u % 2, i * A:(i + 1) * A], ident[0:A, 0:A])
                    return last

                for s in range(UNITS + 2):
                    if s < UNITS:
                        h, j = s // J, s % J
                        step(b, ("S", s), lambda w: mm(w[0:A, 0:TOK], Q[:, h, j * A:(j + 1) * A], KP[:, h, :]))
                        conv(nb, 3 + s)
                        late(lb, s, tb)
                    if 1 <= s <= UNITS:
                        u = s - 1
                        pe.wait_ge(p_ready.h, p_ready.at(b, u + 1))
                        step(b, ("T", u), lambda w: turn_p(w, u))
                    if s >= 2:
                        u = s - 2
                        h, j = u // J, u % J
                        if j == 0:
                            o, was, nth = freed(("O", h))
                            if was:
                                pe.wait_ge(was.h, was.at(b, nth))
                        pe.wait_ge((pt_ready_a, pt_ready_d)[u % 2].h, (pt_ready_a, pt_ready_d)[u % 2].at(b, u // 2 + 1))
                        for i in range(J):
                            last = mm(Ob[o][0:A, j * DH:(j + 1) * DH], PT[:, u % 2, i * A:(i + 1) * A],
                                      V[:, i, h * DH:(h + 1) * DH], start=(i == 0), stop=(i == J - 1))
                        pv = o_full[o] if j == J - 1 else pv_done
                        last.then_inc(pv.h, pv.up())

                p = 3 + UNITS
                conv(nb, p)
                pe.wait_ge(o_ready.h, o_ready.at(b, H0))
                for j in range(J):
                    i, was, nth = freed(("oT", j))
                    if was:
                        pe.wait_ge(was.h, was.at(b, nth))
                    for c in range(4):
                        last = pe.transpose(W[i][:, c * A:(c + 1) * A], O[:, j, c * 128:(c + 1) * 128], ident[0:A, 0:A])
                    last.then_inc(w_full[i].h, w_full[i].up())
                conv(nb, p + 1)
                i, was, nth = freed(("out0", 0))
                if was:
                    pe.wait_ge(was.h, was.at(b, nth))
                for j in range(J):
                    pe.wait_ge(oT_ready.h, oT_ready.at(b, j + 1))
                    for c in range(4):
                        last = mm(W[i][0:A, j * C:(j + 1) * C], OT[:, j, c * A:(c + 1) * A], woT[:, c, :],
                                  start=(c == 0), stop=(c == 3))
                last.then_inc(w_full[i].h, w_full[i].up())

                conv(nb, p + 2)
                turn(b, 2)
                conv(nb, p + 3)
                p += 4
                pe.wait_ge(xT_ready[0].h, xT_ready[0].at(b, 2))
                step(b, ("gate0", 0), lambda w: gate(w, E0, gate0T, xT))
                pe.wait_ge(x_split.h, x_split.at(b, 2))

                def mix(e):
                    pe.wait_ge(hid_ready.h, hid_ready.at(b, 2 * e + 2))
                    o, was, nth = freed(("Y", e))
                    if was:
                        pe.wait_ge(was.h, was.at(b, nth))
                    for j in range(J):
                        for c in range(2):
                            wt = w2eT[:, 2 * e + c, :] if e < E0 else sdT[:, c, :]
                            last = mm(Ob[o][0:A, j * C:(j + 1) * C], hid[:, 2 * (e % 2) + c, j * A:(j + 1) * A], wt,
                                      start=(c == 0), stop=(c == 1))
                    last.then_inc(o_full[o].h, o_full[o].up())

                for e in range(E0 + 1):
                    for c in range(2):
                        if e < E0:
                            n = 2 * e + c
                            step(b, ("hid", n), lambda w: mm3(w[:, 0:TOK], weight("w1", n * 128, 128), x_halves))
                        else:
                            step(b, ("sg", c), lambda w: mm3(w[:, 0:TOK], weight("sg", c * 128, 128), x_halves))
                            step(b, ("su", c), lambda w: mm3(w[:, 0:TOK], weight("su", c * 128, 128), x_halves))
                        n = 2 * e + c
                        if tb is not None and n % 2 == 0 and n < 4 * TILES:
                            tok_mix(tb, n // 2, lb)
                        conv(nb, p)
                        p += 1
                        if e >= 1 and c == (0 if e == E0 else 1):
                            mix(e - 1)
                conv(nb, p)
                p += 1
                assert p == POINTS
                if nb is not None:
                    tok_out(nb)
                mix(E0)

            pe.wait_ge(s_tokw, 16 * len(tok_loads))
            batch_starts()
            tok_logits(0)
            for n in range(2 * TILES):
                tok_mix(0, n, None)
            pe.wait_ge(s_curw, 16 * len(layer_loads))
            for g in range(H0 // 2):
                if g >= 2:
                    pe.wait_ge(s_posu, g - 1)
                mm(W[g % 2][:, 0:TOK], wposT[:, g * 128:(g + 1) * 128], peT).then_inc(s_pos, 1)
            for c in range(4):
                last = mm(W[2][0:A, 0:C], v_b[:, c:c + 1].to_broadcast((128, A)), woT[:, c, :],
                          start=(c == 0), stop=(c == 3))
            last.then_inc(s_vb, 1)
            tok_logits(1)
            for p in range(POINTS):
                conv(0, p)
                if p >= 3 + UNITS and p < 3 + UNITS + 2 * TILES:
                    tok_mix(1, p - 3 - UNITS, None)
            tok_out(0)
            pe.wait_ge(s_setup, 1)
            present(0, 1, 2, None)
            with pe.Fori(1, B - 1) as it:
                batch_starts()
                present(it, it + 1, it + 2, it - 1)
                batch_ends()
            present(B - 1, None, None, B - 2)
            for s in range(UNITS):
                late(B - 1, s, None)

            turn_bank, y_bank = W[0:2], [W[2], L]

            def expert_in(pr, i):
                pe.wait_ge(t_load[i].h, t_load[i].at(pr, 4))
                for c in range(2):
                    last = pe.transpose(turn_bank[i % 2][:, c * 128:(c + 1) * 128], e_rows[i][:, c, 0:C], ident[:, :])
                last.then_inc(t_xps[i].h, t_xps[i].up())

            def expert_up(pr, i):
                pe.wait_ge(t_xT[i].h, t_xT[i].at(pr, 1))
                if i >= 4:
                    pe.wait_ge(t_h[i - 4].h, t_h[i - 4].at(pr, 1))
                mm(up_bank[i % 4][0:F1, 0:CAP], e_w13[i][:, 0:F1], e_xT[i % 2])
                mm(up_bank[i % 4][0:F1, CAP:], e_w13[i][:, F1:], e_xT[i % 2]).then_inc(t_hps[i].h, t_hps[i].up())

            def expert_down(pr, i):
                pe.wait_ge(t_h[i].h, t_h[i].at(pr, 1))
                if i >= 2:
                    pe.wait_ge(t_y[i - 2].h, t_y[i - 2].at(pr, 1))
                for c in range(2):
                    last = mm(y_bank[i % 2][:, c * C:(c + 1) * C], e_h[i % 4][:, c * 128:(c + 1) * 128], e_w2[i])
                last.then_inc(t_yps[i].h, t_yps[i].up())

            with pe.Fori(0, E1 // NE) as pr:
                batch_starts()
                for i in range(0, NE + 4, 2):
                    for k in i, i + 1:
                        if k < NE:
                            expert_in(pr, k)
                    for k in i - 4, i - 3:
                        if k >= 0:
                            expert_down(pr, k)
                    for k in i, i + 1:
                        if k < NE:
                            expert_up(pr, k)
                batch_ends()

        @block.scalar
        def _(act):
            for dst, src in layer_loads:
                act.dma_start(ap(dst) if not isinstance(dst, bass.AP) else dst, src).then_inc(s_curw, 16)

            def tok_exp(nb):
                act.wait_ge(lg_sub.h, lg_sub.at(nb, 1))
                act.activation(lg[:, :, :], lg[:, :, :], ACT.Exp).then_inc(lg_exp.h, lg_exp.up())

            def tok_band(tb, n):
                act.wait_ge(tok_full.h, tok_full.at(tb, 2 + n))
                t = n // 2
                if n % 2 == 0:
                    act.activation(bandT[:, :], L[0:TW, 0:HEADS_T * TT], ACT.Copy)\
                        .then_inc(bandT_ready.h, bandT_ready.up())
                else:
                    act.activation(y32[:, t * TT:(t + 1) * TT], L[:, 0:TT], ACT.Identity, bias=tok_bias[:, 0:1])\
                        .then_inc(y_ready.h, y_ready.up())

            def conv_out(nb, p):
                if nb is None or p not in CHUNK_END:
                    return
                o = CHUNK_END[p]
                act.wait_ge(zneg_ready.h, zneg_ready.at(nb, o + 1))
                act.activation(zneg[:, :], zneg[:, :], ACT.Exp).then_inc(zexp_ready.h, zexp_ready.up())

            def late(b, unit):
                if b is None or LATE_UNIT.get(unit) != "gate1":
                    return
                act.wait_ge(late_full.h, late_full.at(b, 1 + LATE.index("gate1")))
                act.activation(sc[:, :, :], L[0:A, 0:J * E1], ACT.Exp, scale=-1.0).then_inc(gate1_exp.h, gate1_exp.up())

            def tanh_in(b, use, n):
                i, nth = W_AT[use]
                act.wait_ge(w_full[i].h, w_full[i].at(b, nth))
                if n >= 2:
                    act.wait_ge(hid_ready.h, hid_ready.at(b, n - 1))
                act.activation(th[:, n % 2, :], W[i][:, 0:TOK], ACT.Tanh, scale=0.5 / WS).then_inc(th_ready.h, th_ready.up())

            def present(b, nb, tb, lb):
                for h in range(H0):
                    i, nth = W_AT[("q", h)]
                    act.wait_ge(w_full[i].h, w_full[i].at(b, nth))
                    act.activation(Q[:, h, :], W[i][:, 0:TOK], ACT.Identity, bias=q_b[:, h:h + 1],
                                              scale=DH ** -0.5 / WS).then_inc(q_ready.h, q_ready.up())
                if tb is not None:
                    tok_exp(tb)
                for s in range(UNITS + 1):
                    if s < UNITS:
                        i, nth = W_AT[("S", s)]
                        act.wait_ge(w_full[i].h, w_full[i].at(b, nth))
                        if s >= 2:
                            bank, nth = W_AT[("T", s - 2)]
                            act.wait_ge(w_full[bank].h, w_full[bank].at(b, nth))
                        act.wait_ge(nmax_ready.h, nmax_ready.at(b, s + 1))
                        act.activation(Pm[:, s % 2, :], W[i][0:A, 0:TOK], ACT.Exp,
                                                  bias=nmax[:, s % 2:s % 2 + 1],
                                                  accum_out=psums[:, s // J, s % J:s % J + 1]).then_inc(p_ready.h, p_ready.up())
                        late(lb, s)
                        conv_out(nb, 3 + s)
                    if s >= 1 and (s - 1) % 2 == 0:
                        u = s - 1
                        i, nth = W_AT[("T", u)]
                        act.wait_ge(w_full[i].h, w_full[i].at(b, nth))
                        if u >= 2:
                            pt_used(act, b, u - 2)
                        act.activation(PT[:, 0, :], W[i][0:A, 0:TOK], ACT.Copy).then_inc(pt_ready_a.h, pt_ready_a.up())
                for j in range(J):
                    i, nth = W_AT[("oT", j)]
                    act.wait_ge(w_full[i].h, w_full[i].at(b, nth))
                    act.activation(OT[:, j, :], W[i][:, 0:4 * A], ACT.Copy).then_inc(oT_ready.h, oT_ready.up())
                p = 3 + UNITS + 4
                for n in range(NHID):
                    tanh_in(b, ("hid", n) if n < 2 * E0 else ("sg", n - 2 * E0), n)
                    if n == 1:
                        act.wait_ge(gexp_in.h, gexp_in.at(b, 1))
                        act.activation(gl[:, :], gl[:, :], ACT.Exp).then_inc(gexp_out.h, gexp_out.up())
                    if tb is not None and n % 2 == 0 and n < 4 * TILES:
                        tok_band(tb, n // 2)
                    conv_out(nb, p)
                    p += 1

            act.wait_ge(s_tokw, 16 * len(tok_loads))
            batch_starts()
            tok_exp(0)
            for n in range(2 * OC):
                act.wait_ge(s_stage[n % 2], 16 * (n // 2 + 1))
                act.activation(wc_hi[:, n // 2, (n % 2) * HALF:(n % 2 + 1) * HALF], stage[n % 2], ACT.Copy, scale=CS)\
                    .then_inc(s_hi, 1)
                if n == 3:
                    for m in range(2 * TILES):
                        tok_band(0, m)
            act.wait_ge(s_split, 16 * 6)
            act.activation(w_hl[:, 0, 0:WIDE].rearrange("p (h r d) -> p h r d", h=H0, r=2), q_twice, ACT.Copy, scale=WS)
            act.activation(w_hl[:, 0, WIDE:], w_stage[:, H0 * DH:], ACT.Copy, scale=WS).then_inc(s_whi, 1)
            tok_exp(1)
            for p in range(POINTS):
                conv_out(0, p)
                if p >= 3 + UNITS and p < 3 + UNITS + 2 * TILES:
                    tok_band(1, p - 3 - UNITS)
            act.wait_ge(s_setup, 1)
            present(0, 1, 2, None)
            with act.Fori(1, B - 1) as it:
                batch_starts()
                present(it, it + 1, it + 2, it - 1)
                batch_ends()
            present(B - 1, None, None, B - 2)
            for s in range(UNITS):
                late(B - 1, s)

            def expert_xT(pr, i):
                act.wait_ge(t_xps[i].h, t_xps[i].at(pr, 1))
                act.activation(e_xT[i % 2], W[i % 2][:, 0:CAP], ACT.Copy).then_inc(t_xT[i].h, t_xT[i].up())

            def expert_tanh(pr, i):
                act.wait_ge(t_hps[i].h, t_hps[i].at(pr, 1))
                act.activation(e_th[i % 4], up_bank[i % 4][0:F1, 0:CAP], ACT.Tanh, scale=0.5).then_inc(t_th[i].h, t_th[i].up())

            with act.Fori(0, E1 // NE) as pr:
                batch_starts()
                for i in range(0, NE, 2):
                    expert_xT(pr, i)
                    expert_xT(pr, i + 1)
                    expert_tanh(pr, i)
                    expert_tanh(pr, i + 1)
                batch_ends()

        @block.vector
        def _(dve):
            chain = [step_main, 0]
            steps = {}

            def turn_to(sig, b, first=False):
                chain[:] = [sig, b]
                if first:
                    steps[sig.name] = 0

            def link(ins):
                sig, b = chain
                ins.then_inc(sig.h, sig.up())
                steps[sig.name] += 1
                dve.wait_ge(sig.h, sig.at(b, steps[sig.name]))

            def tok_softmax(nb):
                turn_to(step_tok, nb, first=True)
                dve.wait_ge(tok_full.h, tok_full.at(nb, 1))
                if not (isinstance(nb, int) and nb == 0):
                    dve.wait_ge(band_out.h, band_out.at(nb, 0))
                lgf = lg[:, :, :].rearrange("p i n -> p (i n)")
                ins = dve.tensor_tensor(lg[:, :, :], L[0:TT, 0:TILES * LK].rearrange("p (i n) -> p i n", i=TILES),
                                        tok_mask[:, :, :], ALU.add)
                link(ins)
                by_head = lg[:, :, :].rearrange("p i (k h) -> p i h k", h=HEADS_T)
                flat = lambda x: x[:, :].rearrange("p (i h) -> p i h", h=HEADS_T)
                spread = lambda x: flat(x).unsqueeze(3).to_broadcast((TT, TILES, HEADS_T, TAPS))
                link(dve.tensor_reduce(flat(lmax), by_head, AX.X, ALU.max))
                dve.tensor_tensor(by_head, by_head, spread(lmax), ALU.subtract).then_inc(lg_sub.h, lg_sub.up())
                dve.wait_ge(lg_exp.h, lg_exp.at(nb, 1))
                link(dve.tensor_reduce(flat(lsum), by_head, AX.X, ALU.add))
                link(dve.reciprocal(lsum[:, :], lsum[:, :]))
                dve.tensor_tensor(by_head, by_head, spread(lsum), ALU.mult).then_inc(taps_ready.h, taps_ready.up())

            def tok_split(nb):
                turn_to(step_tok, nb)
                dve.wait_ge(y_ready.h, y_ready.at(nb, TILES))
                link(dve.tensor_copy(y_hi[:, :], y32[:, :]))
                dve.tensor_tensor(y_lo[:, :], y32[:, :], y_hi[:, :], ALU.subtract).then_inc(y_split.h, y_split.up())

            def conv_out(nb, p):
                if nb is None or p not in CHUNK_END:
                    return
                saved = list(chain)
                o = CHUNK_END[p]
                turn_to(step_conv, nb, first=(o == 0))
                i, nth = C_AT[("conv", o)]
                dve.wait_ge(c_full[i].h, c_full[i].at(nb, nth))
                link(dve.tensor_scalar(z[:, :], Cb[i][:, 0:TOK], 1 / CS, conv_b[:, o:o + 1], ALU.mult, ALU.add))
                dve.tensor_scalar(zneg[:, :], z[:, :], 0.0, None, ALU.min).then_inc(zneg_ready.h, zneg_ready.up())
                dve.wait_ge(zneg_ready.h, zneg_ready.at(nb, o + 1))
                link(dve.tensor_scalar(z[:, :], z[:, :], 0.0, ALPHA, ALU.max, ALU.subtract))
                dve.wait_ge(zexp_ready.h, zexp_ready.at(nb, o + 1))
                ins = dve.scalar_tensor_tensor(selu[:, o, :], zneg[:, :], ALPHA, z[:, :], ALU.mult, ALU.add)
                ins.then_inc(selu_ready.h, selu_ready.up())
                dve.wait_ge(selu_ready.h, selu_ready.at(nb, o + 1))
                chain[:] = saved

            def tok_out(nb):
                i, nth = C_AT[("w2", 0)]
                dve.wait_ge(c_full[i].h, c_full[i].at(nb, nth))
                h = h0[:, :].rearrange("p (j c) -> p j c", j=J)
                dve.scalar_tensor_tensor(h, Cb[i][0:A, 0:J * C].rearrange("p (j c) -> p j c", j=J), LAMBDA,
                                         b2[:, :].unsqueeze(1).to_broadcast((A, J, C)), ALU.mult, ALU.add)\
                    .then_inc(h0_ready.h, h0_ready.up())
                dve.wait_ge(h0_ready.h, h0_ready.at(nb, 1))

            def hold():
                dve.memset(gate_dve[:, :], 0.0)

            def norm_sums(src, g):
                for j in range(J):
                    ins = dve.bn_stats(bn[g][:, j, :], src[:, j * C:(j + 1) * C])
                link(ins)
                hold()

            def norm_var(n, g):
                for j in range(J):
                    ins = dve.bn_aggr(mv[g][:, j, :], bn[g][:, j, :])
                link(ins)
                if n == 1 and g == 0:
                    ins = dve.tensor_scalar(ve[g][:, :], mv[g][:, :, 1], 1.0 + EPS, EPS * EPS, ALU.mult, ALU.add)
                else:
                    ins = dve.tensor_scalar(ve[g][:, :], mv[g][:, :, 1], EPS, None, ALU.add)
                ins.then_inc(ln_var[g].h, ln_var[g].up())

            def norm_rows(b, n, src, g):
                dve.wait_ge(ln_rstd[g].h, ln_rstd[g].at(b, n))
                for j in range(J):
                    dst = rows[:, j, 0:C] if (n, g) == (2, 1) else xh[g][:, j, :]
                    ins = dve.tensor_scalar(dst, src[:, j * C:(j + 1) * C], mv[g][:, j, 0:1], rstd[g][:, j:j + 1],
                                            ALU.subtract, ALU.mult)
                ins.then_inc(xh_ready[g].h, xh_ready[g].up())

            def norm(b, n, src):
                norm_sums(src, 0)
                norm_var(n, 0)
                norm_rows(b, n, src, 0)
                i, nth = W_AT[("ln", n)]
                dve.wait_ge(w_full[i].h, w_full[i].at(b, nth))
                if n == 1:
                    ins = dve.tensor_scalar(xT[:, :], W[i][:, 0:TOK], gamma[:, 0:1], beta[:, 0:1], ALU.mult, ALU.add)
                else:
                    ins = dve.tensor_copy(xT[:, :], W[i][:, 0:TOK])
                ins.then_inc(xT_ready[0].h, xT_ready[0].up())
                dve.wait_ge(xT_ready[0].h, xT_ready[0].at(b, n))
                link(dve.tensor_copy(x_hl[:, 0, :], xT[:, :]))
                dve.tensor_tensor(x_hl[:, 1, :], xT[:, :], x_hl[:, 0, :], ALU.subtract)\
                    .then_inc(x_split.h, x_split.up())

            def choose(score, n):
                hold()
                for j in range(J):
                    ins = dve.max(best[:, j, :], score[:, j * 8:(j + 1) * 8])
                link(ins)
                link(dve.memset(best[:, :, n:], -3e30))
                hold()
                for j in range(J):
                    ins = dve.match_replace(rest[:, j * 8:(j + 1) * 8], best[:, j, :], score[:, j * 8:(j + 1) * 8], -3e30)
                link(ins)
                link(dve.tensor_tensor(chosen[:, :], rest[:, :], score, ALU.not_equal))

            def late(b, unit):
                if b is None:
                    return
                saved = list(chain)
                turn_to(step_late, b, first=(unit == 0))
                use = LATE_UNIT.get(unit)
                if use:
                    dve.wait_ge(late_full.h, late_full.at(b, 1 + LATE.index(use)))
                ss3 = ss[:, :, :].rearrange("p (j g) q -> p j (g q)", j=J)
                if unit == 0:
                    norm_sums(h2, 1)
                elif unit == 1:
                    norm_var(1, 1)
                elif unit == 2:
                    norm_rows(b, 1, h2, 1)
                elif use == "ln3":
                    dve.tensor_copy(xTs[1][:, :].rearrange("c (a j) -> c j a", j=J),
                                    L[:, 0:TOK].rearrange("c (j a) -> c j a", j=J))\
                        .then_inc(xT_ready[1].h, xT_ready[1].up())
                elif use == "q1":
                    dve.tensor_tensor(qT1[:, :, :], L[:, 0:TOK].rearrange("c (j a) -> c j a", j=J),
                                      bin_col[:, :].unsqueeze(2).to_broadcast((C, J, A)), ALU.add)\
                        .then_inc(qkv1_ready.h, qkv1_ready.up())
                elif use in ("k1", "v1"):
                    dst = k1 if use == "k1" else v1
                    dve.tensor_tensor(dst[:, :], L[0:A, 0:3 * C], bin_row[:, :], ALU.add)\
                        .then_inc(qkv1_ready.h, qkv1_ready.up())
                elif use == "kv":
                    dve.tensor_tensor(kv[:, :], L[:, 0:C], kvmask[:, :], ALU.mult).then_inc(kv_ready.h, kv_ready.up())
                elif use == "g":
                    dve.tensor_copy(G[:, :], L[:, 0:C]).then_inc(g_ready.h, g_ready.up())
                    h2v = h2[:, :].rearrange("p (j c) -> p j c", j=J)
                    link(dve.tensor_tensor(h2v, h2v, bo1[:, :].unsqueeze(1).to_broadcast((A, J, C)), ALU.add))
                elif use == "out1":
                    dve.wait_ge(h3_stored.h, h3_stored.at(b, 0))
                    dve.tensor_tensor(h3[:, :], L[0:A, 0:J * C], h2[:, :], ALU.add).then_inc(h3_ready.h, h3_ready.up())
                elif unit == 10:
                    dve.wait_ge(h3_ready.h, h3_ready.at(b, 1))
                    norm_sums(h3, 1)
                elif unit == 11:
                    norm_var(2, 1)
                elif unit == 12:
                    dve.wait_ge(rows_sent.h, rows_sent.at(b, 0))
                    norm_rows(b, 2, h3, 1)
                elif use == "ln4":
                    dve.tensor_copy(xTs[1][:, :], L[:, 0:TOK]).then_inc(xT_ready[1].h, xT_ready[1].up())
                elif unit == 15:
                    dve.wait_ge(gate1_exp.h, gate1_exp.at(b, 1))
                    link(dve.tensor_scalar(sc[:, :, :], sc[:, :, :], 1.0, None, ALU.add))
                    link(dve.reciprocal(sc[:, :, :], sc[:, :, :]))
                    link(dve.tensor_tensor(ss3, sc[:, :, :], gate1_b[:, :].unsqueeze(1).to_broadcast((A, J, E1)), ALU.add))
                elif unit == 16:
                    dve.tensor_tensor(tlo[:, :, :], ss[:, :, 0:4], ss[:, :, 4:8], ALU.min)
                    link(dve.tensor_tensor(thi[:, :, :], ss[:, :, 0:4], ss[:, :, 4:8], ALU.max))
                    for w in (2, 1):
                        dve.tensor_tensor(tmi[:, :, 0:w], thi[:, :, 0:w], thi[:, :, w:2 * w], ALU.min)
                        link(dve.tensor_tensor(tlo[:, :, 0:w], tlo[:, :, 0:w], tlo[:, :, w:2 * w], ALU.max))
                        link(dve.tensor_tensor(thi[:, :, 0:w], thi[:, :, 0:w], thi[:, :, w:2 * w], ALU.max))
                        link(dve.tensor_tensor(tlo[:, :, 0:w], tlo[:, :, 0:w], tmi[:, :, 0:w], ALU.max))
                    link(dve.tensor_tensor(gl[:, :].unsqueeze(2), thi[:, :, 0:1], tlo[:, :, 0:1], ALU.add))
                elif unit == 17:
                    choose(gl[:, :], 4)
                elif unit == 18:
                    dve.tensor_scalar(gpen[:, :], chosen[:, :], 1.0, 1e30, ALU.subtract, ALU.mult)
                    link(dve.tensor_tensor(ss[:, :, :], ss[:, :, :], chosen[:, :].unsqueeze(2).to_broadcast((A, J * 8, 8)), ALU.mult))
                    link(dve.tensor_tensor(ss[:, :, :], ss[:, :, :], gpen[:, :].unsqueeze(2).to_broadcast((A, J * 8, 8)), ALU.add))
                elif unit == 19:
                    hold()
                    for j in range(J):
                        ins = dve.max(top[:, j, :], ss3[:, j, :])
                    link(ins)
                elif unit == 20:
                    hold()
                    for j in range(J):
                        ins = dve.match_replace(mr[:, j, :], top[:, j, :], ss3[:, j, :], -3e30)
                    link(ins)
                    dve.tensor_tensor(sel[:, :, :], mr[:, :, :], ss3, ALU.not_equal).then_inc(sel_ready.h, sel_ready.up())
                    dve.wait_ge(sel_ready.h, sel_ready.at(b, 1))
                elif unit == 21:
                    link(dve.tensor_tensor(sc[:, :, :], sc[:, :, :], sel[:, :, :], ALU.mult))
                    link(dve.tensor_reduce(gsum[:, :], sc[:, :, :], AX.X, ALU.add))
                    link(dve.reciprocal(gsum[:, :], gsum[:, :]))
                    dve.scalar_tensor_tensor(rows[:, :, C:C + E1], sc[:, :, :], 2.5,
                                             gsum[:, :].unsqueeze(2).to_broadcast((A, J, E1)), ALU.mult, ALU.mult)
                    link(dve.tensor_copy(rows[:, :, C + E1], tokens[:, :]))
                    link(dve.tensor_scalar(tokens[:, :], tokens[:, :], float(TOK), None, ALU.add))
                elif use == "count":
                    link(dve.tensor_tensor(pos[:, :, :], L[0:A, 0:J * E1].rearrange("p (j e) -> p j e", j=J),
                                           carry[:, :].unsqueeze(1).to_broadcast((A, J, E1)), ALU.add))
                    dve.tensor_tensor(carry[:, :], L[0:A, J * E1:(J + 1) * E1], carry[:, :], ALU.add)\
                        .then_inc(counted.h, counted.up())
                    link(dve.scalar_tensor_tensor(mr[:, :, :], pos[:, :, :], float(CAP), sel[:, :, :], ALU.is_lt, ALU.mult))
                    link(dve.tensor_tensor(pos[:, :, :], slot_base[:, :, :], pos[:, :, :], ALU.subtract))
                    link(dve.tensor_tensor(pos[:, :, :], pos[:, :, :], mr[:, :, :], ALU.mult))
                elif unit == 23:
                    hold()
                    for j in range(J):
                        ins = dve.max(top[:, j, :], pos[:, j, :])
                    link(ins)
                    dve.tensor_scalar(slot_i[:, :], top[:, :, :].rearrange("p j k -> p (j k)"), -1.0,
                                                    float(SLOTS), ALU.mult, ALU.add).then_inc(rows_ready.h, rows_ready.up())
                chain[:] = saved

            def present(b, nb, tb, lb):
                turn_to(step_main, b, first=True)
                norm(b, 1, h0)
                for h in range(0, H0, 2):
                    g = h // 2
                    i, nth = W_AT[("k", g)]
                    dve.wait_ge(w_full[i].h, w_full[i].at(b, nth))
                    dve.tensor_scalar(KP[0:DH, h, :], W[i][0:DH, 0:TOK], 1 / WS, k_b[0:DH, g:g + 1], ALU.mult, ALU.add)
                    dve.tensor_scalar(KP[DH:, h + 1, :], W[i][DH:, 0:TOK], 1 / WS, k_b[DH:, g:g + 1], ALU.mult, ALU.add)\
                        .then_inc(kvp_ready.h, kvp_ready.up())
                for j in range(J):
                    i, nth = W_AT[("v", j)]
                    dve.wait_ge(w_full[i].h, w_full[i].at(b, nth))
                    dve.tensor_copy(V[:, j, :], W[i][0:A, :]).then_inc(kvp_ready.h, kvp_ready.up())
                if tb is not None:
                    tok_softmax(tb)
                turn_to(step_main, b)
                for s in range(UNITS + 3):
                    if s < UNITS:
                        i, nth = W_AT[("S", s)]
                        dve.wait_ge(w_full[i].h, w_full[i].at(b, nth))
                        if s >= 2:
                            dve.wait_ge(p_ready.h, p_ready.at(b, s - 1))
                        dve.tensor_reduce(nmax[:, s % 2:s % 2 + 1], W[i][0:A, 0:TOK], AX.X, ALU.max,
                                                        negate=True).then_inc(nmax_ready.h, nmax_ready.up())
                    if 1 <= s <= UNITS and (s - 1) % 2 == 1:
                        u = s - 1
                        i, nth = W_AT[("T", u)]
                        dve.wait_ge(w_full[i].h, w_full[i].at(b, nth))
                        if u >= 2:
                            pt_used(dve, b, u - 2)
                        dve.tensor_copy(PT[:, 1, :], W[i][0:A, 0:TOK]).then_inc(pt_ready_d.h, pt_ready_d.up())
                    if s < UNITS:
                        conv_out(nb, 3 + s)
                        late(lb, s)
                    if s >= 4 and (s - 4) % J == J - 1 and (s - 4) // J < H0 - 1 or s == UNITS + 2:
                        h = (s - 4) // J if s < UNITS + 2 else H0 - 1
                        dve.wait_ge(p_ready.h, p_ready.at(b, J * h + J))
                        link(dve.reciprocal(prec[:, h, :], psums[:, h, :]))
                        i, nth = O_AT[("O", h)]
                        dve.wait_ge(o_full[i].h, o_full[i].at(b, nth))
                        dve.tensor_tensor(
                            O[:, :, h * DH:(h + 1) * DH], Ob[i][0:A, 0:J * DH].rearrange("p (j d) -> p j d", j=J),
                            prec[:, h, :].unsqueeze(2).to_broadcast((A, J, DH)), ALU.mult).then_inc(o_ready.h, o_ready.up())
                link(dve.tensor_tensor(h0b[:, :].rearrange("p (j c) -> p j c", j=J),
                                       h0[:, :].rearrange("p (j c) -> p j c", j=J),
                                       bo[:, :].unsqueeze(1).to_broadcast((A, J, C)), ALU.add))
                i, nth = W_AT[("out0", 0)]
                dve.wait_ge(w_full[i].h, w_full[i].at(b, nth))
                link(dve.tensor_tensor(h1[:, :], W[i][0:A, 0:J * C], h0b[:, :], ALU.add))

                norm(b, 2, h1)
                gl3 = gl[:, :].rearrange("p (j g) -> p j g", g=8)
                spread8 = lambda x: x[:, :].unsqueeze(2).to_broadcast((A, J, 8))

                def gate_logits():
                    i, nth = W_AT[("gate0", 0)]
                    dve.wait_ge(w_full[i].h, w_full[i].at(b, nth))
                    link(dve.tensor_copy(gl[:, :], W[i][0:A, 0:J * E0]))
                    choose(gl[:, :], 2)
                    link(dve.tensor_reduce(gmx[:, :], gl3, AX.X, ALU.max))
                    dve.tensor_tensor(gl3, gl3, spread8(gmx), ALU.subtract).then_inc(gexp_in.h, gexp_in.up())

                def gate_weights():
                    dve.wait_ge(gexp_out.h, gexp_out.at(b, 1))
                    link(dve.tensor_tensor(comb[:, :], chosen[:, :], gl[:, :], ALU.mult))
                    link(dve.tensor_reduce(gsum[:, :], comb[:, :].rearrange("p (j g) -> p j g", g=8), AX.X, ALU.add))
                    link(dve.reciprocal(gsum[:, :], gsum[:, :]))
                    c3 = comb[:, :].rearrange("p (j g) -> p j g", g=8)
                    link(dve.scalar_tensor_tensor(c3, c3, 0.5 / WS, spread8(gsum), ALU.mult, ALU.mult))

                p = 3 + UNITS + 4

                def mixed(e):
                    o, nth = O_AT[("Y", e)]
                    dve.wait_ge(o_full[o].h, o_full[o].at(b, nth))
                    src = h1 if e == 0 else h2
                    for j in range(J):
                        s = slice(j * C, (j + 1) * C)
                        scale = comb[:, j * 8 + e:j * 8 + e + 1] if e < E0 else 0.5 / WS ** 2
                        ins = dve.scalar_tensor_tensor(h2[:, s], Ob[o][0:A, s], scale, src[:, s], ALU.mult, ALU.add)
                    ins.then_inc(y_added.h, y_added.up())
                    dve.wait_ge(y_added.h, y_added.at(b, e + 1))

                for e in range(E0 + 1):
                    for c in range(2):
                        n = 2 * e + c
                        dst = hid[:, 2 * (e % 2) + c, :]
                        if e >= 2:
                            bank, nth = O_AT[("Y", e - 2)]
                            dve.wait_ge(o_full[bank].h, o_full[bank].at(b, nth))
                        dve.wait_ge(th_ready.h, th_ready.at(b, n + 1))
                        if e < E0:
                            i, nth = W_AT[("hid", n)]
                            dve.wait_ge(w_full[i].h, w_full[i].at(b, nth))
                            dve.scalar_tensor_tensor(dst, th[:, n % 2, :], 1.0, W[i][:, 0:TOK],
                                                                  ALU.add, ALU.mult).then_inc(hid_ready.h, hid_ready.up())
                        else:
                            i, nth = W_AT[("sg", c)]
                            dve.wait_ge(w_full[i].h, w_full[i].at(b, nth))
                            link(dve.scalar_tensor_tensor(sgate[:, :], th[:, n % 2, :], 1.0, W[i][:, 0:TOK],
                                                          ALU.add, ALU.mult))
                            i, nth = W_AT[("su", c)]
                            dve.wait_ge(w_full[i].h, w_full[i].at(b, nth))
                            dve.tensor_tensor(dst, W[i][:, 0:TOK], sgate[:, :], ALU.mult).then_inc(hid_ready.h, hid_ready.up())
                            dve.wait_ge(hid_ready.h, hid_ready.at(b, n + 1))
                        if n == 0:
                            gate_logits()
                        if n == 2:
                            gate_weights()
                        conv_out(nb, p)
                        p += 1
                        if n == NHID - 2 and tb is not None:
                            tok_split(tb)
                            turn_to(step_main, b)
                        if e >= 1 and c == (0 if e == E0 else 1):
                            mixed(e - 1)
                conv_out(nb, p)
                p += 1
                assert p == POINTS
                if nb is not None:
                    tok_out(nb)
                mixed(E0)

            n_set = [0]

            def done(ins):
                n_set[0] += 1
                ins.then_inc(s_set, 1)
                dve.wait_ge(s_set, n_set[0])

            done(dve.memset(carry[:, :], 0.0))
            dve.wait_ge(s_tokw, 16 * len(tok_loads))
            done(dve.tensor_tensor(tok_mask[:, :, :], tok_mask[:, :, :],
                                   tok_bl[:, :].unsqueeze(1).to_broadcast((TT, TILES, LK)), ALU.add))
            batch_starts()
            tok_softmax(0)

            def split_weights(n):
                half = slice((n % 2) * HALF, (n % 2 + 1) * HALF)
                dve.wait_ge(s_hi, n + 1)
                dve.scalar_tensor_tensor(wc_lo[:, n // 2, half], stage[n % 2], CS, wc_hi[:, n // 2, half],
                                         ALU.mult, ALU.subtract).then_inc(s_lo, 1)
            for n in range(4):
                split_weights(n)
            tok_split(0)
            for n in range(4, 2 * OC):
                split_weights(n)
            dve.wait_ge(s_curw, 16 * len(layer_loads))
            for sig in t_out:
                dve.wait_ge(sig.h, 16)
            done(dve.tensor_tensor(q_b[:, :], q_b[:, :], uv[:, :], ALU.add))
            done(dve.tensor_scalar(q_b[:, :], q_b[:, :], DH ** -0.5, None, ALU.mult))
            for g in range(H0 // 2):
                dve.wait_ge(s_pos, g + 1)
                dve.tensor_copy(KP[0:DH, 2 * g + 1, :], W[g % 2][0:DH, 0:TOK])
                dve.tensor_copy(KP[DH:, 2 * g, :], W[g % 2][DH:, 0:TOK]).then_inc(s_posu, 1)
            done(dve.tensor_copy(tri[:, :, :], tri_f))
            dve.wait_ge(s_vb, 1)
            done(dve.tensor_tensor(bo[:, :], bo[:, :], W[2][0:A, 0:C], ALU.add))
            done(dve.tensor_scalar(woT[:, :, :], woT[:, :, :], 1 / WS, None, ALU.mult))
            tok_softmax(1)
            dve.wait_ge(s_whi, 1)
            q_halves = w_hl[:, :, 0:WIDE].rearrange("p x (h r d) -> p x h r d", h=H0, r=2)
            for copy in range(2):
                dve.scalar_tensor_tensor(q_halves[:, 1, :, copy, :], q_twice[:, :, copy, :], WS,
                                         q_halves[:, 0, :, copy, :], ALU.mult, ALU.subtract)
            dve.scalar_tensor_tensor(w_hl[:, 1, WIDE:], w_stage[:, H0 * DH:], WS, w_hl[:, 0, WIDE:],
                                     ALU.mult, ALU.subtract).then_inc(s_setup, 1)
            for p in range(POINTS):
                conv_out(0, p)
            tok_split(1)
            tok_out(0)
            present(0, 1, 2, None)
            with dve.Fori(1, B - 1) as it:
                batch_starts()
                present(it, it + 1, it + 2, it - 1)
                batch_ends()
            present(B - 1, None, None, B - 2)
            for s in range(UNITS):
                late(B - 1, s)

            def expert_h(pr, i):
                k = i % 4
                dve.wait_ge(t_th[i].h, t_th[i].at(pr, 1))
                link(dve.scalar_tensor_tensor(e_s, e_th[k], 1.0, up_bank[k][0:F1, 0:CAP], ALU.add, ALU.mult))
                dve.tensor_tensor(e_h[k], up_bank[k][0:F1, CAP:], e_s, ALU.mult).then_inc(t_h[i].h, t_h[i].up())
                dve.wait_ge(t_h[i].h, t_h[i].at(pr, 1))

            def expert_y(pr, i):
                dve.wait_ge(t_out[i].h, t_out[i].at(pr, 0))
                dve.wait_ge(t_yps[i].h, t_yps[i].at(pr, 1))
                dve.tensor_copy(e_idx[i], e_rows[i][:, :, C + E1])
                y = (W[2], L)[i % 2]
                for c in range(2):
                    w = e_rows[i][:, c, bass.ds(pr * NE + (C + i), 1)]
                    ins = dve.tensor_scalar(e_y[i][:, c, :], y[:, c * C:(c + 1) * C], w, 0.5, ALU.mult, ALU.mult)
                ins.then_inc(t_y[i].h, t_y[i].up())

            with dve.Fori(0, E1 // NE) as pr:
                batch_starts()
                turn_to(t_s, pr, first=True)
                for i in range(0, NE + 2, 2):
                    for k in i - 2, i - 1:
                        if k >= 2:
                            expert_y(pr, k - 2)
                    for k in i, i + 1:
                        if k < NE:
                            expert_h(pr, k)
                for k in range(NE - 2, NE):
                    expert_y(pr, k)
                batch_ends()
    return totals


def pack(i):
    f = lambda a: np.ascontiguousarray(a)
    d = {}
    x = i["x"]
    pad = (TAPS - 1) // 2
    x = np.concatenate([x, np.zeros((1, T, C), np.float32)], axis=0)
    zrow = np.zeros((B + 1, pad, C), np.float32)
    xpad = np.concatenate([zrow, x, np.zeros((B + 1, TP - T, C), np.float32), zrow], axis=1)
    d["xpad"] = f(xpad)
    d["xTp"] = f(xpad[:, pad:pad + TP].transpose(0, 2, 1))
    by_tap = lambda w: w.reshape(HEADS_T, TAPS, -1).transpose(1, 0, 2).reshape(LK, -1)
    d["wlT"] = f(by_tap(i["L0_tok_Wl"]).T)
    d["tok_bl"] = f(by_tap(i["L0_tok_bl"])[:, 0])
    t = np.arange(TP)[:, None] + np.arange(TAPS)[None, :] - pad
    ok = (t >= 0) & (t < T)
    mask = np.where(ok, 0.0, -1e30).astype(np.float32).reshape(TILES, TT, TAPS)
    d["tok_mask"] = f(np.repeat(mask.transpose(1, 0, 2)[..., None], HEADS_T, axis=3).reshape(TT, TILES, LK))
    d["tok_bias"] = f(i["L0_tok_bias"][:, None])
    d["conv_b"] = f(i["L0_tok_bc"].reshape(OC, 128).T)
    d["w2T"] = f(i["L0_tok_W2"].T.reshape(OC, 128, C).transpose(1, 0, 2))
    d["b2"] = f(i["L0_tok_b2"])
    d["wc"] = f(i["L0_tok_Wc"].reshape(OC, 128, C, TAPS).transpose(0, 2, 3, 1).reshape(OC, C, TAPS * 128))
    d["gamma"], d["beta"] = f(i["L0_attn_gamma"][:, None]), f(i["L0_attn_beta"][:, None])
    wq, wk, wv = np.split(i["L0_attn_w_qkv"], 3, axis=0)
    bq, bk, bv = np.split(i["L0_attn_b_qkv"], 3)
    d["wqT"] = f(wq.T)
    d["wkT"], d["wvT"] = f(wk.T), f(wv.T)
    d["q_b"] = f(bq.reshape(H0, DH).T)
    d["k_b"] = f(bk.reshape(H0 // 2, 128).T)
    d["v_b"] = f(bv.reshape(4, 128).T)
    u, v = i["L0_attn_u_bias"].T, i["L0_attn_v_bias"].T
    uv = np.empty((128, H0), np.float32)
    uv[:DH, 0::2], uv[DH:, 0::2], uv[:DH, 1::2], uv[DH:, 1::2] = u[:, 0::2], v[:, 0::2], v[:, 1::2], u[:, 1::2]
    d["uv"] = uv
    rel = np.arange(TOK, dtype=np.float32)[:, None] - np.arange(C, dtype=np.float32)[None, :]
    freq = np.exp(-np.arange(0, 2 * C, 2, dtype=np.float32) * np.float32(np.log(10000.0) / C)).astype(np.float32)
    angle = (rel * freq[None, :]).astype(np.float32)
    pe = np.where(np.arange(C)[None, :] % 2 == 0, np.cos(angle), np.sin(angle)).astype(np.float32)
    d["peT"] = f(pe.reshape(A, J, C).transpose(2, 1, 0).reshape(C, TOK))
    d["wposT"] = f(i["L0_attn_w_pos"].reshape(H0 // 2, 2, DH, C)[:, ::-1].reshape(H0 * DH, C).T)
    d["woT"] = f(i["L0_attn_w_out"].T.reshape(4, 128, C).transpose(1, 0, 2))
    d["bo"] = f(i["L0_attn_b_out"])
    d["gate0T"] = f(i["L0_ffn_gate_w"].T)
    d["w1T"] = f(i["L0_ffn_w1"].reshape(E0 * F0, C).T)
    d["w2eT"] = f(i["L0_ffn_w2"].transpose(0, 2, 1).reshape(E0 * 2, 128, C).transpose(1, 0, 2))
    d["sgT"], d["suT"] = f(i["L0_ffn_sg_gate"].T), f(i["L0_ffn_sg_up"].T)
    d["sdT"] = f(i["L0_ffn_sg_down"].T.reshape(2, 128, C).transpose(1, 0, 2))
    d["winT"] = f(i["L1_attn_w_in"].T)
    d["bin_col"] = f(i["L1_attn_b_in"].reshape(3, C).T)
    d["bin_row"] = f(i["L1_attn_b_in"])
    d["kvmask"] = np.kron(np.eye(8, dtype=np.float32), np.full((16, 16), 0.25, np.float32))
    d["wo1T"] = f(i["L1_attn_w_out"].T)
    d["bo1"] = f(i["L1_attn_b_out"])
    d["gate1T"] = f(i["L1_ffn_gate_w"].T)
    d["gate1_b"] = f(i["L1_ffn_gate_b"])
    d["w1e"], d["w3e"], d["w2e"] = f(i["L1_ffn_w1"]), f(i["L1_ffn_w3"]), f(i["L1_ffn_w2"])
    d["slot_base"] = np.broadcast_to(SLOTS - CAP * np.arange(E1, dtype=np.float32), (A, J, E1)).copy()
    d["tokens"] = (np.arange(A)[:, None] * J + np.arange(J)[None, :]).astype(np.float32)
    a = np.arange(A)
    tri = np.stack([a[:, None] < a[None, :], a[:, None] <= a[None, :], np.ones((A, A), bool)], axis=1)
    d["tri"] = tri.astype(np.float32)
    d["ident"] = np.eye(128, dtype=np.float32)
    empty = np.zeros((CAP, ROW), np.float32)
    empty[:, C + E1] = NTOK + np.arange(CAP)
    d["empty_slots"] = empty
    d["zero_rows"] = np.zeros(CAP * C, np.float32)
    return d


def kernel(**inputs):
    import concourse.bacc as bacc
    from concourse.bass_utils import run_bass_kernel_spmd

    arrays = {f"in_{k}": v for k, v in pack({k: np.asarray(v) for k, v in inputs.items()}).items()}

    def program(per):
        nc = bacc.Bacc("TRN2", target_bir_lowering=False, num_devices=1)
        dram = {k[3:]: nc.dram_tensor(k, v.shape, F32, kind="ExternalInput").ap() for k, v in arrays.items()}
        out = nc.dram_tensor("out", (NTOK + CAP, C), F32, kind="ExternalOutput").ap()
        return nc, build(nc, dram, out, per)

    _, per = program({})
    nc, again = program(per)
    assert again == per
    result = run_bass_kernel_spmd(nc, [arrays], core_ids=[0])
    return result.results[0]["out"][:NTOK].reshape(B, TOK, C)
```
